# Optimizing a Trainium2 kernel written in Bass

```python
import numpy as np
import jax
import jax.numpy as jnp

def _softmax(x, axis=-1):
    return jax.nn.softmax(x, axis=axis)

def _gelu(x):
    return jax.nn.gelu(x, approximate=True)

def _silu(x):
    return jax.nn.silu(x)

def _sigmoid(x):
    return jax.nn.sigmoid(x)

def _layernorm(x, axis=-1, eps=1e-05):
    m = jnp.mean(x, axis=axis, keepdims=True)
    v = jnp.var(x, axis=axis, keepdims=True)
    return (x - m) / jnp.sqrt(v + eps)

def _scatter_add(tgt, idx, src, axis=0):
    return tgt.at[idx].add(src)

def _segment_sum(src, seg, n):
    return jax.ops.segment_sum(src, seg, n)
kernel_name = 'mk_vit_tower_cls_d1_tok_img256_r4_d1f86f'

def setup_inputs(seed: int=0):
    np.random.seed(seed)
    _w = jnp.asarray

    def _rec_inputs():
        import jax
        import jax.numpy as jnp
        _rk = jax.random.key(seed)
        x = -0.000928989 + 1.00043 * jax.random.normal(jax.random.fold_in(_rk, 1), (64, 64, 64, 1), jnp.float32)
        cls_tok = 0.02 * jax.random.normal(jax.random.fold_in(_rk, 5), (1, 1, 64), jnp.float32)
        return (x, cls_tok)
    x, cls_tok = _rec_inputs()

    def _L0_tok_setup():
        import jax, jax.numpy as jnp
        import numpy as np
        L = 4
        M1 = 12
        M2 = 12
        BN_EPS = 1e-05

        def _fourier_layer(v, W1, W2):
            B, C, Sx, Sy = v.shape
            x_ft = jnp.fft.rfft2(v)
            out1 = jnp.einsum('bixy,ioxy->boxy', x_ft[:, :, :M1, :M2], W1)
            out2 = jnp.einsum('bixy,ioxy->boxy', x_ft[:, :, -M1:, :M2], W2)
            out_ft = jnp.zeros((B, C, Sx, Sy // 2 + 1), jnp.complex64)
            out_ft = out_ft.at[:, :, :M1, :M2].set(out1)
            out_ft = out_ft.at[:, :, Sx - M1:, :M2].set(out2)
            return jnp.fft.irfft2(out_ft, s=(Sx, Sy))
        key = jax.random.key(seed)
        ks = jax.random.split(key, 10)
        B, S, d_a, d_v, d_u = (16, 64, 3, 32, 1)
        return {'x': jax.random.normal(ks[0], (B, S, S, 1), jnp.float32), 'p_w': jax.random.normal(ks[1], (d_a, d_v), jnp.float32) * 0.3, 'p_b': jax.random.normal(ks[2], (d_v,), jnp.float32) * 0.1, 'fw1': jax.random.normal(ks[3], (L, d_v, d_v, M1, M2, 2), jnp.float32) * (1.0 / d_v), 'fw2': jax.random.normal(ks[4], (L, d_v, d_v, M1, M2, 2), jnp.float32) * (1.0 / d_v), 'w_w': jax.random.normal(ks[5], (L, d_v, d_v), jnp.float32) * (1.0 / np.sqrt(d_v)), 'w_b': jax.random.normal(ks[6], (L, d_v), jnp.float32) * 0.1, 'bn_g': jnp.ones((L, d_v), jnp.float32), 'bn_b': jnp.zeros((L, d_v), jnp.float32), 'q_w': jax.random.normal(ks[7], (d_v, d_u), jnp.float32) * 0.3, 'q_b': jax.random.normal(ks[8], (d_u,), jnp.float32) * 0.1}
    _L0_tok_all = _L0_tok_setup()
    _L0_tok_in = {k: v for k, v in _L0_tok_all.items() if k in ('p_w', 'p_b', 'fw1', 'fw2', 'w_w', 'w_b', 'bn_g', 'bn_b', 'q_w', 'q_b')}
    del _L0_tok_all

    def _L0_attn_setup():
        import jax, jax.numpy as jnp
        import numpy as np
        HEADS = 8
        EPS = 1e-05

        def _ln(t, w, b, headc):
            m = jnp.mean(t, axis=-1, keepdims=True)
            d = t - m
            std = jnp.sqrt(jnp.sum(d * d, axis=-1, keepdims=True) / (headc - 1))
            return w * (d / (std + EPS)) + b
        key = jax.random.key(seed)
        B, N, C = (32, 1024, 64)
        headc = C // HEADS
        x = jax.random.normal(key, (B, N, C), dtype=jnp.float32)
        return {'x': x, 'kln_weight': jnp.ones((HEADS, 1, headc), dtype=jnp.float32), 'kln_bias': jnp.zeros((HEADS, 1, headc), dtype=jnp.float32), 'vln_weight': jnp.ones((HEADS, 1, headc), dtype=jnp.float32), 'vln_bias': jnp.zeros((HEADS, 1, headc), dtype=jnp.float32)}
    _L0_attn_all = _L0_attn_setup()
    _L0_attn_in = {k: v for k, v in _L0_attn_all.items() if k in ('kln_weight', 'kln_bias', 'vln_weight', 'vln_bias')}
    del _L0_attn_all

    def _L0_ffn_setup():
        import jax, jax.numpy as jnp
        import numpy as np
        NUM_EXPERTS = 8
        TOP_K = 2
        B, S, D = (8, 2048, 64)

        def _moe(tokens, router_w, w1, b1, w2, b2):
            N = tokens.shape[0]
            E = router_w.shape[0]
            logits = tokens.astype(jnp.float32) @ router_w.astype(jnp.float32).T
            probs = jax.nn.softmax(logits, axis=-1)
            rw, re = jax.lax.top_k(probs, TOP_K)
            if TOP_K > 1:
                rw = rw / jnp.maximum(rw.sum(-1, keepdims=True), 1e-12)
            rw = rw.astype(tokens.dtype)
            combine = jnp.zeros((N, E), tokens.dtype).at[jnp.arange(N)[:, None], re].set(rw)
            out = tokens
            for e in range(E):
                h = jax.nn.gelu(tokens @ w1[e] + b1[e], approximate=False)
                y = h @ w2[e] + b2[e]
                out = out + combine[:, e:e + 1] * y
            return out
        key = jax.random.key(seed)
        ks = jax.random.split(key, 4)
        scale = 1.0 / np.sqrt(D).astype(np.float32)
        return {'input_embeddings': jax.random.normal(ks[0], (B, S, D), jnp.float32), 'router_w': jax.random.normal(ks[1], (NUM_EXPERTS, D), jnp.float32) * scale, 'w1': jax.random.normal(ks[2], (NUM_EXPERTS, D, D), jnp.float32) * scale, 'b1': jnp.zeros((NUM_EXPERTS, D), jnp.float32), 'w2': jax.random.normal(ks[3], (NUM_EXPERTS, D, D), jnp.float32) * scale, 'b2': jnp.zeros((NUM_EXPERTS, D), jnp.float32)}
    _L0_ffn_all = _L0_ffn_setup()
    _L0_ffn_in = {k: v for k, v in _L0_ffn_all.items() if k in ('router_w', 'w1', 'b1', 'w2', 'b2')}
    del _L0_ffn_all
    return {'x': x, 'cls_tok': cls_tok, 'L0_tok_p_w': _L0_tok_in['p_w'], 'L0_tok_p_b': _L0_tok_in['p_b'], 'L0_tok_fw1': _L0_tok_in['fw1'], 'L0_tok_fw2': _L0_tok_in['fw2'], 'L0_tok_w_w': _L0_tok_in['w_w'], 'L0_tok_w_b': _L0_tok_in['w_b'], 'L0_tok_bn_g': _L0_tok_in['bn_g'], 'L0_tok_bn_b': _L0_tok_in['bn_b'], 'L0_tok_q_w': _L0_tok_in['q_w'], 'L0_tok_q_b': _L0_tok_in['q_b'], 'L0_attn_kln_weight': _L0_attn_in['kln_weight'], 'L0_attn_kln_bias': _L0_attn_in['kln_bias'], 'L0_attn_vln_weight': _L0_attn_in['vln_weight'], 'L0_attn_vln_bias': _L0_attn_in['vln_bias'], 'L0_ffn_router_w': _L0_ffn_in['router_w'], 'L0_ffn_w1': _L0_ffn_in['w1'], 'L0_ffn_b1': _L0_ffn_in['b1'], 'L0_ffn_w2': _L0_ffn_in['w2'], 'L0_ffn_b2': _L0_ffn_in['b2']}

def reference(x, cls_tok, L0_tok_p_w, L0_tok_p_b, L0_tok_fw1, L0_tok_fw2, L0_tok_w_w, L0_tok_w_b, L0_tok_bn_g, L0_tok_bn_b, L0_tok_q_w, L0_tok_q_b, L0_attn_kln_weight, L0_attn_kln_bias, L0_attn_vln_weight, L0_attn_vln_bias, L0_ffn_router_w, L0_ffn_w1, L0_ffn_b1, L0_ffn_w2, L0_ffn_b2):
    import jax
    import jax.numpy as jnp

    def _L0_tok_ref(x, p_w, p_b, fw1, fw2, w_w, w_b, bn_g, bn_b, q_w, q_b):
        import jax, jax.numpy as jnp
        import numpy as np
        L = 4
        M1 = 12
        M2 = 12
        BN_EPS = 1e-05

        def _fourier_layer(v, W1, W2):
            B, C, Sx, Sy = v.shape
            x_ft = jnp.fft.rfft2(v)
            out1 = jnp.einsum('bixy,ioxy->boxy', x_ft[:, :, :M1, :M2], W1)
            out2 = jnp.einsum('bixy,ioxy->boxy', x_ft[:, :, -M1:, :M2], W2)
            out_ft = jnp.zeros((B, C, Sx, Sy // 2 + 1), jnp.complex64)
            out_ft = out_ft.at[:, :, :M1, :M2].set(out1)
            out_ft = out_ft.at[:, :, Sx - M1:, :M2].set(out2)
            return jnp.fft.irfft2(out_ft, s=(Sx, Sy))
        B, Sx, Sy, _ = x.shape
        gx = jnp.broadcast_to(jnp.linspace(0.0, 1.0, Sx, dtype=jnp.float32)[None, :, None, None], (B, Sx, Sy, 1))
        gy = jnp.broadcast_to(jnp.linspace(0.0, 1.0, Sy, dtype=jnp.float32)[None, None, :, None], (B, Sx, Sy, 1))
        h = jnp.concatenate([x, gx, gy], axis=-1)
        v = h @ p_w + p_b
        v = jnp.transpose(v, (0, 3, 1, 2))
        for i in range(L):
            W1 = fw1[i, ..., 0] + 1j * fw1[i, ..., 1]
            W2 = fw2[i, ..., 0] + 1j * fw2[i, ..., 1]
            x1 = _fourier_layer(v, W1, W2)
            x2 = jnp.einsum('bcxy,cd->bdxy', v, w_w[i]) + w_b[i][None, :, None, None]
            v = x1 + x2
            mean = jnp.mean(v, axis=(0, 2, 3), keepdims=True)
            var = jnp.var(v, axis=(0, 2, 3), keepdims=True)
            v = (v - mean) * jax.lax.rsqrt(var + BN_EPS)
            v = v * bn_g[i][None, :, None, None] + bn_b[i][None, :, None, None]
            if i < L - 1:
                v = jax.nn.relu(v)
        out = jnp.einsum('bcxy,cu->bxyu', v, q_w) + q_b
        return jnp.squeeze(out)

    def _L0_attn_ref(x, kln_weight, kln_bias, vln_weight, vln_bias):
        import jax, jax.numpy as jnp
        import numpy as np
        HEADS = 8
        EPS = 1e-05

        def _ln(t, w, b, headc):
            m = jnp.mean(t, axis=-1, keepdims=True)
            d = t - m
            std = jnp.sqrt(jnp.sum(d * d, axis=-1, keepdims=True) / (headc - 1))
            return w * (d / (std + EPS)) + b
        B, N, C = x.shape
        headc = C // HEADS
        qkv = x.reshape(B, N, HEADS, headc).transpose(0, 2, 1, 3)
        k = _ln(qkv, kln_weight, kln_bias, headc)
        v = _ln(qkv, vln_weight, vln_bias, headc)
        kv = jnp.einsum('bhnd,bhne->bhde', k, v) / N
        out = jnp.einsum('bhnd,bhde->bhne', qkv, kv)
        out = out.transpose(0, 2, 1, 3).reshape(B, N, C)
        return out + x

    def _L0_ffn_ref(input_embeddings, router_w, w1, b1, w2, b2):
        import jax, jax.numpy as jnp
        import numpy as np
        NUM_EXPERTS = 8
        TOP_K = 2
        B, S, D = (8, 2048, 64)

        def _moe(tokens, router_w, w1, b1, w2, b2):
            N = tokens.shape[0]
            E = router_w.shape[0]
            logits = tokens.astype(jnp.float32) @ router_w.astype(jnp.float32).T
            probs = jax.nn.softmax(logits, axis=-1)
            rw, re = jax.lax.top_k(probs, TOP_K)
            if TOP_K > 1:
                rw = rw / jnp.maximum(rw.sum(-1, keepdims=True), 1e-12)
            rw = rw.astype(tokens.dtype)
            combine = jnp.zeros((N, E), tokens.dtype).at[jnp.arange(N)[:, None], re].set(rw)
            out = tokens
            for e in range(E):
                h = jax.nn.gelu(tokens @ w1[e] + b1[e], approximate=False)
                y = h @ w2[e] + b2[e]
                out = out + combine[:, e:e + 1] * y
            return out
        b, s, d = input_embeddings.shape
        tokens = input_embeddings.reshape(b * s, d)
        return _moe(tokens, router_w, w1, b1, w2, b2).reshape(b, s, d)
    h = _L0_tok_ref(x, L0_tok_p_w, L0_tok_p_b, L0_tok_fw1, L0_tok_fw2, L0_tok_w_w, L0_tok_w_b, L0_tok_bn_g, L0_tok_bn_b, L0_tok_q_w, L0_tok_q_b)
    h = jnp.concatenate([jnp.broadcast_to(cls_tok, (h.shape[0], 1, h.shape[2])), h], axis=1)
    h = h + _L0_attn_ref(_layernorm(h, axis=-1), L0_attn_kln_weight, L0_attn_kln_bias, L0_attn_vln_weight, L0_attn_vln_bias)
    h = h + _L0_ffn_ref(_layernorm(h, axis=-1), L0_ffn_router_w, L0_ffn_w1, L0_ffn_b1, L0_ffn_w2, L0_ffn_b2)
    return h

_drawn_inputs = setup_inputs


def setup_inputs(seed=0):
    import zlib

    import numpy as np

    out = dict(_drawn_inputs(seed))
    spreads = {'L0_tok_bn_g': (1.0, 0.2),
     'L0_tok_bn_b': (0.0, 0.1),
     'L0_attn_kln_weight': (1.0, 0.2),
     'L0_attn_kln_bias': (0.0, 0.424),
     'L0_attn_vln_weight': (1.0, 0.2),
     'L0_attn_vln_bias': (0.0, 0.378),
     'L0_ffn_b1': (0.0, 0.715),
     'L0_ffn_b2': (0.0, 0.496)}
    factors = {'L0_tok_p_b': 8.0, 'L0_tok_w_b': 8.0}
    for name, (base, spread) in spreads.items():
        noise = np.random.default_rng([zlib.crc32(name.encode()), seed]).standard_normal(out[name].shape)
        drawn = base * np.exp(spread * noise) if base else spread * noise
        out[name] = jnp.asarray(drawn.astype(out[name].dtype))
    for name, factor in factors.items():
        out[name] = (out[name] * factor).astype(out[name].dtype)
    return out
```

```python
import numpy as np
import concourse.bass as bass
from concourse import mybir
from contextlib import ExitStack

BATCH, SIDE, CHANNELS, LAYERS = 64, 64, 32, 4
KX_HALF, KY = 12, 12
KX = 2 * KX_HALF
POSITIONS = SIDE * SIDE
QUAD = 4
QUADS = BATCH // QUAD
PAIRS = QUADS // 2
FEATURE_ROWS = 3
BN_EPS = 1e-5
HEADS, HEAD_DIM = 8, 8
DIM = HEADS * HEAD_DIM
EXPERTS = 8
TOKENS = SIDE + 1
LN_EPS = 1e-5
SLOTS = BATCH // 2 + 1


def transform_tables():
    kx = np.concatenate([np.arange(KX_HALF), np.arange(SIDE - KX_HALF, SIDE)]).astype(np.float64)
    ky = np.arange(KY, dtype=np.float64)
    pos = np.arange(SIDE, dtype=np.float64)
    ang = 2 * np.pi * np.outer(pos, ky) / SIDE
    fy = np.zeros((2, QUAD, 32, 2, KY, QUAD))
    for half in range(2):
        for j in range(QUAD):
            fy[half, j, :, 0, :, j] = np.cos(ang[half * 32:half * 32 + 32])
            fy[half, j, :, 1, :, j] = -np.sin(ang[half * 32:half * 32 + 32])
    ang = 2 * np.pi * np.outer(pos, kx) / SIDE
    fx = np.zeros((2, SIDE, 2, KX))
    fx[0, :, 0], fx[1, :, 0] = np.cos(ang), np.sin(ang)
    fx[0, :, 1], fx[1, :, 1] = -np.sin(ang), np.cos(ang)
    order = (np.arange(4)[:, None] + 4 * np.arange(16)[None, :]).reshape(-1)
    ang = 2 * np.pi * np.outer(kx, pos[order]) / SIDE
    ix = np.zeros((2, KX, 2, SIDE))
    ix[0, :, 0], ix[1, :, 0] = np.cos(ang), -np.sin(ang)
    ix[0, :, 1], ix[1, :, 1] = np.sin(ang), np.cos(ang)
    ix /= SIDE
    ang = 2 * np.pi * np.outer(ky, pos) / SIDE
    weight = np.where(ky == 0, 1.0, 2.0)[:, None] / SIDE
    iy = np.zeros((4, KY, 2, 4, SIDE))
    for x in range(4):
        iy[x, :, 0, x], iy[x, :, 1, x] = weight * np.cos(ang), -weight * np.sin(ang)
    table = lambda a, rows: np.ascontiguousarray(a.reshape(rows, -1), dtype=np.float32)
    return (np.ascontiguousarray(fy.reshape(2, 128, 96).transpose(1, 0, 2).reshape(128, 192), dtype=np.float32),
            table(fx, 128), table(ix, 48), table(iy, 96))


def shape_tables():
    line = np.linspace(0.0, 1.0, SIDE, dtype=np.float32)
    grids = np.ones((FEATURE_ROWS, SIDE, SIDE), np.float32)
    grids[0] = line[:, None]
    grids[1] = line[None, :]
    p = np.arange(128)
    ident = np.eye(128, dtype=np.float32)
    average = (p[:, None] % 32 == p[None, :] % 32).astype(np.float32) / QUAD
    image_of = (p[:, None] // 32 == np.arange(32)[None, :]).astype(np.float32)
    head = np.arange(64) // HEAD_DIM
    heads = (head[:, None] == head[None, :]).astype(np.float32) / np.float32(TOKENS)
    heads = np.concatenate([heads, heads])
    picks = np.tile(np.repeat(np.eye(EXPERTS, dtype=np.float32), 64, axis=1), (3, 1))
    falling = np.tile(np.arange(EXPERTS, 0, -1, dtype=np.float32), (128, 1))
    return (grids.reshape(FEATURE_ROWS, POSITIONS),
            np.ascontiguousarray(np.concatenate([ident, average, image_of, heads, falling], axis=1)), picks)


def tower_kernel(nc, images, p_rows, p_cols, mode_w, conv_w, layer_cols, q_cols, cls_tok, head_rows,
                 router_t, w1_t, b1_cols, w2_rows, b2_rows, fy_d, fx_d, ix_d, iy_d, grids_d, masks_d, picks_d, out):
    fp32 = mybir.dt.float32
    ALU = mybir.AluOpType
    ACT = mybir.ActivationFunctionType
    AX = mybir.AxisListType

    raw_d = nc.dram_tensor("raw_maps", [LAYERS, QUADS, 128, POSITIONS], fp32, kind="Internal").ap()
    mixed_d = nc.dram_tensor("mixed_modes", [2 * KX, KY, CHANNELS, BATCH], fp32, kind="Internal").ap()
    half_d = nc.dram_tensor("half_inverse", [KY * 2, 4, 16, BATCH * CHANNELS], fp32, kind="Internal").ap()
    tok_d = nc.dram_tensor("token_maps", [BATCH, 8, 512], fp32, kind="Internal").ap()

    ctx = ExitStack()
    with ctx:
        def sem(name):
            return ctx.enter_context(nc.semaphore(name))

        def sems(name, n=2):
            return [sem(f"{name}{i}") for i in range(n)]

        arena = ctx.enter_context(nc.sbuf_tensor("arena", [128, 53000], fp32))
        ps = ctx.enter_context(nc.psum_tensor("ps", [128, 8, 512], fp32))
        top = [0]

        def take(n):
            top[0] += n
            return top[0] - n

        def view(at, n):
            return arena[:, at:at + n]

        at_in = take(2 * POSITIONS)
        at_map = take(2 * POSITIONS)
        at_modes = take(KX * KY * BATCH)
        at_part = take(2 * 48 * CHANNELS)
        at_w = take(2 * KX * 64)
        at_mixed = take(2 * 768)
        at_img = take(POSITIONS)
        at_stage = take(2 * KX * BATCH)
        vin = [view(at_in + s * POSITIONS, POSITIONS) for s in range(2)]
        vmap = [view(at_map + s * POSITIONS, POSITIONS) for s in range(2)]
        modes = view(at_modes, KX * KY * BATCH).rearrange("p (y x b) -> p y x b", y=KY, x=KX)
        part = [view(at_part + s * 48 * CHANNELS, 48 * CHANNELS).rearrange("p (k c) -> p k c", c=CHANNELS)
                for s in range(2)]
        wring = [view(at_w + s * KX * 64, KX * 64).rearrange("p (x n) -> p x n", x=KX) for s in range(2)]
        mixed = [view(at_mixed + s * 768, 768) for s in range(2)]
        img = view(at_img, POSITIONS)
        stage = [view(at_stage + s * KX * BATCH, KX * BATCH).rearrange("p (x b) -> p x b", x=KX) for s in range(2)]
        kxin = [view(at_in + s * 2048, 2048) for s in range(2)]
        xhalf = [view(at_in + 4096 + s * 2048, 2048) for s in range(2)]
        gtile = [view(at_modes + s * 2048, 2048).rearrange("p (g n) -> p g n", g=16) for s in range(2)]
        expand = view(at_map + POSITIONS, BATCH * CHANNELS)
        expconv = view(at_part, BATCH * CHANNELS)
        spect = view(at_stage, 576)
        fy = view(take(192), 192).rearrange("p (h n) -> p h n", h=2)
        fx = view(take(48), 48)
        ix = view(take(128), 128)
        iy = view(take(256), 256)
        masks = view(take(128 + 128 + 32 + 64 + 8), 360)
        ident, average, image_of = masks[:, 0:128], masks[:, 128:256], masks[:, 256:288]
        head_mask, falling = masks[:, 288:352], masks[:, 352:360]
        wbd = view(take(128), 128)
        lcols = view(take(3), 3)
        qcols = view(take(2), 2)
        p0 = view(take(32), 32)
        prow = view(take(32), 32)
        pcol = view(take(4), 4)
        prt = view(take(128), 128)
        p0c = view(take(32), 32)
        prc = view(take(32), 32)
        estage = [view(take(128), 128) for _ in range(2)]
        bnst = view(take(QUADS * 8 * 6), QUADS * 8 * 6).rearrange("p (k s) -> p k s", s=6)
        mv = view(take(2), 2)
        tiny = view(take(8), 8)
        sc, sh = view(take(1), 1), view(take(1), 1)
        proj = view(take(32), 32)
        qbias = view(take(1), 1)
        eps_col = view(take(1), 1)
        hrow = [view(at_map + s * 1024, 1024) for s in range(2)]

        passed = sem("passed")
        tables_in = sem("tables_in")
        zeroed = sem("zeroed")
        grids_in = sem("grids_in")
        layer_in = sem("layer_in")
        t_ready = sem("t_ready")
        t_prod = sem("t_prod")
        e_copied = sems("e_copied")
        ld = sems("ld")
        relu_done = sem("relu_done")
        transposed = sem("transposed")
        dft_full = sem("dft_full")
        part_a, part_v = sem("part_a"), sem("part_v")
        xs_full = sem("xs_full")
        modes_a, modes_v = sem("modes_a"), sem("modes_v")
        w_in = sems("w_in")
        staged = sems("staged")
        mix_full = sems("mix_full")
        mix_ev = sems("mix_ev")
        mix_st = sems("mix_st")
        kx_in = sems("kx_in")
        ix_full = sems("ix_full")
        ix_a, ix_v = sems("ix_a"), sems("ix_v")
        ix_st = sems("ix_st")
        g_in = sems("g_in")
        out_full = sems("out_full")
        out_ev = sems("out_ev")
        stat_done = sems("stat_done")
        map_st = sems("map_st")
        bn_v, bn_p, bn_s = sem("bn_v"), sem("bn_p"), sem("bn_s")
        bn_ready = sem("bn_ready")
        vchain = sem("vchain")
        proj_full = sems("proj_full")
        proj_ev = sems("proj_ev")
        proj_st = sems("proj_st")

        at_tail = at_stage + 2 * KX * BATCH - 4 * SLOTS - 3 * SLOTS * HEADS

        COLS = SLOTS * DIM
        MAPS = (BATCH // 2) * DIM
        TCOLS = SLOTS * 128
        top[0] = 0
        tok = lambda n=COLS: view(take(n), n)
        as_slots = lambda t: t.rearrange("p (s d) -> p s d", d=DIM)
        as_heads = lambda t: t.rearrange("p (g d) -> p g d", d=HEAD_DIM)
        h0, n1, dev, sq, kk, vk, hsum, h1, n2 = (tok() for _ in range(9))
        n1t = view(take(TCOLS), TCOLS)
        kvm = view(take(4096), 4096)
        hid = [view(take(TCOLS), TCOLS) for _ in range(EXPERTS // 2)]
        clsrow = hid[0][:, 0:4096]
        hrows = view(take(256), 256)
        router = view(take(EXPERTS), EXPERTS)
        w1 = view(take(512), 512)
        w2 = view(take(256), 256).rearrange("p (e d) -> p e d", d=DIM)
        b1 = view(take(4), 4)
        b2 = view(take(DIM), DIM)
        clso = view(take(DIM), DIM)
        bf16 = mybir.dt.bfloat16
        combt = view(take(TCOLS // 2), TCOLS // 2).bitcast(bf16)
        picks = view(take(512), 512)
        pick = view(take(256), 256).bitcast(bf16)
        b2p = [view(take(DIM // 2), DIM // 2).bitcast(bf16) for _ in range(3)]
        assert top[0] <= at_tail
        comb3 = kk[:, 1320:2112].rearrange("p (s e) -> p s e", e=24)
        s1, s2, s3, s4 = (view(at_tail + SLOTS * i, SLOTS) for i in range(4))
        g1, g2, g3 = (view(at_tail + 4 * SLOTS + SLOTS * HEADS * i, SLOTS * HEADS) for i in range(3))

        tok_in = sem("tok_in")
        ln_sum, ln_root = sem("ln_sum"), sem("ln_root")
        n1_ready, kv_ready = sem("n1_ready"), sem("kv_ready")
        n2_ready = sem("n2_ready")
        job_full = sems("job_full")
        job_ev = sems("job_ev")
        cls_in = sem("cls_in")
        exp_out = sem("exp_out")
        split_ready = sem("split_ready")
        out_ready = sem("out_ready")
        stored = sem("stored")
        (J_N1T, J_N1T2, J_N1C, J_KV, J_KV2, J_CLS, J_CLS2, J_ATT, J_N2T, J_N2T2, J_N2C, J_LOG) = range(12)
        J_UP = 12
        J_CT = J_UP + 12
        J_BC = J_CT + 3
        J_OUT = J_BC + 12
        PARTS = ((0, 2048), (2048, 2048), (4096, 128))

        def bank(k):
            return 4 * (k % 2)

        def wait_full(eng, k):
            eng.wait_ge(job_full[k % 2], k // 2 + 1)

        def wait_evacuated(eng, k):
            eng.wait_ge(job_ev[k % 2], k // 2 + 1)

        def sync_tokens(sp):
            for s in range(2):
                sp.wait_ge(proj_st[s], 64 * PAIRS)
            sp.dma_start(as_slots(h0)[:, 0:BATCH // 2, :],
                         tok_d.rearrange("(s e) r (u y) -> (e r u) s y", e=2, y=DIM)).then_inc(tok_in, 16)
            sp.dma_start(as_slots(h0)[:, BATCH // 2, :], cls_tok.broadcast_to([128, DIM])).then_inc(tok_in, 16)
            sp.dma_start(hrows.rearrange("p (a d) -> p a d", a=4),
                         head_rows.unsqueeze(0).broadcast_to([128, 4, DIM])).then_inc(tok_in, 16)
            sp.dma_start(router[0:64], router_t).then_inc(tok_in, 16)
            sp.dma_start(w1[0:64].rearrange("p (e f) -> p e f", e=EXPERTS), w1_t).then_inc(tok_in, 16)
            sp.dma_start(w2, w2_rows).then_inc(tok_in, 16)
            sp.dma_start(b1, b1_cols).then_inc(tok_in, 16)
            sp.dma_start(picks[0:24], picks_d).then_inc(tok_in, 16)
            for i in range(3):
                sp.dma_start(b2[8 * i:8 * i + 8], b2_rows).then_inc(tok_in, 16)
            wait_evacuated(sp, J_CLS)
            wait_evacuated(sp, J_CLS2)
            for e in range(2):
                sp.dma_start(clso[e:BATCH:2], clsrow[0:1, 2048 * e:2048 * e + 2048]
                             .rearrange("a (b d) -> a b d", d=DIM)).then_inc(cls_in, 16)
            sp.wait_ge(out_ready, 2)
            o = as_slots(dev)
            for e in range(2):
                sp.dma_start(out[e:BATCH:2, 1:TOKENS, :].rearrange("s t d -> t s d"),
                             o[64 * e:64 * e + 64, 0:BATCH // 2, :]).then_inc(stored, 16)
            sp.dma_start(out[:, 0, :], o[0:BATCH, BATCH // 2, :]).then_inc(stored, 16)
            sp.wait_ge(stored, 48)

        def scalar_tokens(act):
            def root(k, dst, src, scale, bias):
                act.wait_ge(ln_sum, k)
                nc.scalar.activation(dst, src, ACT.Sqrt, bias=bias, scale=scale).then_inc(ln_root, 1)

            def evac(k, dst, rows, width):
                wait_full(act, k)
                src = ps[0:rows, bank(k):bank(k) + 4, :].rearrange("p b n -> p (b n)")[:, 0:width]
                nc.scalar.copy(dst, src).then_inc(job_ev[k % 2], 1)

            root(1, s3, s2, 1.0 / DIM, eps_col)
            for k, (at, n) in zip((J_N1T, J_N1T2, J_N1C), PARTS):
                evac(k, n1t[0:64, at:at + n], 64, n)
            root(2, g3, g2, 1.0 / (HEAD_DIM - 1), 0.0)
            for k, at in ((J_CLS, 0), (J_CLS2, 2048)):
                evac(k, clsrow[0:1, at:at + 2048], 1, 2048)
            root(3, s3, s2, 1.0 / DIM, eps_col)
            for k, (at, n) in zip((J_N2T, J_N2T2, J_N2C), PARTS):
                evac(k, n1t[0:64, at:at + n], 64, n)
            wait_evacuated(act, J_LOG)
            nc.scalar.activation(g2, g1, ACT.Exp).then_inc(exp_out, 1)
            for p in range(EXPERTS // 2):
                for i, (at, n) in enumerate(PARTS):
                    k = J_UP + 3 * p + i
                    wait_full(act, k)
                    src = ps[:, bank(k):bank(k) + 4, :].rearrange("p b n -> p (b n)")[:, 0:n]
                    nc.scalar.activation(hid[p][:, at:at + n], src, ACT.Gelu, bias=b1[:, p:p + 1])\
                        .then_inc(job_ev[k % 2], 1)
            for i, (at, n) in enumerate(PARTS):
                evac(J_CT + i, combt[0:24, at:at + n], 24, n)

        def tensor_tokens(pe):
            def begin(k):
                pe.wait_ge(job_ev[k % 2], k // 2)

            def cols(k, rows, width):
                return ps[rows, bank(k):bank(k) + 4, :].rearrange("p b n -> p (b n)")[:, 0:width]

            def turn(k, tiles, source, rows=slice(0, 64)):
                begin(k)
                for i, t in enumerate(tiles):
                    last = nc.tensor.transpose(cols(k, rows, 2048)[:, 128 * i:128 * i + 128], source[:, t, :],
                                               ident)
                last.then_inc(job_full[k % 2], 1)

            groups = (range(0, 16), range(16, 32), range(32, 33))
            for s in range(2):
                pe.wait_ge(proj_ev[s], PAIRS)
            pe.wait_ge(tok_in, 16 * 11)
            pe.wait_ge(n1_ready, 1)
            for k, tiles in zip((J_N1T, J_N1T2, J_N1C), groups):
                turn(k, tiles, as_slots(n1))
            pe.wait_ge(kv_ready, 1)
            k3, v3 = as_slots(kk), as_slots(vk)
            for e, k in ((0, J_KV), (1, J_KV2)):
                begin(k)
                rows = slice(64 * e, 64 * e + 64)
                for t in range(BATCH // 2):
                    dst = cols(k, slice(0, 64), 2048)[:, 64 * t:64 * t + 64]
                    nc.tensor.matmul(dst, k3[rows, t, :], v3[rows, t, :], start=True, stop=False)
                    last = nc.tensor.matmul(dst, k3[rows, BATCH // 2, :], v3[rows, BATCH // 2, :],
                                            start=False, stop=True)
                last.then_inc(job_full[k % 2], 1)
            wait_evacuated(pe, J_KV2)
            for k, at in ((J_CLS, 0), (J_CLS2, 2048)):
                begin(k)
                for c in range(4):
                    last = nc.tensor.matmul(ps[0:1, bank(k) + c, :], n1t[0:64, 4096:4097],
                                            kvm[0:64, at + 512 * c:at + 512 * c + 512], start=True, stop=True)
                last.then_inc(job_full[k % 2], 1)
            begin(J_ATT)
            for b in range(BATCH):
                t, e = b // 2, b % 2
                last = nc.tensor.matmul(cols(J_ATT, slice(64 * e, 64 * e + 64), 2048)[:, 64 * t:64 * t + 64],
                                        n1t[0:64, 128 * t + 64 * e:128 * t + 64 * e + 64],
                                        kvm[0:64, 2048 * e + 64 * t:2048 * e + 64 * t + 64], start=True, stop=True)
            last.then_inc(job_full[J_ATT % 2], 1)
            pe.wait_ge(n2_ready, 1)
            for k, tiles in zip((J_N2T, J_N2T2, J_N2C), groups):
                turn(k, tiles, as_slots(n2))
            wait_evacuated(pe, J_N2C)
            wait_evacuated(pe, J_N2T2)
            begin(J_LOG)
            for t in range(SLOTS):
                last = nc.tensor.matmul(cols(J_LOG, slice(0, 128), 264)[:, 8 * t:8 * t + 8],
                                        n1t[0:64, 128 * t:128 * t + 128], router[0:64, :], start=True, stop=True)
            last.then_inc(job_full[J_LOG % 2], 1)
            for p in range(EXPERTS // 2):
                for i, (at, n) in enumerate(PARTS):
                    k = J_UP + 3 * p + i
                    begin(k)
                    for c in range(0, n, 512):
                        w = min(512, n - c)
                        last = nc.tensor.matmul(ps[:, bank(k) + c // 512, 0:w], w1[0:64, 128 * p:128 * p + 128],
                                                n1t[0:64, at + c:at + c + w], start=True, stop=True)
                    last.then_inc(job_full[k % 2], 1)
            pe.wait_ge(split_ready, 1)
            for i, tiles in enumerate(groups):
                turn(J_CT + i, tiles, comb3, rows=slice(0, 24))
            wait_evacuated(pe, J_CT + 1)
            wait_evacuated(pe, J_CT + 2)
            for p in range(EXPERTS // 2):
                for i, (at, n) in enumerate(PARTS):
                    k = J_BC + 3 * p + i
                    begin(k)
                    for c in range(0, n, 512):
                        w = min(512, n - c)
                        last = nc.tensor.matmul(ps[:, bank(k) + c // 512, 0:w], pick[0:24, 128 * p:128 * p + 128],
                                                combt[0:24, at + c:at + c + w], start=True, stop=True)
                    last.then_inc(job_full[k % 2], 1)
            wait_evacuated(pe, J_BC + 11)
            wait_evacuated(pe, J_BC + 10)
            for k, tiles in ((J_OUT, range(32)), (J_OUT + 1, range(32, 33))):
                begin(k)
                for i, t in enumerate(tiles):
                    dst = cols(k, slice(0, 128), 2048)[:, 64 * i:64 * i + 64]
                    for p in range(EXPERTS // 2):
                        nc.tensor.matmul(dst, hid[p][:, 128 * t:128 * t + 128], w2[:, p, :], start=(p == 0),
                                         stop=False)
                    for i3 in range(3):
                        last = nc.tensor.matmul(dst, combt[0:24, 128 * t:128 * t + 128], b2p[i3][0:24, :],
                                                start=False, stop=(i3 == 2))
                last.then_inc(job_full[k % 2], 1)

        def vector_chain(dve, links):
            def link(ins):
                links[0] += 1
                ins.then_inc(vchain, 1)
                dve.wait_ge(vchain, links[0])

            def layer_norm(src, dst, k):
                x3, d3 = as_slots(src), as_slots(dev)
                wide = lambda t: t.unsqueeze(2).broadcast_to([128, SLOTS, DIM])
                link(nc.vector.reduce_sum(s1, x3, AX.X))
                link(nc.vector.tensor_scalar(s4, s1, 1.0 / DIM, None, ALU.mult))
                link(nc.vector.tensor_tensor(d3, x3, wide(s4), ALU.subtract))
                link(nc.vector.tensor_tensor(sq, dev, dev, ALU.mult))
                nc.vector.reduce_sum(s2, as_slots(sq), AX.X).then_inc(ln_sum, 1)
                dve.wait_ge(ln_root, k)
                link(nc.vector.reciprocal(s4, s3))
                link(nc.vector.tensor_tensor(as_slots(dst), d3, wide(s4), ALU.mult))

            dve.wait_ge(tok_in, 16 * 11)
            layer_norm(h0, n1, 1)
            nc.vector.tensor_tensor(hsum, h0, n1, ALU.add).then_inc(n1_ready, 1)
            n3, d3 = as_heads(n1), as_heads(dev)
            wide = lambda t: t.unsqueeze(2).broadcast_to([128, SLOTS * HEADS, HEAD_DIM])
            link(nc.vector.reduce_sum(g1, n3, AX.X))
            link(nc.vector.tensor_scalar(g2, g1, 1.0 / HEAD_DIM, None, ALU.mult))
            link(nc.vector.tensor_tensor(d3, n3, wide(g2), ALU.subtract))
            link(nc.vector.tensor_tensor(sq, dev, dev, ALU.mult))
            nc.vector.reduce_sum(g2, as_heads(sq), AX.X).then_inc(ln_sum, 1)
            dve.wait_ge(ln_root, 2)
            link(nc.vector.tensor_scalar(g1, g3, LN_EPS, None, ALU.add))
            link(nc.vector.reciprocal(g2, g1))
            link(nc.vector.tensor_tensor(as_heads(sq), d3, wide(g2), ALU.mult))
            row = lambda i: hrows[:, 64 * i:64 * i + 64].unsqueeze(1).broadcast_to([128, SLOTS, DIM])
            link(nc.vector.tensor_tensor(as_slots(kk), as_slots(sq), row(0), ALU.mult))
            link(nc.vector.tensor_tensor(as_slots(kk), as_slots(kk), row(1), ALU.add))
            link(nc.vector.tensor_tensor(as_slots(vk), as_slots(sq), row(2), ALU.mult))
            link(nc.vector.tensor_tensor(as_slots(vk), as_slots(vk), row(3), ALU.add))
            nc.vector.tensor_scalar(vk[:, MAPS:COLS], vk[:, MAPS:COLS], 1.0 / 64, None, ALU.mult)\
                .then_inc(kv_ready, 1)
            for k, at in ((J_KV, 0), (J_KV2, 2048)):
                wait_full(dve, k)
                src = ps[0:64, bank(k):bank(k) + 4, :].rearrange("p b (i d) -> p (b i) d", d=DIM)
                nc.vector.tensor_tensor(kvm[0:64, at:at + 2048].rearrange("p (i d) -> p i d", d=DIM), src,
                                        head_mask[0:64].unsqueeze(1).broadcast_to([64, 32, DIM]), ALU.mult)\
                    .then_inc(job_ev[k % 2], 1)
            wait_full(dve, J_ATT)
            link(nc.vector.tensor_copy(h1[:, MAPS:COLS], hsum[:, MAPS:COLS]))
            nc.vector.tensor_tensor(h1[:, 0:MAPS], ps[:, bank(J_ATT):bank(J_ATT) + 4, :]
                                    .rearrange("p b n -> p (b n)"), hsum[:, 0:MAPS], ALU.add)\
                .then_inc(job_ev[J_ATT % 2], 1)
            wait_evacuated(dve, J_ATT)
            dve.wait_ge(cls_in, 32)
            link(nc.vector.tensor_tensor(h1[0:BATCH, MAPS:COLS], hsum[0:BATCH, MAPS:COLS], clso[0:BATCH], ALU.add))
            layer_norm(h1, n2, 3)
            nc.vector.tensor_tensor(hsum, h1, n2, ALU.add).then_inc(n2_ready, 1)
            wait_full(dve, J_LOG)
            e3 = lambda t: t.rearrange("p (s e) -> p s e", e=EXPERTS)
            wide = lambda t: t.unsqueeze(2).broadcast_to([128, SLOTS, EXPERTS])
            fall = falling.unsqueeze(1).broadcast_to([128, SLOTS, EXPERTS])
            logits = ps[:, bank(J_LOG), 0:SLOTS * EXPERTS]
            link(nc.vector.reduce_max(s1, e3(logits), AX.X))
            nc.vector.tensor_tensor(e3(g1), e3(logits), wide(s1), ALU.subtract).then_inc(job_ev[J_LOG % 2], 1)
            wait_evacuated(dve, J_LOG)
            dve.wait_ge(exp_out, 1)
            link(nc.vector.reduce_sum(s1, e3(g2), AX.X))
            link(nc.vector.reciprocal(s2, s1))
            link(nc.vector.tensor_tensor(e3(g1), e3(g2), wide(s2), ALU.mult))
            link(nc.vector.reduce_max(s1, e3(g1), AX.X))
            first, other, key = e3(kk[:, 0:264]), e3(kk[:, 264:528]), e3(kk[:, 528:792])
            second, flag = e3(kk[:, 792:1056]), e3(kk[:, 1056:1320])
            link(nc.vector.tensor_tensor(flag, e3(g1), wide(s1), ALU.is_equal))
            link(nc.vector.tensor_tensor(key, flag, fall, ALU.mult))
            link(nc.vector.reduce_max(s2, key, AX.X))
            link(nc.vector.tensor_tensor(first, key, wide(s2), ALU.is_equal))
            link(nc.vector.scalar_tensor_tensor(out=other, in0=first, scalar=-2.0, in1=e3(g1), op0=ALU.mult,
                                                op1=ALU.add))
            link(nc.vector.reduce_max(s3, other, AX.X))
            link(nc.vector.tensor_tensor(flag, other, wide(s3), ALU.is_equal))
            link(nc.vector.tensor_tensor(key, flag, fall, ALU.mult))
            link(nc.vector.reduce_max(s2, key, AX.X))
            link(nc.vector.tensor_tensor(second, key, wide(s2), ALU.is_equal))
            link(nc.vector.tensor_tensor(flag, first, second, ALU.add))
            link(nc.vector.tensor_tensor(key, flag, e3(g1), ALU.mult))
            link(nc.vector.tensor_tensor(s4, s1, s3, ALU.add))
            link(nc.vector.tensor_scalar(s4, s4, 1e-12, None, ALU.max))
            link(nc.vector.reciprocal(s2, s4))
            link(nc.vector.tensor_tensor(flag, key, wide(s2), ALU.mult))
            def three(value, rest, half, outs):
                link(nc.vector.tensor_copy(half, value))
                link(nc.vector.tensor_copy(outs[0], half))
                link(nc.vector.tensor_tensor(rest, value, half, ALU.subtract))
                link(nc.vector.tensor_copy(half, rest))
                link(nc.vector.tensor_copy(outs[1], half))
                link(nc.vector.tensor_tensor(rest, rest, half, ALU.subtract))
                link(nc.vector.tensor_copy(outs[2], rest))

            three(flag, key, e3(vk[:, 0:132].bitcast(bf16)), [comb3[:, :, 8 * i:8 * i + 8] for i in range(3)])
            three(b2[0:24], vk[0:24, 132:196], vk[0:24, 196:228].bitcast(bf16), [t[0:24] for t in b2p])
            nc.vector.tensor_copy(pick[0:24], picks[0:24]).then_inc(split_ready, 1)
            for p in range(EXPERTS // 2):
                for i, (at, n) in enumerate(PARTS):
                    k = J_BC + 3 * p + i
                    wait_full(dve, k)
                    src = ps[:, bank(k):bank(k) + 4, :].rearrange("p b n -> p (b n)")[:, 0:n]
                    nc.vector.tensor_tensor(hid[p][:, at:at + n], hid[p][:, at:at + n], src, ALU.mult)\
                        .then_inc(job_ev[k % 2], 1)
            for k, (at, n) in ((J_OUT, (0, MAPS)), (J_OUT + 1, (MAPS, DIM))):
                wait_full(dve, k)
                src = ps[:, bank(k):bank(k) + 4, :].rearrange("p b n -> p (b n)")[:, 0:n]
                nc.vector.tensor_tensor(dev[:, at:at + n], src, hsum[:, at:at + n], ALU.add).then_inc(out_ready, 1)

        block = ctx.enter_context(nc.Block())

        def apart(eng):
            eng.sem_inc(passed, 1)

        def raw_tile(l, q):
            if isinstance(l, int) and isinstance(q, int):
                return raw_d[l, q]
            return raw_d[bass.ds(l, 1), bass.ds(q, 1), :, :].rearrange("a b p n -> (a b p) n")

        def y_step(l, q):
            return 1 + 16 * (l - 1) + q

        def x_step(l, q):
            return 1 + 16 * l + q

        def load_use(p, it):
            return 8 * p + it

        @block.sync
        def _(sp):
            for dst, src in ((fy.rearrange("p h n -> p (h n)"), fy_d), (fx, fx_d), (ix[0:48, :], ix_d),
                             (iy[0:96, :], iy_d), (masks, masks_d), (qcols, q_cols), (pcol[0:32, :], p_cols),
                             (img[0:BATCH, :], images), (p0, p_rows[0:1, :].broadcast_to([128, 32]))):
                sp.dma_start(dst, src).then_inc(tables_in, 16)
            sp.wait_ge(zeroed, 4)
            sp.dma_start(img[BATCH:BATCH + FEATURE_ROWS, :], grids_d).then_inc(grids_in, 16)
            sp.dma_start(prow[BATCH:BATCH + FEATURE_ROWS, :], p_rows[1:4, :]).then_inc(grids_in, 16)

            def layer_tables(l):
                for j in range(QUAD):
                    src = conv_w[l] if isinstance(l, int) else \
                        conv_w[bass.ds(l, 1), :, :].rearrange("a c o -> (a c) o")
                    sp.dma_start(wbd[32 * j:32 * j + 32, 32 * j:32 * j + 32], src).then_inc(layer_in, 16)
                src = layer_cols[l] if isinstance(l, int) else \
                    layer_cols[bass.ds(l, 1), :, :].rearrange("a p n -> (a p) n")
                sp.dma_start(lcols, src).then_inc(layer_in, 16)

            def weights(l, ky, s):
                src = mode_w[l, ky] if isinstance(l, int) and isinstance(ky, int) else \
                    mode_w[bass.ds(l, 1), bass.ds(ky, 1), :, :].rearrange("a b p n -> (a b p) n")
                sp.dma_start(wring[s][0:64].rearrange("p x n -> p (x n)"), src).then_inc(w_in[s], 16)

            def mix(l):
                for s in range(2):
                    sp.wait_ge(mix_full[s], 6 * l)
                    weights(l, s, s)

                def steps(it, more):
                    for s in range(2):
                        sp.wait_ge(mix_ev[s], 6 * l + it + 1)
                        for m in range(2):
                            for ri in range(2):
                                rows = mixed_d[ri * KX + m * 12:ri * KX + m * 12 + 12, bass.ds(2 * it + s, 1), :, :]
                                sp.dma_start(rows.rearrange("k a o b -> o (k a) b"),
                                             mixed[s][64 * m + 32 * ri:64 * m + 32 * ri + 32]
                                             .rearrange("o (k b) -> o k b", b=BATCH)).then_inc(mix_st[s], 16)
                        if more:
                            sp.wait_ge(mix_full[s], 6 * l + it + 1)
                            weights(l, 2 * it + s + 2, s)

                with sp.Fori(0, KY // 2 - 1) as it:
                    steps(it, True)
                steps(KY // 2 - 1, False)

                def kx_load(ky, it, s):
                    sp.wait_ge(mix_st[s], 64 * (6 * l + it + 1))
                    sp.dma_start(kxin[s][0:48], mixed_d[:, bass.ds(ky, 1), :, :].rearrange("k a o b -> k (a o b)"))\
                      .then_inc(kx_in[s], 16)

                for s in range(2):
                    kx_load(s, 0, s)

                def inverse(it, more):
                    for s in range(2):
                        sp.wait_ge(ix_a[s], 6 * l + it + 1)
                        sp.wait_ge(ix_v[s], 6 * l + it + 1)
                        dst = half_d[bass.ds(2 * (2 * it + s), 2), :, :, :].rearrange("r x g n -> (r x g) n")
                        sp.dma_start(dst, xhalf[s]).then_inc(ix_st[s], 16)
                        if more:
                            kx_load(2 * it + s + 2, it + 1, s)

                with sp.Fori(0, KY // 2 - 1) as it:
                    inverse(it, True)
                inverse(KY // 2 - 1, False)
                for s in range(2):
                    sp.wait_ge(ix_st[s], 16 * (6 * l + 6))

            def g_load(q, s):
                for x in range(4):
                    src = half_d[:, x, :, bass.ds(q * 128, 128)]
                    sp.dma_start(gtile[s][24 * x:24 * x + 24], src).then_inc(g_in[s], 16)

            def output_pass(l, first):
                for s in range(2):
                    g_load(s, s)
                    if not first:
                        sp.dma_start(vin[s], raw_tile(l - 1, s)).then_inc(ld[s], 16)

                def steps(it, more):
                    for s in range(2):
                        q = 2 * it + s
                        for h in range(2):
                            sp.wait_ge(out_ev[h], 16 * l + q + 1)
                        sp.dma_start(raw_tile(l, q), vmap[s]).then_inc(map_st[s], 16)
                        if more:
                            g_load(q + 2, s)
                            if not first:
                                sp.dma_start(vin[s], raw_tile(l - 1, q + 2)).then_inc(ld[s], 16)

                with sp.Fori(0, PAIRS - 1) as it:
                    steps(it, True)
                steps(PAIRS - 1, False)

            def spectrum_pass(l):
                def load(it, s):
                    sp.wait_ge(map_st[s], 16 * (8 * (l - 1) + it + 1))
                    sp.dma_start(vin[s], raw_tile(l - 1, 2 * it + s)).then_inc(ld[s], 16)

                for s in range(2):
                    load(0, s)
                with sp.Fori(0, PAIRS - 1) as it:
                    for s in range(2):
                        sp.wait_ge(transposed, y_step(l, 2 * it + s) + 1)
                        load(it + 1, s)
                for s in range(2):
                    sp.wait_ge(transposed, y_step(l, QUADS - 2 + s) + 1)
                    apart(sp)

            layer_tables(0)
            mix(0)
            output_pass(0, True)
            with sp.Fori(1, LAYERS) as l:
                spectrum_pass(l)
                layer_tables(l)
                mix(l)
                output_pass(l, False)

            for s in range(2):
                sp.wait_ge(map_st[s], 16 * (8 * (LAYERS - 1) + 1))
                sp.dma_start(vin[s], raw_d[LAYERS - 1, s]).then_inc(ld[s], 16)

            def project(it, more):
                for s in range(2):
                    sp.wait_ge(proj_ev[s], it + 1)
                    for c in range(4):
                        dst = tok_d[bass.ds((2 * it + s) * QUAD, QUAD), c:c + 5:4, :]
                        sp.dma_start(dst, hrow[s][32 * c:32 * c + QUAD].rearrange("j (r n) -> j r n", r=2))\
                          .then_inc(proj_st[s], 16)
                    if more:
                        sp.wait_ge(map_st[s], 16 * (8 * (LAYERS - 1) + it + 2))
                        sp.dma_start(vin[s], raw_tile(LAYERS - 1, 2 * it + s + 2)).then_inc(ld[s], 16)

            with sp.Fori(0, PAIRS - 1) as it:
                project(it, True)
            project(PAIRS - 1, False)
            sync_tokens(sp)

        @block.gpsimd
        def _(pool):
            def mix(l):
                pool.wait_ge(modes_a, x_step(l, QUADS))
                pool.wait_ge(modes_v, x_step(l, QUADS))
                apart(pool)
                with pool.Fori(0, KY // 2) as it:
                    for s in range(2):
                        pool.wait_ge(w_in[s], 16 * (6 * l + it + 1))
                        pool.wait_ge(mix_full[s], 6 * l + it)
                        pool.wait_ge(staged[1 - s], 2 * (6 * l + it + s))
                        apart(pool)
                        nc.gpsimd.tensor_scalar(wring[s][32:64, :, 0:32], wring[s][32:64, :, 0:32], -1.0, None,
                                                ALU.mult).then_inc(staged[s], 1)
                        pool.wait_ge(staged[s], 2 * (6 * l + it) + 1)
                        src = modes[0:64, bass.ds(2 * it + s, 1), :, :].rearrange("p a x b -> p (a x) b")
                        nc.gpsimd.tensor_copy(stage[s][0:64], src).then_inc(staged[s], 1)

            mix(0)
            with pool.Fori(1, LAYERS) as l:
                mix(l)

        @block.scalar
        def _(act):
            def part_evac(l, q, s, c):
                for h in range(2):
                    act.wait_ge(dft_full, 2 * c + h + 1)
                    if h == 0 and not isinstance(c, int):
                        act.wait_ge(xs_full, x_step(l, q) - 1)
                    for ri in range(2):
                        src = ps[0:64, 2 * h:2 * h + 2, 0:384].rearrange("p b (c n) -> p n b c", c=4)
                        last = nc.scalar.copy(
                            part[s][64 * ri:64 * ri + 64, :, 16 * h:16 * h + 16:2]
                            .rearrange("p k (b c) -> p k b c", c=4),
                            src[:, 48 * ri:48 * ri + 48])
                    last.then_inc(part_a, 1)

            def modes_evac(q, s, c):
                act.wait_ge(xs_full, c + 1)
                for j in range(2):
                    for ri in range(2):
                        src = ps[32 * j:32 * j + 32, 4 + 2 * s:6 + 2 * s, 0:288]\
                            .rearrange("p h (y r x) -> p h y r x", y=6, r=2)[:, :, :, ri, :]
                        dst = modes[32 * ri:32 * ri + 32, :, :, bass.ds(QUAD * q + j, 1)]\
                            .rearrange("p (h y) x b -> p h y (x b)", h=2)
                        last = nc.scalar.copy(dst, src)
                last.then_inc(modes_a, 1)

            def relu(p, it, s):
                act.wait_ge(ld[s], 16 * (load_use(p, it) + 1))
                nc.scalar.activation(vin[s], vin[s], ACT.Relu, bias=sh, scale=sc).then_inc(relu_done, 1)

            def mix(l):
                with act.Fori(0, KY // 2) as it:
                    for s in range(2):
                        act.wait_ge(mix_full[s], 6 * l + it + 1)
                        act.wait_ge(mix_st[s], 64 * (6 * l + it))
                        nc.scalar.copy(mixed[s].rearrange("p (h n) -> p h n", h=2), ps[:, 2 * s:2 * s + 2, 0:384])\
                            .then_inc(mix_ev[s], 1)
                with act.Fori(0, KY // 2) as it:
                    for s in range(2):
                        act.wait_ge(ix_full[s], 6 * l + it + 1)
                        act.wait_ge(ix_st[s], 16 * (6 * l + it))
                        nc.scalar.copy(xhalf[s][:, 0:1024].rearrange("p (h n) -> p h n", h=2),
                                       ps[:, 4 * s:4 * s + 2, :]).then_inc(ix_a[s], 1)

            def map_evac(l, it, s):
                for h in range(2):
                    act.wait_ge(out_full[h], 16 * l + 2 * it + s + 1)
                    if h == 0:
                        act.wait_ge(map_st[s], 16 * (8 * l + it))
                        act.wait_ge(stat_done[s], 8 * l + it)
                    nc.scalar.copy(vmap[s][:, 2048 * h:2048 * h + 2048].rearrange("p (b n) -> p b n", b=4),
                                   ps[:, 4 * h:4 * h + 4, :]).then_inc(out_ev[h], 1)

            def norm_root(l):
                act.wait_ge(bn_p, 2 * l + 2)
                nc.scalar.activation(tiny[:, 3:4], ps[:, 1, 0:1], ACT.Sqrt, bias=eps_col).then_inc(bn_s, 1)

            act.wait_ge(zeroed, 5)
            part_evac(0, 0, 0, 0)
            act.wait_ge(xs_full, 1)
            nc.scalar.copy(spect[:, 0:288], ps[:, 4, 0:288]).then_inc(modes_a, 1)
            with act.Fori(0, PAIRS) as it:
                for s in range(2):
                    modes_evac(2 * it + s, s, x_step(0, 2 * it + s))
            mix(0)
            with act.Fori(0, PAIRS) as it:
                for s in range(2):
                    map_evac(0, it, s)
            norm_root(0)

            with act.Fori(1, LAYERS) as l:
                act.wait_ge(bn_ready, l)
                relu(2 * l - 2, 0, 0)
                relu(2 * l - 2, 0, 1)
                part_evac(l, 0, 0, y_step(l, 0))
                with act.Fori(0, PAIRS - 1) as it:
                    for s in range(2):
                        relu(2 * l - 2, it + 1, s)
                        part_evac(l, 2 * it + s + 1, 1 - s, y_step(l, 2 * it + s + 1))
                        modes_evac(2 * it + s, s, x_step(l, 2 * it + s))
                part_evac(l, QUADS - 1, 1, y_step(l, QUADS - 1))
                for s in range(2):
                    modes_evac(QUADS - 2 + s, s, x_step(l, QUADS - 2 + s))
                mix(l)
                relu(2 * l - 1, 0, 0)
                relu(2 * l - 1, 0, 1)
                with act.Fori(0, PAIRS - 1) as it:
                    for s in range(2):
                        map_evac(l, it, s)
                        relu(2 * l - 1, it + 1, s)
                for s in range(2):
                    map_evac(l, PAIRS - 1, s)
                norm_root(l)

            act.wait_ge(bn_v, 3 * LAYERS + 2)
            act.wait_ge(map_st[0], 16 * 8 * LAYERS)
            act.wait_ge(map_st[1], 16 * 8 * LAYERS)
            with act.Fori(0, PAIRS) as it:
                for s in range(2):
                    act.wait_ge(proj_full[s], it + 1)
                    act.wait_ge(proj_st[s], 64 * it)
                    nc.scalar.activation(hrow[s].rearrange("p (r n) -> p r n", r=2), ps[:, 2 * s:2 * s + 2, :],
                                         ACT.Identity, bias=qbias).then_inc(proj_ev[s], 1)
            scalar_tokens(act)

        @block.tensor
        def _(pe):
            def y_transform(l, q, s, c):
                pe.wait_ge(transposed, c + 1)
                blocks = vmap[s].rearrange("p (h d m) -> p h d m", h=2, d=16)
                for h in range(2):
                    if not isinstance(c, int):
                        pe.wait_ge(part_a, 2 * c + h - 1)
                        pe.wait_ge(part_v, 2 * c + h - 1)
                    for d in range(8 * h, 8 * h + 8):
                        for yh in range(2):
                            last = nc.tensor.matmul(ps[:, d // 4, 96 * (d % 4):96 * (d % 4) + 96],
                                                    blocks[:, yh, d], fy[:, yh, :], start=(yh == 0), stop=(yh == 1))
                    last.then_inc(dft_full, 1)

            def x_transform(l, q, s, c, x):
                pe.wait_ge(part_a, 2 * c + 2)
                pe.wait_ge(part_v, 2 * c + 2)
                if not isinstance(x, int):
                    pe.wait_ge(modes_a, x - 1)
                    pe.wait_ge(modes_v, x - 1)
                for ky in range(KY):
                    last = nc.tensor.matmul(ps[:, 4 + 2 * s + ky // 6, 48 * (ky % 6):48 * (ky % 6) + 48],
                                            part[s][:, 4 * ky:4 * ky + 4, :].rearrange("p j c -> p (j c)"), fx,
                                            start=True, stop=True)
                last.then_inc(xs_full, 1)

            def mix(l):
                with pe.Fori(0, KY // 2) as it:
                    for s in range(2):
                        pe.wait_ge(staged[s], 2 * (6 * l + it + 1))
                        pe.wait_ge(mix_ev[s], 6 * l + it)
                        apart(pe)
                        for k in range(KX):
                            m, i = k // 12, k % 12
                            last = nc.tensor.matmul(ps[64 * m:64 * m + 64, 2 * s + i // 6, 64 * (i % 6):64 * (i % 6) + 64],
                                                    wring[s][0:64, k, :], stage[s][0:64, k, :], start=True, stop=True)
                        last.then_inc(mix_full[s], 1)
                for s in range(2):
                    pe.wait_ge(mix_ev[s], 6 * l + 6)
                apart(pe)
                with pe.Fori(0, KY // 2) as it:
                    for s in range(2):
                        pe.wait_ge(kx_in[s], 16 * (6 * l + it + 1))
                        pe.wait_ge(ix_a[s], 6 * l + it)
                        pe.wait_ge(ix_v[s], 6 * l + it)
                        for g in range(4):
                            rows = kxin[s][0:48].rearrange("k (o b) -> k b o", b=BATCH)[:, 16 * g:16 * g + 16, :]
                            last = nc.tensor.matmul(ps[:, 4 * s + g, :], ix[0:48, :], rows, start=True, stop=True)
                        last.then_inc(ix_full[s], 1)
                for s in range(2):
                    pe.wait_ge(ix_a[s], 6 * l + 6)
                    pe.wait_ge(ix_v[s], 6 * l + 6)
                apart(pe)

            def map_out(l, it, s, stationary, source):
                pe.wait_ge(g_in[s], 64 * (8 * l + it + 1))
                for h in range(2):
                    pe.wait_ge(out_ev[h], 16 * l + 2 * it + s)
                    for k in range(4):
                        n = 4 * h + k
                        nc.tensor.matmul(ps[:, n, :], stationary, source[:, 512 * n:512 * n + 512],
                                         start=True, stop=False)
                        for g in range(2):
                            last = nc.tensor.matmul(ps[:, n, 256 * g:256 * g + 256], gtile[s][0:96, 2 * n + g, :],
                                                    iy[0:96, :], start=False, stop=(g == 1))
                    last.then_inc(out_full[h], 1)

            def norm_sums(l):
                for k in range(2):
                    pe.wait_ge(bn_v, 3 * l + 1 + k)
                    if k == 0:
                        for h in range(2):
                            pe.wait_ge(out_ev[h], 16 * l + 16)
                    nc.tensor.matmul(ps[:, k, 0:1], average, (mv if k == 0 else tiny)[:, 0:1], start=True, stop=True)\
                        .then_inc(bn_p, 1)

            pe.wait_ge(tables_in, 16 * 9)
            y_transform(0, 0, 0, 0)
            x_transform(0, 0, 0, 0, 0)
            pe.wait_ge(layer_in, 80)
            pe.wait_ge(t_ready, 2)
            nc.tensor.matmul(ps[:, 0, 0:32], pcol[0:32, 0:1].broadcast_to([32, 128]), wbd[0:32, 0:32],
                             start=True, stop=True)
            nc.tensor.matmul(ps[:, 1, 0:32], prt[0:32, :], wbd[0:32, 0:32], start=True, stop=True)\
                .then_inc(t_prod, 1)
            pe.wait_ge(modes_a, 1)
            pe.wait_ge(modes_v, 1)
            with pe.Fori(0, PAIRS) as it:
                for s in range(2):
                    pe.wait_ge(e_copied[s], it + 1)
                    pe.wait_ge(modes_a, 2 * it + s)
                    pe.wait_ge(modes_v, 2 * it + s)
                    for h in range(2):
                        last = nc.tensor.matmul(ps[:, 4 + 2 * s + h, 0:288], estage[s], spect[:, 288 * h:288 * h + 288],
                                                start=True, stop=True)
                    last.then_inc(xs_full, 1)
            mix(0)
            with pe.Fori(0, PAIRS) as it:
                for s in range(2):
                    pe.wait_ge(e_copied[s], 8 + it + 1)
                    map_out(0, it, s, estage[s], img)
            norm_sums(0)

            with pe.Fori(1, LAYERS) as l:
                pe.wait_ge(bn_ready, l)
                y_transform(l, 0, 0, y_step(l, 0))
                with pe.Fori(0, PAIRS - 1) as it:
                    for s in range(2):
                        q = 2 * it + s
                        y_transform(l, q + 1, 1 - s, y_step(l, q + 1))
                        x_transform(l, q, s, y_step(l, q), x_step(l, q))
                y_transform(l, QUADS - 1, 1, y_step(l, QUADS - 1))
                for s in range(2):
                    x_transform(l, QUADS - 2 + s, s, y_step(l, QUADS - 2 + s), x_step(l, QUADS - 2 + s))
                pe.wait_ge(layer_in, 80 * (l + 1))
                apart(pe)
                mix(l)
                with pe.Fori(0, PAIRS) as it:
                    for s in range(2):
                        pe.wait_ge(relu_done, 16 * (2 * l - 1) + 2 * it + s + 1)
                        map_out(l, it, s, wbd, vin[s])
                norm_sums(l)

            pe.wait_ge(bn_v, 3 * LAYERS + 1)
            nc.tensor.matmul(ps[:, 7, 0:1], tiny[:, 6:7].broadcast_to([128, 128]), tiny[:, 7:8], start=True, stop=True)\
                .then_inc(bn_p, 1)
            with pe.Fori(0, PAIRS) as it:
                for s in range(2):
                    pe.wait_ge(ld[s], 16 * (load_use(2 * LAYERS - 2, it) + 1))
                    pe.wait_ge(proj_ev[s], it)
                    for n in range(8):
                        last = nc.tensor.matmul(ps[32 * (n % 4):32 * (n % 4) + 32, 2 * s + n // 4, :], proj,
                                                vin[s][:, 512 * n:512 * n + 512], start=True, stop=True)
                    last.then_inc(proj_full[s], 1)
            tensor_tokens(pe)

        @block.vector
        def _(dve):
            links = [0]

            def link(ins):
                links[0] += 1
                ins.then_inc(vchain, 1)
                dve.wait_ge(vchain, links[0])

            def part_evac(l, q, s, c):
                for h in range(2):
                    dve.wait_ge(dft_full, 2 * c + h + 1)
                    if h == 0 and not isinstance(c, int):
                        dve.wait_ge(xs_full, x_step(l, q) - 1)
                    for ri in range(2):
                        src = ps[64:128, 2 * h:2 * h + 2, 0:384].rearrange("p b (c n) -> p n b c", c=4)
                        last = nc.vector.tensor_copy(
                            part[s][64 * ri:64 * ri + 64, :, 16 * h + 1:16 * h + 16:2]
                            .rearrange("p k (b c) -> p k b c", c=4), src[:, 48 * ri:48 * ri + 48])
                    last.then_inc(part_v, 1)

            def modes_evac(q, s, c):
                dve.wait_ge(xs_full, c + 1)
                for j in range(2, 4):
                    for ri in range(2):
                        src = ps[32 * j:32 * j + 32, 4 + 2 * s:6 + 2 * s, 0:288]\
                            .rearrange("p h (y r x) -> p h y r x", y=6, r=2)[:, :, :, ri, :]
                        dst = modes[32 * ri:32 * ri + 32, :, :, bass.ds(QUAD * q + j, 1)]\
                            .rearrange("p (h y) x b -> p h y (x b)", h=2)
                        last = nc.vector.tensor_copy(dst, src)
                last.then_inc(modes_v, 1)

            def y_rows(tile):
                return tile.rearrange("p (h c x) -> p x h c", h=2, x=SIDE)

            def x_y(tile):
                return tile.rearrange("p (x h y) -> p x h y", h=2, x=SIDE)

            def block_transpose(l, q, s, c):
                dve.wait_ge(relu_done, 16 * (2 * l - 2) + q + 1)
                dve.wait_ge(dft_full, 2 * c - 2)
                nc.vector.transpose(y_rows(vmap[s]), x_y(vin[s])).then_inc(transposed, 1)

            def mix(l):
                with dve.Fori(0, KY // 2) as it:
                    for s in range(2):
                        dve.wait_ge(ix_full[s], 6 * l + it + 1)
                        dve.wait_ge(ix_st[s], 16 * (6 * l + it))
                        nc.vector.tensor_copy(xhalf[s][:, 1024:2048].rearrange("p (h n) -> p h n", h=2),
                                              ps[:, 4 * s + 2:4 * s + 4, :]).then_inc(ix_v[s], 1)

            def statistics(l, it, s):
                for h in range(2):
                    dve.wait_ge(out_ev[h], 16 * l + 2 * it + s + 1)
                    for k in range(4):
                        n = 4 * h + k
                        last = nc.vector.bn_stats(
                            out=bnst[:, bass.ds((2 * it + s) * 8 + n, 1), :].rearrange("p a s -> p (a s)"),
                            in_=vmap[s][:, 512 * n:512 * n + 512])
                last.then_inc(stat_done[s], 1)

            def norm(l, first):
                for s in range(2):
                    dve.wait_ge(stat_done[s], 8 * l + 8)
                dve.wait_ge(layer_in, 80 * (l + 1))
                apart(dve)
                nc.vector.bn_aggr(out=mv, in_=bnst).then_inc(bn_v, 1)
                dve.wait_ge(bn_p, 2 * l + 1)
                dve.wait_ge(bn_v, 3 * l + 1)
                nc.vector.tensor_tensor(tiny[:, 1:2], mv[:, 0:1], ps[:, 0, 0:1], ALU.subtract).then_inc(t_ready, 1)
                dve.wait_ge(t_ready, 4 + 6 * l + 1)
                nc.vector.scalar_tensor_tensor(out=tiny[:, 0:1], in0=tiny[:, 1:2], scalar=tiny[:, 1:2],
                                               in1=mv[:, 1:2], op0=ALU.mult, op1=ALU.add).then_inc(bn_v, 1)
                nc.vector.tensor_tensor(tiny[:, 2:3], ps[:, 0, 0:1], lcols[:, 0:1], ALU.add).then_inc(t_ready, 1)
                dve.wait_ge(t_ready, 4 + 6 * l + 2)
                nc.vector.tensor_tensor(tiny[:, 4:5], lcols[:, 0:1], tiny[:, 2:3], ALU.subtract).then_inc(t_ready, 1)
                dve.wait_ge(bn_s, l + 1)
                nc.vector.reciprocal(tiny[:, 5:6], tiny[:, 3:4]).then_inc(t_ready, 1)
                dve.wait_ge(t_ready, 4 + 6 * l + 4)
                nc.vector.tensor_tensor(sc, tiny[:, 5:6], lcols[:, 1:2], ALU.mult).then_inc(t_ready, 1)
                dve.wait_ge(t_ready, 4 + 6 * l + 5)
                nc.vector.scalar_tensor_tensor(out=sh, in0=sc, scalar=tiny[:, 4:5], in1=lcols[:, 2:3],
                                               op0=ALU.mult, op1=ALU.add).then_inc(t_ready, 1)
                dve.wait_ge(t_ready, 4 + 6 * l + 6)
                nc.vector.tensor_copy(tiny[:, 6:7], sh).then_inc(bn_v, 1)
                dve.wait_ge(bn_v, 3 * l + 3)
                nc.vector.tensor_copy(tiny[:, 7:8], sh).then_inc(bn_ready, 1)

            nc.vector.memset(img[64:128, :], 0.0).then_inc(zeroed, 1)
            nc.vector.memset(prow, 0.0).then_inc(zeroed, 1)
            nc.vector.memset(wbd, 0.0).then_inc(zeroed, 1)
            nc.vector.memset(prt, 0.0).then_inc(zeroed, 1)
            nc.vector.memset(eps_col, BN_EPS).then_inc(zeroed, 1)

            dve.wait_ge(tables_in, 16 * 9)
            dve.wait_ge(grids_in, 32)
            dve.wait_ge(zeroed, 5)
            nc.vector.transpose(y_rows(vmap[0]), x_y(img)).then_inc(transposed, 1)
            exp3 = expand.rearrange("p (b c) -> p b c", c=CHANNELS)
            link(nc.vector.tensor_tensor(exp3, ident[:, 0:BATCH].unsqueeze(2).broadcast_to([128, BATCH, CHANNELS]),
                                         p0.unsqueeze(1).broadcast_to([128, BATCH, CHANNELS]), ALU.mult))
            nc.vector.tensor_tensor(exp3, exp3, prow.unsqueeze(1).broadcast_to([128, BATCH, CHANNELS]),
                                    ALU.add).then_inc(t_ready, 1)
            nc.vector.tensor_copy(prt[0:32, BATCH:BATCH + FEATURE_ROWS], pcol[0:32, 1:4]).then_inc(t_ready, 1)
            part_evac(0, 0, 0, 0)
            dve.wait_ge(xs_full, 1)
            nc.vector.tensor_copy(spect[:, 288:576], ps[:, 5, 0:288]).then_inc(modes_v, 1)
            dve.wait_ge(t_prod, 1)
            nc.vector.tensor_copy(p0c, ps[:, 0, 0:32])
            link(nc.vector.tensor_copy(prc, ps[:, 1, 0:32]))
            expc3 = expconv.rearrange("p (b c) -> p b c", c=CHANNELS)
            nc.vector.tensor_tensor(expc3, ident[:, 0:BATCH].unsqueeze(2).broadcast_to([128, BATCH, CHANNELS]),
                                    p0c.unsqueeze(1).broadcast_to([128, BATCH, CHANNELS]), ALU.mult).then_inc(t_ready, 1)
            dve.wait_ge(t_ready, 3)
            nc.vector.tensor_tensor(expc3, expc3, prc.unsqueeze(1).broadcast_to([128, BATCH, CHANNELS]),
                                    ALU.add).then_inc(t_ready, 1)
            dve.wait_ge(t_ready, 4)
            with dve.Fori(0, PAIRS) as it:
                for s in range(2):
                    q = 2 * it + s
                    dve.wait_ge(xs_full, q)
                    nc.vector.tensor_copy(estage[s], expand[:, bass.ds(q * 128, 128)]).then_inc(e_copied[s], 1)
                    modes_evac(q, s, x_step(0, q))
            mix(0)
            for s in range(2):
                nc.vector.tensor_copy(estage[s], expconv[:, 128 * s:128 * s + 128]).then_inc(e_copied[s], 1)

            def expand_stats(it, more):
                for s in range(2):
                    statistics(0, it, s)
                    if more:
                        nc.vector.tensor_copy(estage[s], expconv[:, bass.ds((2 * it + s + 2) * 128, 128)])\
                            .then_inc(e_copied[s], 1)

            with dve.Fori(0, PAIRS - 1) as it:
                expand_stats(it, True)
            expand_stats(PAIRS - 1, False)
            norm(0, True)

            with dve.Fori(1, LAYERS) as l:
                for s in range(2):
                    dve.wait_ge(map_st[s], 16 * 8 * l)
                block_transpose(l, 0, 0, y_step(l, 0))
                block_transpose(l, 1, 1, y_step(l, 1))
                part_evac(l, 0, 0, y_step(l, 0))
                with dve.Fori(0, PAIRS - 1) as it:
                    for s in range(2):
                        q = 2 * it + s
                        block_transpose(l, q + 2, s, y_step(l, q + 2))
                        part_evac(l, q + 1, 1 - s, y_step(l, q + 1))
                        modes_evac(q, s, x_step(l, q))
                part_evac(l, QUADS - 1, 1, y_step(l, QUADS - 1))
                for s in range(2):
                    modes_evac(QUADS - 2 + s, s, x_step(l, QUADS - 2 + s))
                mix(l)
                with dve.Fori(0, PAIRS) as it:
                    for s in range(2):
                        statistics(l, it, s)
                norm(l, False)

            dve.wait_ge(bn_ready, LAYERS)
            link(nc.vector.tensor_tensor(tiny[:, 1:2], sc, qcols[:, 0:1], ALU.mult))
            link(nc.vector.tensor_scalar(proj, image_of, tiny[:, 1:2], None, ALU.mult))
            nc.vector.tensor_scalar(tiny[:, 7:8], qcols[:, 0:1], 1.0 / QUAD, None, ALU.mult).then_inc(bn_v, 1)
            dve.wait_ge(bn_p, 2 * LAYERS + 1)
            nc.vector.tensor_tensor(qbias, ps[:, 7, 0:1], qcols[:, 1:2], ALU.add).then_inc(bn_v, 1)
            vector_chain(dve, links)


INPUTS = ["images", "p_rows", "p_cols", "mode_w", "conv_w", "layer_cols", "q_cols", "cls_tok", "head_rows",
          "router_t", "w1_t", "b1_cols", "w2_rows", "b2_rows", "fy", "fx", "ix", "iy", "grids", "masks", "picks"]


def laid_out(x, cls_tok, L0_tok_p_w, L0_tok_p_b, L0_tok_fw1, L0_tok_fw2, L0_tok_w_w, L0_tok_w_b, L0_tok_bn_g,
             L0_tok_bn_b, L0_tok_q_w, L0_tok_q_b, L0_attn_kln_weight, L0_attn_kln_bias, L0_attn_vln_weight,
             L0_attn_vln_bias, L0_ffn_router_w, L0_ffn_w1, L0_ffn_b1, L0_ffn_w2, L0_ffn_b2):
    a = np.asarray
    p_rows = np.concatenate([a(L0_tok_p_w), a(L0_tok_p_b).reshape(1, -1)])
    f = np.stack([a(L0_tok_fw1), a(L0_tok_fw2)], axis=1)
    f = f.transpose(0, 5, 6, 2, 1, 4, 3).reshape(LAYERS, KY, 2, CHANNELS, KX, CHANNELS)
    direct, swapped = f.transpose(0, 1, 3, 4, 2, 5), f[:, :, ::-1].transpose(0, 1, 3, 4, 2, 5)
    mode_w = np.stack([direct, swapped], axis=2).reshape(LAYERS, KY, 64, KX * 64)
    cols = np.stack([a(L0_tok_w_b), a(L0_tok_bn_g), a(L0_tok_bn_b)], axis=2)
    layer_cols = np.tile(cols, (1, QUAD, 1))
    q_cols = np.stack([np.tile(a(L0_tok_q_w)[:, 0], QUAD), np.tile(a(L0_tok_q_b), 128)], axis=1)
    head_rows = np.stack([a(v).reshape(-1) for v in
                          (L0_attn_kln_weight, L0_attn_kln_bias, L0_attn_vln_weight, L0_attn_vln_bias)])
    fy, fx, ix, iy = transform_tables()
    grids, masks, picks = shape_tables()
    return {
        "images": a(x).reshape(BATCH, POSITIONS), "p_rows": p_rows, "p_cols": p_rows.T, "mode_w": mode_w,
        "conv_w": a(L0_tok_w_w), "layer_cols": layer_cols, "q_cols": q_cols, "cls_tok": a(cls_tok).reshape(1, DIM),
        "head_rows": head_rows, "router_t": a(L0_ffn_router_w).T, "w1_t": a(L0_ffn_w1).transpose(1, 0, 2),
        "b1_cols": a(L0_ffn_b1).reshape(EXPERTS // 2, 128).T, "w2_rows": a(L0_ffn_w2).reshape(EXPERTS // 2, 128, DIM)
        .transpose(1, 0, 2), "b2_rows": a(L0_ffn_b2), "fy": fy, "fx": fx, "ix": ix, "iy": iy, "grids": grids,
        "masks": masks, "picks": picks}


def kernel(**inputs):
    import concourse.bacc as bacc
    from concourse.bass_utils import run_bass_kernel_spmd

    nc = bacc.Bacc("TRN2", target_bir_lowering=False, num_devices=1)
    laid = laid_out(**inputs)
    arrays, args = {}, []
    for name in INPUTS:
        array = np.ascontiguousarray(laid[name])
        arrays[f"in_{name}"] = array
        args.append(nc.dram_tensor(f"in_{name}", array.shape, mybir.dt.from_np(array.dtype), kind="ExternalInput").ap())
    out = nc.dram_tensor("out_tokens", (BATCH, TOKENS, DIM), mybir.dt.float32, kind="ExternalOutput").ap()
    tower_kernel(nc, *args, out)
    r = run_bass_kernel_spmd(nc, [arrays], core_ids=[0])
    return r.results[0]["out_tokens"]
```

```python
import numpy as np
import concourse.bass as bass
from concourse import mybir
from contextlib import ExitStack

BATCH, SIDE, CHANNELS, LAYERS = 64, 64, 32, 4
KX_HALF, KY = 12, 12
KX = 2 * KX_HALF
POSITIONS = SIDE * SIDE
QUAD = 4
QUADS = BATCH // QUAD
PAIRS = QUADS // 2
FEATURE_ROWS = 3
BN_EPS = 1e-5
HEADS, HEAD_DIM = 8, 8
DIM = HEADS * HEAD_DIM
EXPERTS = 8
TOKENS = SIDE + 1
LN_EPS = 1e-5
SLOTS = BATCH // 2 + 1


def transform_tables():
    kx = np.concatenate([np.arange(KX_HALF), np.arange(SIDE - KX_HALF, SIDE)]).astype(np.float64)
    ky = np.arange(KY, dtype=np.float64)
    pos = np.arange(SIDE, dtype=np.float64)
    ang = 2 * np.pi * np.outer(pos, ky) / SIDE
    fy = np.zeros((2, QUAD, 32, 2, KY, QUAD))
    for half in range(2):
        for j in range(QUAD):
            fy[half, j, :, 0, :, j] = np.cos(ang[half * 32:half * 32 + 32])
            fy[half, j, :, 1, :, j] = -np.sin(ang[half * 32:half * 32 + 32])
    ang = 2 * np.pi * np.outer(pos, kx) / SIDE
    fx = np.zeros((2, SIDE, 2, KX))
    fx[0, :, 0], fx[1, :, 0] = np.cos(ang), np.sin(ang)
    fx[0, :, 1], fx[1, :, 1] = -np.sin(ang), np.cos(ang)
    order = (np.arange(4)[:, None] + 4 * np.arange(16)[None, :]).reshape(-1)
    ang = 2 * np.pi * np.outer(kx, pos[order]) / SIDE
    ix = np.zeros((2, KX, 2, SIDE))
    ix[0, :, 0], ix[1, :, 0] = np.cos(ang), -np.sin(ang)
    ix[0, :, 1], ix[1, :, 1] = np.sin(ang), np.cos(ang)
    ix = (ix / SIDE).reshape(48, 128)
    ix2 = np.zeros((2, 48, 2, 128))
    ix2[0, :, 0], ix2[1, :, 1] = ix, ix
    ang = 2 * np.pi * np.outer(ky, pos) / SIDE
    weight = np.where(ky == 0, 1.0, 2.0)[:, None] / SIDE
    iy = np.zeros((4, KY, 2, 4, SIDE))
    for x in range(4):
        iy[x, :, 0, x], iy[x, :, 1, x] = weight * np.cos(ang), -weight * np.sin(ang)
    table = lambda a, rows: np.ascontiguousarray(a.reshape(rows, -1), dtype=np.float32)
    return (np.ascontiguousarray(fy.reshape(2, 128, 96).transpose(1, 0, 2).reshape(128, 192), dtype=np.float32),
            table(fx, 128), table(ix2, 96), table(iy, 96))


def shape_tables():
    line = np.linspace(0.0, 1.0, SIDE, dtype=np.float32)
    grids = np.ones((FEATURE_ROWS, SIDE, SIDE), np.float32)
    grids[0] = line[:, None]
    grids[1] = line[None, :]
    p = np.arange(128)
    ident = np.eye(128, dtype=np.float32)
    average = (p[:, None] % 32 == p[None, :] % 32).astype(np.float32) / QUAD
    image_of = (p[:, None] // 32 == np.arange(32)[None, :]).astype(np.float32)
    head = np.arange(64) // HEAD_DIM
    heads = (head[:, None] == head[None, :]).astype(np.float32) / np.float32(TOKENS)
    heads = np.concatenate([heads, heads])
    picks = np.tile(np.repeat(np.eye(EXPERTS, dtype=np.float32), 64, axis=1), (3, 1))
    falling = np.tile(np.arange(EXPERTS, 0, -1, dtype=np.float32), (128, 1))
    return (grids.reshape(FEATURE_ROWS, POSITIONS),
            np.ascontiguousarray(np.concatenate([ident, average, image_of, heads, falling], axis=1)), picks)


def tower_kernel(nc, images, p_rows, p_cols, mode_w, conv_w, layer_cols, q_cols, cls_tok, head_rows,
                 router_t, w1_t, b1_cols, w2_rows, b2_rows, fy_d, fx_d, ix_d, iy_d, grids_d, masks_d, picks_d, out):
    fp32 = mybir.dt.float32
    ALU = mybir.AluOpType
    ACT = mybir.ActivationFunctionType
    AX = mybir.AxisListType

    raw_d = nc.dram_tensor("raw_maps", [LAYERS, QUADS, 128, POSITIONS], fp32, kind="Internal").ap()
    mixed_d = nc.dram_tensor("mixed_modes", [2 * KX, KY, CHANNELS, BATCH], fp32, kind="Internal").ap()
    half_d = nc.dram_tensor("half_inverse", [KY * 2, 4, 16, BATCH * CHANNELS], fp32, kind="Internal").ap()
    tok_d = nc.dram_tensor("token_maps", [BATCH, 8, 512], fp32, kind="Internal").ap()

    ctx = ExitStack()
    with ctx:
        def sem(name):
            return ctx.enter_context(nc.semaphore(name))

        def sems(name, n=2):
            return [sem(f"{name}{i}") for i in range(n)]

        arena = ctx.enter_context(nc.sbuf_tensor("arena", [128, 53000], fp32))
        ps = ctx.enter_context(nc.psum_tensor("ps", [128, 8, 512], fp32))
        top = [0]

        def take(n):
            top[0] += n
            return top[0] - n

        def view(at, n):
            return arena[:, at:at + n]

        at_in = take(2 * POSITIONS)
        at_map = take(2 * POSITIONS)
        at_modes = take(KX * KY * BATCH)
        at_part = take(2 * 48 * CHANNELS)
        at_w = take(2 * KX * 64)
        at_mixed = take(2 * 768)
        at_img = take(POSITIONS)
        at_half = take(2 * 2048)
        vin = [view(at_in + s * POSITIONS, POSITIONS) for s in range(2)]
        vmap = [view(at_map + s * POSITIONS, POSITIONS) for s in range(2)]
        modes = view(at_modes, KX * KY * BATCH).rearrange("p (y x b) -> p y x b", y=KY, x=KX)
        part = [view(at_part + s * 48 * CHANNELS, 48 * CHANNELS).rearrange("p (k c) -> p k c", c=CHANNELS)
                for s in range(2)]
        wring = [view(at_w + s * KX * 64, KX * 64).rearrange("p (x n) -> p x n", x=KX) for s in range(2)]
        mixed = [view(at_mixed + s * 768, 768) for s in range(2)]
        img = view(at_img, POSITIONS)
        kxin = [view(at_in + 4096 + s * 2048, 2048) for s in range(2)]
        xhalf = [view(at_half + s * 2048, 2048) for s in range(2)]
        gtile = [view(at_modes + s * 2048, 2048).rearrange("p (g n) -> p g n", g=16) for s in range(2)]
        expand = view(at_map + POSITIONS, BATCH * CHANNELS)
        expconv = view(at_part, BATCH * CHANNELS)
        spect = view(at_half, 576)
        bnst = view(at_part + BATCH * CHANNELS, QUADS * 8 * 6).rearrange("p (k s) -> p k s", s=6)
        at_small = top[0]
        fy = view(take(192), 192).rearrange("p (h n) -> p h n", h=2)
        fx = view(take(48), 48)
        ix = view(take(256), 256)
        iy = view(take(256), 256)
        masks = view(take(128 + 128 + 32 + 64 + 8), 360)
        ident, average, image_of = masks[:, 0:128], masks[:, 128:256], masks[:, 256:288]
        head_mask, falling = masks[:, 288:352], masks[:, 352:360]
        wbd = view(take(128), 128)
        lcols = view(take(3), 3)
        qcols = view(take(2), 2)
        p0 = view(take(32), 32)
        prow = view(take(32), 32)
        pcol = view(take(4), 4)
        prt = view(take(128), 128)
        p0c = view(take(32), 32)
        prc = view(take(32), 32)
        estage = [view(take(128), 128) for _ in range(2)]
        mv = view(take(2), 2)
        tiny = view(take(8), 8)
        sc, sh = view(take(1), 1), view(take(1), 1)
        proj = view(take(32), 32)
        qbias = view(take(1), 1)
        eps_col = view(take(1), 1)
        hrow = [view(at_map + s * 1024, 1024) for s in range(2)]

        tables_in = sem("tables_in")
        zeroed = sem("zeroed")
        grids_in = sem("grids_in")
        layer_in = sem("layer_in")
        t_ready = sem("t_ready")
        t_prod = sem("t_prod")
        e_copied = sems("e_copied")
        ld = [sems("ld_a"), sems("ld_b")]
        relu_done = sem("relu_done")
        transposed = sem("transposed")
        dft_full = sem("dft_full")
        part_a, part_v = sem("part_a"), sem("part_v")
        xs_full = sem("xs_full")
        modes_a, modes_v = sem("modes_a"), sem("modes_v")
        w_in = sems("w_in")
        signed = sems("signed")
        mix_full = sems("mix_full")
        mix_ev = sems("mix_ev")
        mix_st = sems("mix_st")
        kx_in = sems("kx_in")
        ix_full = sems("ix_full")
        ix_ev = sems("ix_ev")
        ix_st = sems("ix_st")
        g_in = sems("g_in")
        out_full = sems("out_full")
        out_ev = sems("out_ev")
        stat_done = sems("stat_done")
        map_st = sems("map_st")
        bn_v, bn_p, bn_s = sem("bn_v"), sem("bn_p"), sem("bn_s")
        bn_ready = sem("bn_ready")
        vchain = sem("vchain")
        proj_full, proj_ev, proj_st = sems("proj_full"), sems("proj_ev"), sems("proj_st")
        passed = sem("passed")
        from_one = [dft_full, xs_full, modes_a, modes_v, *out_ev, *stat_done, *map_st, *proj_ev, *proj_st]

        def past(n):
            return n + 1

        at_tail = at_small - 4 * SLOTS - 3 * SLOTS * HEADS

        COLS = SLOTS * DIM
        MAPS = (BATCH // 2) * DIM
        TCOLS = SLOTS * 128
        top[0] = 0
        tok = lambda n=COLS: view(take(n), n)
        as_slots = lambda t: t.rearrange("p (s d) -> p s d", d=DIM)
        as_heads = lambda t: t.rearrange("p (g d) -> p g d", d=HEAD_DIM)
        h0, n1, dev, sq, kk, vk, hsum, h1, n2 = (tok() for _ in range(9))
        n1t = view(take(TCOLS), TCOLS)
        kvm = view(take(4096), 4096)
        hid = [view(take(TCOLS), TCOLS) for _ in range(EXPERTS // 2)]
        clsrow = hid[0][:, 0:4096]
        hrows = view(take(256), 256)
        router = view(take(EXPERTS), EXPERTS)
        w1 = view(take(512), 512)
        w2 = view(take(256), 256).rearrange("p (e d) -> p e d", d=DIM)
        b1 = view(take(4), 4)
        b2 = view(take(DIM), DIM)
        clso = view(take(DIM), DIM)
        bf16 = mybir.dt.bfloat16
        combt = view(take(TCOLS // 2), TCOLS // 2).bitcast(bf16)
        picks = view(take(512), 512)
        pick = view(take(256), 256).bitcast(bf16)
        b2p = [view(take(DIM // 2), DIM // 2).bitcast(bf16) for _ in range(3)]
        assert top[0] <= at_tail
        comb3 = kk[:, 1320:2112].rearrange("p (s e) -> p s e", e=24)
        s1, s2, s3, s4 = (view(at_tail + SLOTS * i, SLOTS) for i in range(4))
        g1, g2, g3 = (view(at_tail + 4 * SLOTS + SLOTS * HEADS * i, SLOTS * HEADS) for i in range(3))

        tok_in = sem("tok_in")
        ln_sum, ln_root = sem("ln_sum"), sem("ln_root")
        n1_ready, kv_ready = sem("n1_ready"), sem("kv_ready")
        n2_ready = sem("n2_ready")
        job_full = sems("job_full")
        job_ev = sems("job_ev")
        cls_in = sem("cls_in")
        exp_out = sem("exp_out")
        split_ready = sem("split_ready")
        out_ready = sem("out_ready")
        stored = sem("stored")
        (J_N1T, J_N1T2, J_N1C, J_KV, J_KV2, J_CLS, J_CLS2, J_ATT, J_N2T, J_N2T2, J_N2C, J_LOG) = range(12)
        J_UP = 12
        J_CT = J_UP + 12
        J_BC = J_CT + 3
        J_OUT = J_BC + 12
        PARTS = ((0, 2048), (2048, 2048), (4096, 128))

        def bank(k):
            return 4 * (k % 2)

        def wait_full(eng, k):
            eng.wait_ge(job_full[k % 2], k // 2 + 1)

        def wait_evacuated(eng, k):
            eng.wait_ge(job_ev[k % 2], k // 2 + 1)

        def sync_tokens(sp):
            for s in range(2):
                sp.wait_ge(proj_st[s], past(64 * PAIRS))
            sp.dma_start(as_slots(h0)[:, 0:BATCH // 2, :],
                         tok_d.rearrange("(s e) r (u y) -> (e r u) s y", e=2, y=DIM)).then_inc(tok_in, 16)
            sp.dma_start(as_slots(h0)[:, BATCH // 2, :], cls_tok.broadcast_to([128, DIM])).then_inc(tok_in, 16)
            sp.dma_start(hrows.rearrange("p (a d) -> p a d", a=4),
                         head_rows.unsqueeze(0).broadcast_to([128, 4, DIM])).then_inc(tok_in, 16)
            sp.dma_start(router[0:64], router_t).then_inc(tok_in, 16)
            sp.dma_start(w1[0:64].rearrange("p (e f) -> p e f", e=EXPERTS), w1_t).then_inc(tok_in, 16)
            sp.dma_start(w2, w2_rows).then_inc(tok_in, 16)
            sp.dma_start(b1, b1_cols).then_inc(tok_in, 16)
            sp.dma_start(picks[0:24], picks_d).then_inc(tok_in, 16)
            for i in range(3):
                sp.dma_start(b2[8 * i:8 * i + 8], b2_rows).then_inc(tok_in, 16)
            wait_evacuated(sp, J_CLS)
            wait_evacuated(sp, J_CLS2)
            for e in range(2):
                sp.dma_start(clso[e:BATCH:2], clsrow[0:1, 2048 * e:2048 * e + 2048]
                             .rearrange("a (b d) -> a b d", d=DIM)).then_inc(cls_in, 16)
            sp.wait_ge(out_ready, 2)
            o = as_slots(dev)
            for e in range(2):
                sp.dma_start(out[e:BATCH:2, 1:TOKENS, :].rearrange("s t d -> t s d"),
                             o[64 * e:64 * e + 64, 0:BATCH // 2, :]).then_inc(stored, 16)
            sp.dma_start(out[:, 0, :], o[0:BATCH, BATCH // 2, :]).then_inc(stored, 16)
            sp.wait_ge(stored, 48)

        def scalar_tokens(act):
            def root(k, dst, src, scale, bias):
                act.wait_ge(ln_sum, k)
                nc.scalar.activation(dst, src, ACT.Sqrt, bias=bias, scale=scale).then_inc(ln_root, 1)

            def evac(k, dst, rows, width):
                wait_full(act, k)
                src = ps[0:rows, bank(k):bank(k) + 4, :].rearrange("p b n -> p (b n)")[:, 0:width]
                nc.scalar.copy(dst, src).then_inc(job_ev[k % 2], 1)

            root(1, s3, s2, 1.0 / DIM, eps_col)
            for k, (at, n) in zip((J_N1T, J_N1T2, J_N1C), PARTS):
                evac(k, n1t[0:64, at:at + n], 64, n)
            root(2, g3, g2, 1.0 / (HEAD_DIM - 1), 0.0)
            for k, at in ((J_CLS, 0), (J_CLS2, 2048)):
                evac(k, clsrow[0:1, at:at + 2048], 1, 2048)
            root(3, s3, s2, 1.0 / DIM, eps_col)
            for k, (at, n) in zip((J_N2T, J_N2T2, J_N2C), PARTS):
                evac(k, n1t[0:64, at:at + n], 64, n)
            wait_evacuated(act, J_LOG)
            nc.scalar.activation(g2, g1, ACT.Exp).then_inc(exp_out, 1)
            for p in range(EXPERTS // 2):
                for i, (at, n) in enumerate(PARTS):
                    k = J_UP + 3 * p + i
                    wait_full(act, k)
                    src = ps[:, bank(k):bank(k) + 4, :].rearrange("p b n -> p (b n)")[:, 0:n]
                    nc.scalar.activation(hid[p][:, at:at + n], src, ACT.Gelu, bias=b1[:, p:p + 1])\
                        .then_inc(job_ev[k % 2], 1)
            for i, (at, n) in enumerate(PARTS):
                evac(J_CT + i, combt[0:24, at:at + n], 24, n)

        def tensor_tokens(pe):
            def begin(k):
                pe.wait_ge(job_ev[k % 2], k // 2)

            def cols(k, rows, width):
                return ps[rows, bank(k):bank(k) + 4, :].rearrange("p b n -> p (b n)")[:, 0:width]

            def turn(k, tiles, source, rows=slice(0, 64)):
                begin(k)
                for i, t in enumerate(tiles):
                    last = nc.tensor.transpose(cols(k, rows, 2048)[:, 128 * i:128 * i + 128], source[:, t, :],
                                               ident)
                last.then_inc(job_full[k % 2], 1)

            groups = (range(0, 16), range(16, 32), range(32, 33))
            for s in range(2):
                pe.wait_ge(proj_ev[s], past(PAIRS))
            pe.wait_ge(tok_in, 16 * 11)
            pe.wait_ge(n1_ready, 1)
            for k, tiles in zip((J_N1T, J_N1T2, J_N1C), groups):
                turn(k, tiles, as_slots(n1))
            pe.wait_ge(kv_ready, 1)
            k3, v3 = as_slots(kk), as_slots(vk)
            for e, k in ((0, J_KV), (1, J_KV2)):
                begin(k)
                rows = slice(64 * e, 64 * e + 64)
                for t in range(BATCH // 2):
                    dst = cols(k, slice(0, 64), 2048)[:, 64 * t:64 * t + 64]
                    nc.tensor.matmul(dst, k3[rows, t, :], v3[rows, t, :], start=True, stop=False)
                    last = nc.tensor.matmul(dst, k3[rows, BATCH // 2, :], v3[rows, BATCH // 2, :],
                                            start=False, stop=True)
                last.then_inc(job_full[k % 2], 1)
            wait_evacuated(pe, J_KV2)
            for k, at in ((J_CLS, 0), (J_CLS2, 2048)):
                begin(k)
                for c in range(4):
                    last = nc.tensor.matmul(ps[0:1, bank(k) + c, :], n1t[0:64, 4096:4097],
                                            kvm[0:64, at + 512 * c:at + 512 * c + 512], start=True, stop=True)
                last.then_inc(job_full[k % 2], 1)
            begin(J_ATT)
            for b in range(BATCH):
                t, e = b // 2, b % 2
                last = nc.tensor.matmul(cols(J_ATT, slice(64 * e, 64 * e + 64), 2048)[:, 64 * t:64 * t + 64],
                                        n1t[0:64, 128 * t + 64 * e:128 * t + 64 * e + 64],
                                        kvm[0:64, 2048 * e + 64 * t:2048 * e + 64 * t + 64], start=True, stop=True)
            last.then_inc(job_full[J_ATT % 2], 1)
            pe.wait_ge(n2_ready, 1)
            for k, tiles in zip((J_N2T, J_N2T2, J_N2C), groups):
                turn(k, tiles, as_slots(n2))
            wait_evacuated(pe, J_N2C)
            wait_evacuated(pe, J_N2T2)
            begin(J_LOG)
            for t in range(SLOTS):
                last = nc.tensor.matmul(cols(J_LOG, slice(0, 128), 264)[:, 8 * t:8 * t + 8],
                                        n1t[0:64, 128 * t:128 * t + 128], router[0:64, :], start=True, stop=True)
            last.then_inc(job_full[J_LOG % 2], 1)
            for p in range(EXPERTS // 2):
                for i, (at, n) in enumerate(PARTS):
                    k = J_UP + 3 * p + i
                    begin(k)
                    for c in range(0, n, 512):
                        w = min(512, n - c)
                        last = nc.tensor.matmul(ps[:, bank(k) + c // 512, 0:w], w1[0:64, 128 * p:128 * p + 128],
                                                n1t[0:64, at + c:at + c + w], start=True, stop=True)
                    last.then_inc(job_full[k % 2], 1)
            pe.wait_ge(split_ready, 1)
            for i, tiles in enumerate(groups):
                turn(J_CT + i, tiles, comb3, rows=slice(0, 24))
            wait_evacuated(pe, J_CT + 1)
            wait_evacuated(pe, J_CT + 2)
            for p in range(EXPERTS // 2):
                for i, (at, n) in enumerate(PARTS):
                    k = J_BC + 3 * p + i
                    begin(k)
                    for c in range(0, n, 512):
                        w = min(512, n - c)
                        last = nc.tensor.matmul(ps[:, bank(k) + c // 512, 0:w], pick[0:24, 128 * p:128 * p + 128],
                                                combt[0:24, at + c:at + c + w], start=True, stop=True)
                    last.then_inc(job_full[k % 2], 1)
            wait_evacuated(pe, J_BC + 11)
            wait_evacuated(pe, J_BC + 10)
            for k, tiles in ((J_OUT, range(32)), (J_OUT + 1, range(32, 33))):
                begin(k)
                for i, t in enumerate(tiles):
                    dst = cols(k, slice(0, 128), 2048)[:, 64 * i:64 * i + 64]
                    for p in range(EXPERTS // 2):
                        nc.tensor.matmul(dst, hid[p][:, 128 * t:128 * t + 128], w2[:, p, :], start=(p == 0),
                                         stop=False)
                    for i3 in range(3):
                        last = nc.tensor.matmul(dst, combt[0:24, 128 * t:128 * t + 128], b2p[i3][0:24, :],
                                                start=False, stop=(i3 == 2))
                last.then_inc(job_full[k % 2], 1)

        def vector_chain(dve, links):
            def link(ins):
                links[0] += 1
                ins.then_inc(vchain, 1)
                dve.wait_ge(vchain, links[0])

            def layer_norm(src, dst, k):
                x3, d3 = as_slots(src), as_slots(dev)
                wide = lambda t: t.unsqueeze(2).broadcast_to([128, SLOTS, DIM])
                link(nc.vector.reduce_sum(s1, x3, AX.X))
                link(nc.vector.tensor_scalar(s4, s1, 1.0 / DIM, None, ALU.mult))
                link(nc.vector.tensor_tensor(d3, x3, wide(s4), ALU.subtract))
                link(nc.vector.tensor_tensor(sq, dev, dev, ALU.mult))
                nc.vector.reduce_sum(s2, as_slots(sq), AX.X).then_inc(ln_sum, 1)
                dve.wait_ge(ln_root, k)
                link(nc.vector.reciprocal(s4, s3))
                link(nc.vector.tensor_tensor(as_slots(dst), d3, wide(s4), ALU.mult))

            dve.wait_ge(tok_in, 16 * 11)
            layer_norm(h0, n1, 1)
            nc.vector.tensor_tensor(hsum, h0, n1, ALU.add).then_inc(n1_ready, 1)
            n3, d3 = as_heads(n1), as_heads(dev)
            wide = lambda t: t.unsqueeze(2).broadcast_to([128, SLOTS * HEADS, HEAD_DIM])
            link(nc.vector.reduce_sum(g1, n3, AX.X))
            link(nc.vector.tensor_scalar(g2, g1, 1.0 / HEAD_DIM, None, ALU.mult))
            link(nc.vector.tensor_tensor(d3, n3, wide(g2), ALU.subtract))
            link(nc.vector.tensor_tensor(sq, dev, dev, ALU.mult))
            nc.vector.reduce_sum(g2, as_heads(sq), AX.X).then_inc(ln_sum, 1)
            dve.wait_ge(ln_root, 2)
            link(nc.vector.tensor_scalar(g1, g3, LN_EPS, None, ALU.add))
            link(nc.vector.reciprocal(g2, g1))
            link(nc.vector.tensor_tensor(as_heads(sq), d3, wide(g2), ALU.mult))
            row = lambda i: hrows[:, 64 * i:64 * i + 64].unsqueeze(1).broadcast_to([128, SLOTS, DIM])
            link(nc.vector.tensor_tensor(as_slots(kk), as_slots(sq), row(0), ALU.mult))
            link(nc.vector.tensor_tensor(as_slots(kk), as_slots(kk), row(1), ALU.add))
            link(nc.vector.tensor_tensor(as_slots(vk), as_slots(sq), row(2), ALU.mult))
            link(nc.vector.tensor_tensor(as_slots(vk), as_slots(vk), row(3), ALU.add))
            nc.vector.tensor_scalar(vk[:, MAPS:COLS], vk[:, MAPS:COLS], 1.0 / 64, None, ALU.mult)\
                .then_inc(kv_ready, 1)
            for k, at in ((J_KV, 0), (J_KV2, 2048)):
                wait_full(dve, k)
                src = ps[0:64, bank(k):bank(k) + 4, :].rearrange("p b (i d) -> p (b i) d", d=DIM)
                nc.vector.tensor_tensor(kvm[0:64, at:at + 2048].rearrange("p (i d) -> p i d", d=DIM), src,
                                        head_mask[0:64].unsqueeze(1).broadcast_to([64, 32, DIM]), ALU.mult)\
                    .then_inc(job_ev[k % 2], 1)
            wait_full(dve, J_ATT)
            link(nc.vector.tensor_copy(h1[:, MAPS:COLS], hsum[:, MAPS:COLS]))
            nc.vector.tensor_tensor(h1[:, 0:MAPS], ps[:, bank(J_ATT):bank(J_ATT) + 4, :]
                                    .rearrange("p b n -> p (b n)"), hsum[:, 0:MAPS], ALU.add)\
                .then_inc(job_ev[J_ATT % 2], 1)
            wait_evacuated(dve, J_ATT)
            dve.wait_ge(cls_in, 32)
            link(nc.vector.tensor_tensor(h1[0:BATCH, MAPS:COLS], hsum[0:BATCH, MAPS:COLS], clso[0:BATCH], ALU.add))
            layer_norm(h1, n2, 3)
            nc.vector.tensor_tensor(hsum, h1, n2, ALU.add).then_inc(n2_ready, 1)
            wait_full(dve, J_LOG)
            e3 = lambda t: t.rearrange("p (s e) -> p s e", e=EXPERTS)
            wide = lambda t: t.unsqueeze(2).broadcast_to([128, SLOTS, EXPERTS])
            fall = falling.unsqueeze(1).broadcast_to([128, SLOTS, EXPERTS])
            logits = ps[:, bank(J_LOG), 0:SLOTS * EXPERTS]
            link(nc.vector.reduce_max(s1, e3(logits), AX.X))
            nc.vector.tensor_tensor(e3(g1), e3(logits), wide(s1), ALU.subtract).then_inc(job_ev[J_LOG % 2], 1)
            wait_evacuated(dve, J_LOG)
            dve.wait_ge(exp_out, 1)
            link(nc.vector.reduce_sum(s1, e3(g2), AX.X))
            link(nc.vector.reciprocal(s2, s1))
            link(nc.vector.tensor_tensor(e3(g1), e3(g2), wide(s2), ALU.mult))
            link(nc.vector.reduce_max(s1, e3(g1), AX.X))
            first, other, key = e3(kk[:, 0:264]), e3(kk[:, 264:528]), e3(kk[:, 528:792])
            second, flag = e3(kk[:, 792:1056]), e3(kk[:, 1056:1320])
            link(nc.vector.tensor_tensor(flag, e3(g1), wide(s1), ALU.is_equal))
            link(nc.vector.tensor_tensor(key, flag, fall, ALU.mult))
            link(nc.vector.reduce_max(s2, key, AX.X))
            link(nc.vector.tensor_tensor(first, key, wide(s2), ALU.is_equal))
            link(nc.vector.scalar_tensor_tensor(out=other, in0=first, scalar=-2.0, in1=e3(g1), op0=ALU.mult,
                                                op1=ALU.add))
            link(nc.vector.reduce_max(s3, other, AX.X))
            link(nc.vector.tensor_tensor(flag, other, wide(s3), ALU.is_equal))
            link(nc.vector.tensor_tensor(key, flag, fall, ALU.mult))
            link(nc.vector.reduce_max(s2, key, AX.X))
            link(nc.vector.tensor_tensor(second, key, wide(s2), ALU.is_equal))
            link(nc.vector.tensor_tensor(flag, first, second, ALU.add))
            link(nc.vector.tensor_tensor(key, flag, e3(g1), ALU.mult))
            link(nc.vector.tensor_tensor(s4, s1, s3, ALU.add))
            link(nc.vector.tensor_scalar(s4, s4, 1e-12, None, ALU.max))
            link(nc.vector.reciprocal(s2, s4))
            link(nc.vector.tensor_tensor(flag, key, wide(s2), ALU.mult))
            def three(value, rest, half, outs):
                link(nc.vector.tensor_copy(half, value))
                link(nc.vector.tensor_copy(outs[0], half))
                link(nc.vector.tensor_tensor(rest, value, half, ALU.subtract))
                link(nc.vector.tensor_copy(half, rest))
                link(nc.vector.tensor_copy(outs[1], half))
                link(nc.vector.tensor_tensor(rest, rest, half, ALU.subtract))
                link(nc.vector.tensor_copy(outs[2], rest))

            three(flag, key, e3(vk[:, 0:132].bitcast(bf16)), [comb3[:, :, 8 * i:8 * i + 8] for i in range(3)])
            three(b2[0:24], vk[0:24, 132:196], vk[0:24, 196:228].bitcast(bf16), [t[0:24] for t in b2p])
            nc.vector.tensor_copy(pick[0:24], picks[0:24]).then_inc(split_ready, 1)
            for p in range(EXPERTS // 2):
                for i, (at, n) in enumerate(PARTS):
                    k = J_BC + 3 * p + i
                    wait_full(dve, k)
                    src = ps[:, bank(k):bank(k) + 4, :].rearrange("p b n -> p (b n)")[:, 0:n]
                    nc.vector.tensor_tensor(hid[p][:, at:at + n], hid[p][:, at:at + n], src, ALU.mult)\
                        .then_inc(job_ev[k % 2], 1)
            for k, (at, n) in ((J_OUT, (0, MAPS)), (J_OUT + 1, (MAPS, DIM))):
                wait_full(dve, k)
                src = ps[:, bank(k):bank(k) + 4, :].rearrange("p b n -> p (b n)")[:, 0:n]
                nc.vector.tensor_tensor(dev[:, at:at + n], src, hsum[:, at:at + n], ALU.add).then_inc(out_ready, 1)

        block = ctx.enter_context(nc.Block())

        def apart(eng):
            eng.sem_inc(passed, 1)

        def raw_half(l, q, h):
            if isinstance(l, int) and isinstance(q, int):
                return raw_d[l, q, :, 2048 * h:2048 * h + 2048]
            return raw_d[bass.ds(l, 1), bass.ds(q, 1), :, 2048 * h:2048 * h + 2048].rearrange("a b p n -> (a b p) n")

        def half(tile, h):
            return tile[:, 2048 * h:2048 * h + 2048]

        def y_step(l, q):
            return 1 + QUADS * (l - 1) + q

        def x_step(l, q):
            return 1 + QUADS * l + q

        def input_use(p, it):
            return PAIRS * p + it

        MIX_ORDER = [("mix", 0), ("mix", 1)]
        for p in range(1, KY // 2):
            MIX_ORDER += [("mix", 2 * p), ("mix", 2 * p + 1), ("inverse", p - 1)]
        MIX_ORDER += [("inverse", KY // 2 - 1)]
        RING = KY // 2

        @block.sync
        def _(sp):
            for s in from_one:
                sp.sem_inc(s, 1)
            for dst, src in ((img[0:BATCH, :], images), (fy.rearrange("p h n -> p (h n)"), fy_d), (fx, fx_d),
                             (ix[0:96, :], ix_d), (iy[0:96, :], iy_d), (masks, masks_d), (qcols, q_cols),
                             (pcol[0:32, :], p_cols), (p0, p_rows[0:1, :].broadcast_to([128, 32]))):
                sp.dma_start(dst, src).then_inc(tables_in, 16)
            sp.wait_ge(zeroed, 4)
            sp.dma_start(img[BATCH:BATCH + FEATURE_ROWS, :], grids_d).then_inc(grids_in, 16)
            sp.dma_start(prow[BATCH:BATCH + FEATURE_ROWS, :], p_rows[1:4, :]).then_inc(grids_in, 16)

            def layer_tables(l):
                for j in range(QUAD):
                    src = conv_w[l] if isinstance(l, int) else \
                        conv_w[bass.ds(l, 1), :, :].rearrange("a c o -> (a c) o")
                    sp.dma_start(wbd[32 * j:32 * j + 32, 32 * j:32 * j + 32], src).then_inc(layer_in, 16)
                src = layer_cols[l] if isinstance(l, int) else \
                    layer_cols[bass.ds(l, 1), :, :].rearrange("a p n -> (a p) n")
                sp.dma_start(lcols, src).then_inc(layer_in, 16)

            def weights(l, ky):
                src = mode_w[l, ky] if isinstance(l, int) else \
                    mode_w[bass.ds(l, 1), ky, :, :].rearrange("a p n -> (a p) n")
                sp.dma_start(wring[ky % 2][0:64].rearrange("p x n -> p (x n)"), src).then_inc(w_in[ky % 2], 16)

            def mix(l):
                def bring_back(p):
                    for s in range(2):
                        sp.wait_ge(mix_st[s], 64 * (RING * l + p + 1))
                    if p >= 2:
                        sp.wait_ge(ix_full[1], KY * l + 2 * p - 2)
                    for e in range(2):
                        sp.dma_start(kxin[p % 2][48 * e:48 * e + 48],
                                     mixed_d[:, 2 * p + e, :, :].rearrange("k o b -> k (o b)"))\
                          .then_inc(kx_in[p % 2], 16)

                def store_inverse(p):
                    for ky in (2 * p, 2 * p + 1):
                        for h in range(2):
                            sp.wait_ge(ix_ev[h], KY * l + ky + 1)
                        sp.dma_start(half_d[2 * ky:2 * ky + 2].rearrange("r x g n -> (r x g) n"), xhalf[ky % 2])\
                          .then_inc(ix_st[ky % 2], 16)

                for ky in range(KY):
                    s = ky % 2
                    sp.wait_ge(mix_ev[s], RING * l + ky // 2 + 1)
                    for m in range(2):
                        for ri in range(2):
                            k = ri * KX + m * KX_HALF
                            sp.dma_start(mixed_d[k:k + KX_HALF, ky, :, :].rearrange("k o b -> o k b"),
                                         mixed[s][64 * m + 32 * ri:64 * m + 32 * ri + 32]
                                         .rearrange("o (k b) -> o k b", b=BATCH)).then_inc(mix_st[s], 16)
                    if ky + 2 < KY:
                        weights(l, ky + 2)
                    if ky >= 2 and s == 0:
                        bring_back(ky // 2 - 1)
                    if ky >= 5 and s == 1:
                        store_inverse((ky - 5) // 2)
                bring_back(KY // 2 - 1)
                store_inverse(KY // 2 - 2)
                store_inverse(KY // 2 - 1)

            def g_load(q, s):
                for x in range(4):
                    src = half_d[:, x, :, bass.ds(q * 128, 128)]
                    sp.dma_start(gtile[s][24 * x:24 * x + 24], src).then_inc(g_in[s], 16)

            def input_load(l, q, s, h):
                sp.dma_start(half(vin[s], h), raw_half(l - 1, q, h)).then_inc(ld[s][h], 16)

            def output_pass(l, first):
                for s in range(2):
                    sp.wait_ge(ix_st[s], 16 * RING * (l + 1))
                for s in range(2):
                    g_load(s, s)
                    if s and not first:
                        for h in range(2):
                            input_load(l, 1, 1, h)

                def steps(it, more):
                    for s in range(2):
                        q = 2 * it + s
                        for h in range(2):
                            if more:
                                sp.wait_ge(out_full[h], QUADS * l + q + 1)
                                if not first:
                                    input_load(l, q + 2, s, h)
                                if h:
                                    g_load(q + 2, s)
                                elif first:
                                    apart(sp)
                            sp.wait_ge(out_ev[h], past(QUADS * l + q + 1))
                            sp.dma_start(raw_half(l, q, h), half(vmap[s], h)).then_inc(map_st[s], 16)

                with sp.Fori(0, PAIRS - 1) as it:
                    steps(it, True)
                steps(PAIRS - 1, False)

            def spectrum_pass(l):
                for s in range(2):
                    sp.wait_ge(map_st[s], past(32 * PAIRS * l))
                for s in range(2):
                    for h in range(2):
                        input_load(l, s, s, h)
                for ky in range(2):
                    weights(l, ky)
                with sp.Fori(0, PAIRS - 1) as it:
                    for s in range(2):
                        sp.wait_ge(transposed, y_step(l, 2 * it + s) + 1)
                        for h in range(2):
                            input_load(l, 2 * it + s + 2, s, h)
                sp.wait_ge(transposed, y_step(l, QUADS - 2) + 1)
                apart(sp)
                for h in range(2):
                    input_load(l, 0, 0, h)
                sp.wait_ge(transposed, y_step(l, QUADS - 1) + 1)
                apart(sp)

            layer_tables(0)
            for ky in range(2):
                weights(0, ky)
            mix(0)
            output_pass(0, True)
            with sp.Fori(1, LAYERS) as l:
                spectrum_pass(l)
                layer_tables(l)
                mix(l)
                output_pass(l, False)

            for s in range(2):
                sp.wait_ge(map_st[s], past(32 * PAIRS * LAYERS))
            for s in range(2):
                for h in range(2):
                    input_load(LAYERS, s, s, h)

            def project(it, more):
                for s in range(2):
                    if more:
                        sp.wait_ge(proj_full[s], it + 1)
                        for h in range(2):
                            input_load(LAYERS, 2 * it + s + 2, s, h)
                    sp.wait_ge(proj_ev[s], past(it + 1))
                    for c in range(4):
                        dst = tok_d[bass.ds((2 * it + s) * QUAD, QUAD), c:c + 5:4, :]
                        sp.dma_start(dst, hrow[s][32 * c:32 * c + QUAD].rearrange("j (r n) -> j r n", r=2))\
                          .then_inc(proj_st[s], 16)

            with sp.Fori(0, PAIRS - 1) as it:
                project(it, True)
            project(PAIRS - 1, False)
            sync_tokens(sp)

        @block.scalar
        def _(act):
            def part_evac(l, q, s, c):
                for h in range(2):
                    act.wait_ge(dft_full, past(2 * c + h + 1))
                    if h == 0 and not isinstance(c, int):
                        act.wait_ge(xs_full, past(x_step(l, q) - 1))
                    for ri in range(2):
                        src = ps[0:64, 2 * h:2 * h + 2, 0:384].rearrange("p b (c n) -> p n b c", c=4)
                        last = nc.scalar.copy(
                            part[s][64 * ri:64 * ri + 64, :, 16 * h:16 * h + 16:2]
                            .rearrange("p k (b c) -> p k b c", c=4), src[:, 48 * ri:48 * ri + 48])
                    last.then_inc(part_a, 1)

            def modes_evac(q, s, c):
                act.wait_ge(xs_full, past(c + 1))
                for j in range(2):
                    for ri in range(2):
                        src = ps[32 * j:32 * j + 32, 4 + 2 * s:6 + 2 * s, 0:288]\
                            .rearrange("p h (y r x) -> p h y r x", y=6, r=2)[:, :, :, ri, :]
                        dst = modes[32 * ri:32 * ri + 32, :, :, bass.ds(QUAD * q + j, 1)]\
                            .rearrange("p (h y) x b -> p h y (x b)", h=2)
                        last = nc.scalar.copy(dst, src)
                last.then_inc(modes_a, 1)

            def relu(p, it, s, h):
                act.wait_ge(ld[s][h], 16 * (input_use(p, it) + 1))
                nc.scalar.activation(half(vin[s], h), half(vin[s], h), ACT.Relu, bias=sh, scale=sc)\
                    .then_inc(relu_done, 1)

            def mix(l):
                for what, n in MIX_ORDER:
                    if what == "mix":
                        s, i = n % 2, RING * l + n // 2
                        act.wait_ge(mix_full[s], i + 1)
                        act.wait_ge(mix_st[s], 64 * i)
                        nc.scalar.copy(mixed[s].rearrange("p (h n) -> p h n", h=2), ps[:, 2 * s:2 * s + 2, 0:384])\
                            .then_inc(mix_ev[s], 1)
                    else:
                        for ky in (2 * n, 2 * n + 1):
                            act.wait_ge(ix_full[0], KY * l + ky + 1)
                            act.wait_ge(ix_st[ky % 2], 16 * (RING * l + n))
                            nc.scalar.copy(xhalf[ky % 2][:, 0:1024].rearrange("p (h n) -> p h n", h=2),
                                           ps[:, 4:6, :]).then_inc(ix_ev[0], 1)

            def map_evac(l, it, s, h):
                act.wait_ge(out_full[h], QUADS * l + 2 * it + s + 1)
                if h == 0:
                    act.wait_ge(map_st[s], past(32 * (PAIRS * l + it)))
                    act.wait_ge(stat_done[s], past(PAIRS * l + it))
                nc.scalar.copy(half(vmap[s], h).rearrange("p (b n) -> p b n", b=4), ps[:, 4 * h:4 * h + 4, :])\
                    .then_inc(out_ev[h], 1)

            def norm_root(l):
                act.wait_ge(bn_p, 2 * l + 2)
                nc.scalar.activation(tiny[:, 3:4], ps[:, 1, 0:1], ACT.Sqrt, bias=eps_col).then_inc(bn_s, 1)

            act.wait_ge(zeroed, 5)
            part_evac(0, 0, 0, 0)
            act.wait_ge(xs_full, past(1))
            nc.scalar.copy(spect[:, 0:288], ps[:, 4, 0:288]).then_inc(modes_a, 1)
            with act.Fori(0, PAIRS) as it:
                for s in range(2):
                    modes_evac(2 * it + s, s, x_step(0, 2 * it + s))
            mix(0)
            with act.Fori(0, PAIRS) as it:
                for s in range(2):
                    for h in range(2):
                        map_evac(0, it, s, h)
            norm_root(0)

            with act.Fori(1, LAYERS) as l:
                act.wait_ge(bn_ready, l)
                for s in range(2):
                    for h in range(2):
                        relu(2 * l - 2, 0, s, h)
                part_evac(l, 0, 0, y_step(l, 0))
                for h in range(2):
                    relu(2 * l - 2, 1, 0, h)

                def spectrum(l, it, s, more):
                    q = 2 * it + s
                    if not isinstance(q, int) or q + 1 < QUADS:
                        part_evac(l, q + 1, 1 - s, y_step(l, q + 1))
                    modes_evac(q, s, x_step(l, q))
                    if more:
                        for h in range(2):
                            relu(2 * l - 2, it + 1 + s, 1 - s, h)

                with act.Fori(0, PAIRS - 2) as it:
                    for s in range(2):
                        spectrum(l, it, s, True)
                for q in range(QUADS - 4, QUADS):
                    spectrum(l, q // 2, q % 2, q + 3 < QUADS)
                for h in range(2):
                    relu(2 * l - 1, 0, 0, h)
                mix(l)
                relu(2 * l - 1, 0, 1, 0)

                def output(l, it, last):
                    for i in range(4):
                        map_evac(l, it, i // 2, i % 2)
                        n = i + 3
                        if not last or n < 4:
                            relu(2 * l - 1, it + n // 4, n % 4 // 2, n % 2)

                with act.Fori(0, PAIRS - 1) as it:
                    output(l, it, False)
                output(l, PAIRS - 1, True)
                norm_root(l)

            act.wait_ge(bn_v, 3 * LAYERS + 2)
            for s in range(2):
                act.wait_ge(map_st[s], past(32 * PAIRS * LAYERS))
            with act.Fori(0, PAIRS) as it:
                for s in range(2):
                    act.wait_ge(proj_full[s], it + 1)
                    act.wait_ge(proj_st[s], past(64 * it))
                    nc.scalar.activation(hrow[s].rearrange("p (r n) -> p r n", r=2), ps[:, 2 * s:2 * s + 2, :],
                                         ACT.Identity, bias=qbias).then_inc(proj_ev[s], 1)
            scalar_tokens(act)

        @block.tensor
        def _(pe):
            def y_transform(l, q, s, c):
                pe.wait_ge(transposed, c + 1)
                blocks = vmap[s].rearrange("p (h d m) -> p h d m", h=2, d=16)
                for h in range(2):
                    if not isinstance(c, int):
                        pe.wait_ge(part_a, 2 * c + h - 1)
                        pe.wait_ge(part_v, 2 * c + h - 1)
                    for d in range(8 * h, 8 * h + 8):
                        for yh in range(2):
                            last = nc.tensor.matmul(ps[:, d // 4, 96 * (d % 4):96 * (d % 4) + 96],
                                                    blocks[:, yh, d], fy[:, yh, :], start=(yh == 0), stop=(yh == 1))
                    last.then_inc(dft_full, 1)

            def x_transform(l, q, s, c, x):
                pe.wait_ge(part_a, 2 * c + 2)
                pe.wait_ge(part_v, 2 * c + 2)
                if not isinstance(x, int):
                    pe.wait_ge(modes_a, past(x - 1))
                    pe.wait_ge(modes_v, past(x - 1))
                for ky in range(KY):
                    last = nc.tensor.matmul(ps[:, 4 + 2 * s + ky // 6, 48 * (ky % 6):48 * (ky % 6) + 48],
                                            part[s][:, 4 * ky:4 * ky + 4, :].rearrange("p j c -> p (j c)"), fx,
                                            start=True, stop=True)
                last.then_inc(xs_full, 1)

            def mix(l):
                pe.wait_ge(modes_a, past(x_step(l, QUADS)))
                pe.wait_ge(modes_v, past(x_step(l, QUADS)))
                for what, n in MIX_ORDER:
                    if what == "mix":
                        s, i = n % 2, RING * l + n // 2
                        pe.wait_ge(signed[s], i + 1)
                        pe.wait_ge(mix_ev[s], i)
                        apart(pe)
                        for k in range(KX_HALF):
                            for m in range(2):
                                last = nc.tensor.matmul(
                                    ps[64 * m:64 * m + 64, 2 * s + k // 6, 64 * (k % 6):64 * (k % 6) + 64],
                                    wring[s][0:64, KX_HALF * m + k, :], modes[0:64, n, KX_HALF * m + k, :],
                                    start=True, stop=True)
                        last.then_inc(mix_full[s], 1)
                    else:
                        pe.wait_ge(kx_in[n % 2], 32 * (RING // 2 * l + n // 2 + 1))
                        for e in range(2):
                            for h in range(2):
                                pe.wait_ge(ix_ev[h], KY * l + 2 * n + e)
                                for g in (2 * h, 2 * h + 1):
                                    rows = kxin[n % 2][0:96].rearrange("k (o b) -> k b o", b=BATCH)
                                    last = nc.tensor.matmul(ps[:, 4 + g, :], ix[0:96, 128 * e:128 * e + 128],
                                                            rows[:, 16 * g:16 * g + 16, :], start=True, stop=True)
                                last.then_inc(ix_full[h], 1)
                for s in range(2):
                    pe.wait_ge(mix_ev[s], RING * (l + 1))
                    pe.wait_ge(ix_ev[s], KY * (l + 1))
                apart(pe)

            def map_out(l, it, s, stationary, source, ready):
                pe.wait_ge(g_in[s], 64 * (PAIRS * l + it + 1))
                for h in range(2):
                    ready(h)
                    pe.wait_ge(out_ev[h], past(QUADS * l + 2 * it + s))
                    for k in range(4):
                        n = 4 * h + k
                        nc.tensor.matmul(ps[:, n, :], stationary, source[:, 512 * n:512 * n + 512],
                                         start=True, stop=False)
                        for g in range(2):
                            last = nc.tensor.matmul(ps[:, n, 256 * g:256 * g + 256], gtile[s][0:96, 2 * n + g, :],
                                                    iy[0:96, :], start=False, stop=(g == 1))
                    last.then_inc(out_full[h], 1)

            def norm_sums(l):
                for h in range(2):
                    pe.wait_ge(out_ev[h], past(QUADS * (l + 1)))
                for k in range(2):
                    pe.wait_ge(bn_v, 3 * l + 1 + k)
                    nc.tensor.matmul(ps[:, k, 0:1], average, (mv if k == 0 else tiny)[:, 0:1], start=True, stop=True)\
                        .then_inc(bn_p, 1)

            pe.wait_ge(tables_in, 16 * 9)
            y_transform(0, 0, 0, 0)
            x_transform(0, 0, 0, 0, 0)
            pe.wait_ge(layer_in, 80)
            pe.wait_ge(t_ready, 2)
            nc.tensor.matmul(ps[:, 0, 0:32], pcol[0:32, 0:1].broadcast_to([32, 128]), wbd[0:32, 0:32],
                             start=True, stop=True)
            nc.tensor.matmul(ps[:, 1, 0:32], prt[0:32, :], wbd[0:32, 0:32], start=True, stop=True)\
                .then_inc(t_prod, 1)
            pe.wait_ge(modes_a, past(1))
            pe.wait_ge(modes_v, past(1))
            with pe.Fori(0, PAIRS) as it:
                for s in range(2):
                    pe.wait_ge(e_copied[s], it + 1)
                    pe.wait_ge(modes_a, past(2 * it + s))
                    pe.wait_ge(modes_v, past(2 * it + s))
                    for h in range(2):
                        last = nc.tensor.matmul(ps[:, 4 + 2 * s + h, 0:288], estage[s], spect[:, 288 * h:288 * h + 288],
                                                start=True, stop=True)
                    last.then_inc(xs_full, 1)
            mix(0)
            with pe.Fori(0, PAIRS) as it:
                for s in range(2):
                    pe.wait_ge(e_copied[s], PAIRS + it + 1)
                    map_out(0, it, s, estage[s], img, lambda h: None)
            norm_sums(0)

            with pe.Fori(1, LAYERS) as l:
                pe.wait_ge(bn_ready, l)
                y_transform(l, 0, 0, y_step(l, 0))
                with pe.Fori(0, PAIRS - 1) as it:
                    for s in range(2):
                        q = 2 * it + s
                        y_transform(l, q + 1, 1 - s, y_step(l, q + 1))
                        x_transform(l, q, s, y_step(l, q), x_step(l, q))
                y_transform(l, QUADS - 1, 1, y_step(l, QUADS - 1))
                for s in range(2):
                    x_transform(l, QUADS - 2 + s, s, y_step(l, QUADS - 2 + s), x_step(l, QUADS - 2 + s))
                pe.wait_ge(layer_in, 80 * (l + 1))
                mix(l)
                with pe.Fori(0, PAIRS) as it:
                    for s in range(2):
                        halves = 2 * (QUADS * (2 * l - 1) + 2 * it + s)
                        map_out(l, it, s, wbd, vin[s], lambda h: pe.wait_ge(relu_done, halves + h + 1))
                norm_sums(l)

            pe.wait_ge(bn_v, 3 * LAYERS + 1)
            nc.tensor.matmul(ps[:, 7, 0:1], tiny[:, 6:7].broadcast_to([128, 128]), tiny[:, 7:8], start=True, stop=True)\
                .then_inc(bn_p, 1)
            with pe.Fori(0, PAIRS) as it:
                for s in range(2):
                    for h in range(2):
                        pe.wait_ge(ld[s][h], 16 * (input_use(2 * LAYERS - 2, it) + 1))
                        if h == 0:
                            pe.wait_ge(proj_ev[s], past(it))
                        for n in range(4):
                            last = nc.tensor.matmul(ps[32 * n:32 * n + 32, 2 * s + h, :], proj,
                                                    half(vin[s], h)[:, 512 * n:512 * n + 512], start=True, stop=True)
                    last.then_inc(proj_full[s], 1)
            tensor_tokens(pe)

        @block.vector
        def _(dve):
            links = [0]

            def link(ins):
                links[0] += 1
                ins.then_inc(vchain, 1)
                dve.wait_ge(vchain, links[0])

            def part_evac(l, q, s, c):
                for h in range(2):
                    dve.wait_ge(dft_full, past(2 * c + h + 1))
                    if h == 0 and not isinstance(c, int):
                        dve.wait_ge(xs_full, past(x_step(l, q) - 1))
                    for ri in range(2):
                        src = ps[64:128, 2 * h:2 * h + 2, 0:384].rearrange("p b (c n) -> p n b c", c=4)
                        last = nc.vector.tensor_copy(
                            part[s][64 * ri:64 * ri + 64, :, 16 * h + 1:16 * h + 16:2]
                            .rearrange("p k (b c) -> p k b c", c=4), src[:, 48 * ri:48 * ri + 48])
                    last.then_inc(part_v, 1)

            def modes_evac(q, s, c):
                dve.wait_ge(xs_full, past(c + 1))
                for j in range(2, 4):
                    for ri in range(2):
                        src = ps[32 * j:32 * j + 32, 4 + 2 * s:6 + 2 * s, 0:288]\
                            .rearrange("p h (y r x) -> p h y r x", y=6, r=2)[:, :, :, ri, :]
                        dst = modes[32 * ri:32 * ri + 32, :, :, bass.ds(QUAD * q + j, 1)]\
                            .rearrange("p (h y) x b -> p h y (x b)", h=2)
                        last = nc.vector.tensor_copy(dst, src)
                last.then_inc(modes_v, 1)

            def y_rows(tile):
                return tile.rearrange("p (h c x) -> p x h c", h=2, x=SIDE)

            def x_y(tile):
                return tile.rearrange("p (x h y) -> p x h y", h=2, x=SIDE)

            def block_transpose(l, q, s, c):
                dve.wait_ge(relu_done, 2 * (QUADS * (2 * l - 2) + q + 1))
                dve.wait_ge(dft_full, past(2 * c - 2))
                nc.vector.transpose(y_rows(vmap[s]), x_y(vin[s])).then_inc(transposed, 1)

            def mix(l):
                def sign(ky):
                    w = wring[ky % 2][32:64, :, 0:32]
                    dve.wait_ge(w_in[ky % 2], 16 * (RING * l + ky // 2 + 1))
                    nc.vector.tensor_scalar(w, w, -1.0, None, ALU.mult).then_inc(signed[ky % 2], 1)

                sign(0)
                sign(1)
                for what, n in MIX_ORDER:
                    if what == "mix":
                        if n + 2 < KY:
                            sign(n + 2)
                    else:
                        for ky in (2 * n, 2 * n + 1):
                            dve.wait_ge(ix_full[1], KY * l + ky + 1)
                            dve.wait_ge(ix_st[ky % 2], 16 * (RING * l + n))
                            nc.vector.tensor_copy(xhalf[ky % 2][:, 1024:2048].rearrange("p (h n) -> p h n", h=2),
                                                  ps[:, 6:8, :]).then_inc(ix_ev[1], 1)

            def statistics(l, it, s):
                for h in range(2):
                    dve.wait_ge(out_ev[h], past(QUADS * l + 2 * it + s + 1))
                    for k in range(4):
                        n = 4 * h + k
                        last = nc.vector.bn_stats(
                            out=bnst[:, bass.ds((2 * it + s) * 8 + n, 1), :].rearrange("p a s -> p (a s)"),
                            in_=vmap[s][:, 512 * n:512 * n + 512])
                last.then_inc(stat_done[s], 1)

            def norm(l):
                for s in range(2):
                    dve.wait_ge(stat_done[s], past(PAIRS * (l + 1)))
                dve.wait_ge(layer_in, 80 * (l + 1))
                apart(dve)
                nc.vector.bn_aggr(out=mv, in_=bnst).then_inc(bn_v, 1)
                dve.wait_ge(bn_p, 2 * l + 1)
                dve.wait_ge(bn_v, 3 * l + 1)
                nc.vector.tensor_tensor(tiny[:, 1:2], mv[:, 0:1], ps[:, 0, 0:1], ALU.subtract).then_inc(t_ready, 1)
                dve.wait_ge(t_ready, 4 + 6 * l + 1)
                nc.vector.scalar_tensor_tensor(out=tiny[:, 0:1], in0=tiny[:, 1:2], scalar=tiny[:, 1:2],
                                               in1=mv[:, 1:2], op0=ALU.mult, op1=ALU.add).then_inc(bn_v, 1)
                nc.vector.tensor_tensor(tiny[:, 2:3], ps[:, 0, 0:1], lcols[:, 0:1], ALU.add).then_inc(t_ready, 1)
                dve.wait_ge(t_ready, 4 + 6 * l + 2)
                nc.vector.tensor_tensor(tiny[:, 4:5], lcols[:, 0:1], tiny[:, 2:3], ALU.subtract).then_inc(t_ready, 1)
                dve.wait_ge(bn_s, l + 1)
                nc.vector.reciprocal(tiny[:, 5:6], tiny[:, 3:4]).then_inc(t_ready, 1)
                dve.wait_ge(t_ready, 4 + 6 * l + 4)
                nc.vector.tensor_tensor(sc, tiny[:, 5:6], lcols[:, 1:2], ALU.mult).then_inc(t_ready, 1)
                dve.wait_ge(t_ready, 4 + 6 * l + 5)
                nc.vector.scalar_tensor_tensor(out=sh, in0=sc, scalar=tiny[:, 4:5], in1=lcols[:, 2:3],
                                               op0=ALU.mult, op1=ALU.add).then_inc(t_ready, 1)
                dve.wait_ge(t_ready, 4 + 6 * l + 6)
                nc.vector.tensor_copy(tiny[:, 6:7], sh).then_inc(bn_v, 1)
                dve.wait_ge(bn_v, 3 * l + 3)
                nc.vector.tensor_copy(tiny[:, 7:8], sh).then_inc(bn_ready, 1)

            nc.vector.memset(img[64:128, :], 0.0).then_inc(zeroed, 1)
            nc.vector.memset(prow, 0.0).then_inc(zeroed, 1)
            nc.vector.memset(wbd, 0.0).then_inc(zeroed, 1)
            nc.vector.memset(prt, 0.0).then_inc(zeroed, 1)
            nc.vector.memset(eps_col, BN_EPS).then_inc(zeroed, 1)

            dve.wait_ge(tables_in, 16 * 9)
            dve.wait_ge(grids_in, 32)
            dve.wait_ge(zeroed, 5)
            nc.vector.transpose(y_rows(vmap[0]), x_y(img)).then_inc(transposed, 1)
            exp3 = expand.rearrange("p (b c) -> p b c", c=CHANNELS)
            link(nc.vector.tensor_tensor(exp3, ident[:, 0:BATCH].unsqueeze(2).broadcast_to([128, BATCH, CHANNELS]),
                                         p0.unsqueeze(1).broadcast_to([128, BATCH, CHANNELS]), ALU.mult))
            nc.vector.tensor_tensor(exp3, exp3, prow.unsqueeze(1).broadcast_to([128, BATCH, CHANNELS]),
                                    ALU.add).then_inc(t_ready, 1)
            nc.vector.tensor_copy(prt[0:32, BATCH:BATCH + FEATURE_ROWS], pcol[0:32, 1:4]).then_inc(t_ready, 1)
            part_evac(0, 0, 0, 0)
            dve.wait_ge(xs_full, past(1))
            nc.vector.tensor_copy(spect[:, 288:576], ps[:, 5, 0:288]).then_inc(modes_v, 1)
            dve.wait_ge(t_ready, 1)
            for s in range(2):
                nc.vector.tensor_copy(estage[s], expand[:, 128 * s:128 * s + 128]).then_inc(e_copied[s], 1)
            dve.wait_ge(t_prod, 1)
            nc.vector.tensor_copy(p0c, ps[:, 0, 0:32])
            link(nc.vector.tensor_copy(prc, ps[:, 1, 0:32]))
            expc3 = expconv.rearrange("p (b c) -> p b c", c=CHANNELS)
            nc.vector.tensor_tensor(expc3, ident[:, 0:BATCH].unsqueeze(2).broadcast_to([128, BATCH, CHANNELS]),
                                    p0c.unsqueeze(1).broadcast_to([128, BATCH, CHANNELS]), ALU.mult).then_inc(t_ready, 1)
            dve.wait_ge(t_ready, 3)
            nc.vector.tensor_tensor(expc3, expc3, prc.unsqueeze(1).broadcast_to([128, BATCH, CHANNELS]),
                                    ALU.add).then_inc(t_ready, 1)
            dve.wait_ge(t_ready, 4)

            def expanded(it, more):
                for s in range(2):
                    dve.wait_ge(xs_full, past(x_step(0, 2 * it + s) + 1))
                    if more:
                        nc.vector.tensor_copy(estage[s], expand[:, bass.ds((2 * it + s + 2) * 128, 128)])\
                            .then_inc(e_copied[s], 1)
                    modes_evac(2 * it + s, s, x_step(0, 2 * it + s))

            with dve.Fori(0, PAIRS - 1) as it:
                expanded(it, True)
            expanded(PAIRS - 1, False)
            for s in range(2):
                nc.vector.tensor_copy(estage[s], expconv[:, 128 * s:128 * s + 128]).then_inc(e_copied[s], 1)
            mix(0)

            def expand_stats(it, more):
                for s in range(2):
                    if more:
                        dve.wait_ge(out_full[1], 2 * it + s + 1)
                        nc.vector.tensor_copy(estage[s], expconv[:, bass.ds((2 * it + s + 2) * 128, 128)])\
                            .then_inc(e_copied[s], 1)
                    statistics(0, it, s)

            with dve.Fori(0, PAIRS - 1) as it:
                expand_stats(it, True)
            expand_stats(PAIRS - 1, False)
            norm(0)

            with dve.Fori(1, LAYERS) as l:
                for s in range(2):
                    dve.wait_ge(map_st[s], past(32 * PAIRS * l))
                block_transpose(l, 0, 0, y_step(l, 0))
                block_transpose(l, 1, 1, y_step(l, 1))
                part_evac(l, 0, 0, y_step(l, 0))
                with dve.Fori(0, PAIRS - 1) as it:
                    for s in range(2):
                        q = 2 * it + s
                        block_transpose(l, q + 2, s, y_step(l, q + 2))
                        part_evac(l, q + 1, 1 - s, y_step(l, q + 1))
                        modes_evac(q, s, x_step(l, q))
                part_evac(l, QUADS - 1, 1, y_step(l, QUADS - 1))
                for s in range(2):
                    modes_evac(QUADS - 2 + s, s, x_step(l, QUADS - 2 + s))
                mix(l)
                with dve.Fori(0, PAIRS) as it:
                    for s in range(2):
                        statistics(l, it, s)
                norm(l)

            dve.wait_ge(bn_ready, LAYERS)
            link(nc.vector.tensor_tensor(tiny[:, 1:2], sc, qcols[:, 0:1], ALU.mult))
            link(nc.vector.tensor_scalar(proj, image_of, tiny[:, 1:2], None, ALU.mult))
            nc.vector.tensor_scalar(tiny[:, 7:8], qcols[:, 0:1], 1.0 / QUAD, None, ALU.mult).then_inc(bn_v, 1)
            dve.wait_ge(bn_p, 2 * LAYERS + 1)
            nc.vector.tensor_tensor(qbias, ps[:, 7, 0:1], qcols[:, 1:2], ALU.add).then_inc(bn_v, 1)
            vector_chain(dve, links)


INPUTS = ["images", "p_rows", "p_cols", "mode_w", "conv_w", "layer_cols", "q_cols", "cls_tok", "head_rows",
          "router_t", "w1_t", "b1_cols", "w2_rows", "b2_rows", "fy", "fx", "ix", "iy", "grids", "masks", "picks"]


def laid_out(x, cls_tok, L0_tok_p_w, L0_tok_p_b, L0_tok_fw1, L0_tok_fw2, L0_tok_w_w, L0_tok_w_b, L0_tok_bn_g,
             L0_tok_bn_b, L0_tok_q_w, L0_tok_q_b, L0_attn_kln_weight, L0_attn_kln_bias, L0_attn_vln_weight,
             L0_attn_vln_bias, L0_ffn_router_w, L0_ffn_w1, L0_ffn_b1, L0_ffn_w2, L0_ffn_b2):
    a = np.asarray
    p_rows = np.concatenate([a(L0_tok_p_w), a(L0_tok_p_b).reshape(1, -1)])
    f = np.stack([a(L0_tok_fw1), a(L0_tok_fw2)], axis=1)
    f = f.transpose(0, 5, 6, 2, 1, 4, 3).reshape(LAYERS, KY, 2, CHANNELS, KX, CHANNELS)
    direct, swapped = f.transpose(0, 1, 3, 4, 2, 5), f[:, :, ::-1].transpose(0, 1, 3, 4, 2, 5)
    mode_w = np.stack([direct, swapped], axis=2).reshape(LAYERS, KY, 64, KX * 64)
    cols = np.stack([a(L0_tok_w_b), a(L0_tok_bn_g), a(L0_tok_bn_b)], axis=2)
    layer_cols = np.tile(cols, (1, QUAD, 1))
    q_cols = np.stack([np.tile(a(L0_tok_q_w)[:, 0], QUAD), np.tile(a(L0_tok_q_b), 128)], axis=1)
    head_rows = np.stack([a(v).reshape(-1) for v in
                          (L0_attn_kln_weight, L0_attn_kln_bias, L0_attn_vln_weight, L0_attn_vln_bias)])
    fy, fx, ix, iy = transform_tables()
    grids, masks, picks = shape_tables()
    return {
        "images": a(x).reshape(BATCH, POSITIONS), "p_rows": p_rows, "p_cols": p_rows.T, "mode_w": mode_w,
        "conv_w": a(L0_tok_w_w), "layer_cols": layer_cols, "q_cols": q_cols, "cls_tok": a(cls_tok).reshape(1, DIM),
        "head_rows": head_rows, "router_t": a(L0_ffn_router_w).T, "w1_t": a(L0_ffn_w1).transpose(1, 0, 2),
        "b1_cols": a(L0_ffn_b1).reshape(EXPERTS // 2, 128).T, "w2_rows": a(L0_ffn_w2).reshape(EXPERTS // 2, 128, DIM)
        .transpose(1, 0, 2), "b2_rows": a(L0_ffn_b2), "fy": fy, "fx": fx, "ix": ix, "iy": iy, "grids": grids,
        "masks": masks, "picks": picks}


def kernel(**inputs):
    import concourse.bacc as bacc
    from concourse.bass_utils import run_bass_kernel_spmd

    nc = bacc.Bacc("TRN2", target_bir_lowering=False, num_devices=1)
    laid = laid_out(**inputs)
    arrays, args = {}, []
    for name in INPUTS:
        array = np.ascontiguousarray(laid[name])
        arrays[f"in_{name}"] = array
        args.append(nc.dram_tensor(f"in_{name}", array.shape, mybir.dt.from_np(array.dtype), kind="ExternalInput").ap())
    out = nc.dram_tensor("out_tokens", (BATCH, TOKENS, DIM), mybir.dt.float32, kind="ExternalOutput").ap()
    tower_kernel(nc, *args, out)
    r = run_bass_kernel_spmd(nc, [arrays], core_ids=[0])
    return r.results[0]["out_tokens"]
```

```python
import numpy as np
import concourse.bass as bass
from concourse import mybir
from contextlib import ExitStack

BATCH, SIDE, CHANNELS, LAYERS = 64, 64, 32, 4
KX_HALF, KY = 12, 12
KX = 2 * KX_HALF
POSITIONS = SIDE * SIDE
QUAD = 4
QUADS = BATCH // QUAD
PAIRS = QUADS // 2
FEATURE_ROWS = 3
BN_EPS = 1e-5
HEADS, HEAD_DIM = 8, 8
DIM = HEADS * HEAD_DIM
EXPERTS = 8
TOKENS = SIDE + 1
LN_EPS = 1e-5
SLOTS = BATCH // 2 + 1


def transform_tables():
    kx = np.concatenate([np.arange(KX_HALF), np.arange(SIDE - KX_HALF, SIDE)]).astype(np.float64)
    ky = np.arange(KY, dtype=np.float64)
    pos = np.arange(SIDE, dtype=np.float64)
    ang = 2 * np.pi * np.outer(pos, ky) / SIDE
    fy = np.zeros((2, QUAD, 32, 2, KY, QUAD))
    for half in range(2):
        for j in range(QUAD):
            fy[half, j, :, 0, :, j] = np.cos(ang[half * 32:half * 32 + 32])
            fy[half, j, :, 1, :, j] = -np.sin(ang[half * 32:half * 32 + 32])
    ang = 2 * np.pi * np.outer(pos, kx) / SIDE
    fx = np.zeros((2, SIDE, 2, KX))
    fx[0, :, 0], fx[1, :, 0] = np.cos(ang), np.sin(ang)
    fx[0, :, 1], fx[1, :, 1] = -np.sin(ang), np.cos(ang)
    order = (np.arange(4)[:, None] + 4 * np.arange(16)[None, :]).reshape(-1)
    ang = 2 * np.pi * np.outer(kx, pos[order]) / SIDE
    ix = np.zeros((2, KX, 2, SIDE))
    ix[0, :, 0], ix[1, :, 0] = np.cos(ang), -np.sin(ang)
    ix[0, :, 1], ix[1, :, 1] = np.sin(ang), np.cos(ang)
    ix = (ix / SIDE).reshape(48, 128)
    ix2 = np.zeros((2, 48, 2, 128))
    ix2[0, :, 0], ix2[1, :, 1] = ix, ix
    ang = 2 * np.pi * np.outer(ky, pos) / SIDE
    weight = np.where(ky == 0, 1.0, 2.0)[:, None] / SIDE
    iy = np.zeros((4, KY, 2, 4, SIDE))
    for x in range(4):
        iy[x, :, 0, x], iy[x, :, 1, x] = weight * np.cos(ang), -weight * np.sin(ang)
    table = lambda a, rows: np.ascontiguousarray(a.reshape(rows, -1), dtype=np.float32)
    return (np.ascontiguousarray(fy.reshape(2, 128, 96).transpose(1, 0, 2).reshape(128, 192), dtype=np.float32),
            table(fx, 128), table(ix2, 96), table(iy, 96))


def shape_tables():
    line = np.linspace(0.0, 1.0, SIDE, dtype=np.float32)
    grids = np.ones((FEATURE_ROWS, SIDE, SIDE), np.float32)
    grids[0] = line[:, None]
    grids[1] = line[None, :]
    p = np.arange(128)
    ident = np.eye(128, dtype=np.float32)
    average = (p[:, None] % 32 == p[None, :] % 32).astype(np.float32) / QUAD
    image_of = (p[:, None] // 32 == np.arange(32)[None, :]).astype(np.float32)
    split_rows = ((p[:, None] % 64 == np.arange(32)[None, :])).astype(np.float32)
    head = np.arange(64) // HEAD_DIM
    heads = (head[:, None] == head[None, :]).astype(np.float32) / np.float32(TOKENS)
    heads = np.concatenate([heads, heads])
    picks = np.tile(np.repeat(np.eye(EXPERTS, dtype=np.float32), 64, axis=1), (3, 1))
    falling = np.tile(np.arange(EXPERTS, 0, -1, dtype=np.float32), (128, 1))
    return (grids.reshape(FEATURE_ROWS, POSITIONS),
            np.ascontiguousarray(np.concatenate([ident, average, image_of, heads, falling, split_rows], axis=1)), picks)


def tower_kernel(nc, images, p_rows, p_cols, mode_w, conv_w, layer_cols, q_cols, cls_tok, head_rows,
                 router_t, w1_t, b1_cols, w2_rows, b2_rows, fy_d, fx_d, ix_d, iy_d, grids_d, masks_d, picks_d, out):
    fp32 = mybir.dt.float32
    ALU = mybir.AluOpType
    ACT = mybir.ActivationFunctionType
    AX = mybir.AxisListType

    raw_d = nc.dram_tensor("raw_maps", [LAYERS, QUADS, 128, POSITIONS], fp32, kind="Internal").ap()
    mixed_d = nc.dram_tensor("mixed_modes", [2 * KX, KY // 2, CHANNELS, 2 * BATCH], fp32, kind="Internal").ap()
    half_d = nc.dram_tensor("half_inverse", [KY * 2, 4, 16, BATCH * CHANNELS], fp32, kind="Internal").ap()
    tok_d = nc.dram_tensor("token_maps", [BATCH, 8, 512], fp32, kind="Internal").ap()

    ctx = ExitStack()
    with ctx:
        def sem(name):
            return ctx.enter_context(nc.semaphore(name))

        def sems(name, n=2):
            return [sem(f"{name}{i}") for i in range(n)]

        fp32r = mybir.dt.float32r
        MODES = KX * KY * BATCH
        with nc.sbuf_tensor("inputs", [128, 2 * POSITIONS], fp32) as inputs:
            pass
        inputs_r = ctx.enter_context(nc.sbuf_tensor("inputs_r", [128, 2 * POSITIONS], fp32r))
        with nc.sbuf_tensor("modes_region", [128, MODES], fp32) as modes_region:
            pass
        MODES_R = 4 * 2048 + 2 * 1024 + 4 * 128 + 2 * 256
        modes_r = ctx.enter_context(nc.sbuf_tensor("modes_r", [128, MODES_R], fp32r))
        ctx.enter_context(nc.sbuf_tensor("rest_of_modes", [128, MODES - MODES_R], fp32))
        AT_ARENA = 2 * POSITIONS + MODES
        arena = ctx.enter_context(nc.sbuf_tensor("arena", [128, 53032 - AT_ARENA], fp32))
        ps = ctx.enter_context(nc.psum_tensor("ps", [128, 8, 512], fp32))
        top = [0]

        def take(n):
            top[0] += n
            return top[0] - n

        def view(at, n):
            if at + n <= 2 * POSITIONS:
                return inputs[:, at:at + n]
            if at + n <= AT_ARENA:
                return modes_region[:, at - 2 * POSITIONS:at - 2 * POSITIONS + n]
            return arena[:, at - AT_ARENA:at - AT_ARENA + n]

        at_in = take(2 * POSITIONS)
        at_modes = take(MODES)
        at_map = take(2 * POSITIONS)
        at_part = take(2 * 48 * CHANNELS)
        at_w = take(2 * KX * 64)
        at_w2 = take(KX * 64)
        at_img = take(POSITIONS)
        at_half = take(2 * 2048)
        vin = [view(at_in + s * POSITIONS, POSITIONS) for s in range(2)]
        vmap = [view(at_map + s * POSITIONS, POSITIONS) for s in range(2)]
        modes = view(at_modes, KX * KY * BATCH).rearrange("p (y x b) -> p y x b", y=KY, x=KX)
        part = [view(at_part + s * 48 * CHANNELS, 48 * CHANNELS).rearrange("p (k c) -> p k c", c=CHANNELS)
                for s in range(2)]
        wring = [view(at, KX * 64).rearrange("p (x n) -> p x n", x=KX)
                 for at in (at_w, at_w + KX * 64, at_w2, at_map)]
        mixed = [view(at_map + POSITIONS + s * 1536, 1536).rearrange("p (h k e b) -> p e h k b", h=2, e=2, b=BATCH)
                 for s in range(2)]
        img = view(at_img, POSITIONS)
        kxin = [view(at_in + 4096 + s * 2048, 2048) for s in range(2)]
        xhalf = [view(at_half + s * 2048, 2048) for s in range(2)]
        at_g = at_modes + MODES_R
        gtile = [view(at_g + s * 2048, 2048).rearrange("p (g n) -> p g n", g=16) for s in range(2)]
        expand = view(at_map + POSITIONS, BATCH * CHANNELS)
        expconv = view(at_part, BATCH // 2 * CHANNELS)
        feats = [inputs_r[:, u * POSITIONS:(u + 1) * POSITIONS] for u in range(2)]
        part_r = lambda at, n: modes_r[:, at:at + n]
        ghigh = [part_r(s * 2048, 2048).rearrange("p (g n) -> p g n", g=16) for s in range(2)]
        glow = [part_r(4096 + s * 2048, 2048).rearrange("p (g n) -> p g n", g=16) for s in range(2)]
        exphigh, explow = part_r(8192, 1024), part_r(9216, 1024)
        rstage = [[part_r(10240 + 256 * s + 128 * i, 128) for i in range(2)] for s in range(2)]
        iyhigh, iylow = part_r(10752, 256), part_r(11008, 256)
        spect = view(at_half, 576)
        bnst = view(at_part + BATCH * CHANNELS, QUADS * 8 * 6).rearrange("p (k s) -> p k s", s=6)
        at_small = top[0]
        fy = view(take(192), 192).rearrange("p (h n) -> p h n", h=2)
        fx = view(take(48), 48)
        ix = view(take(256), 256)
        iy = view(take(256), 256)
        masks = view(take(128 + 128 + 32 + 64 + 8 + 32), 392)
        ident, average, image_of = masks[:, 0:128], masks[:, 128:256], masks[:, 256:288]
        head_mask, falling, split_rows = masks[:, 288:352], masks[:, 352:360], masks[:, 360:392]
        wbd = view(take(128), 128)
        lcols = view(take(3), 3)
        qcols = view(take(2), 2)
        p0 = view(take(32), 32)
        prow = view(take(32), 32)
        pcol = view(take(4), 4)
        prt = view(take(128), 128)
        p0c = view(take(32), 32)
        prc = view(take(32), 32)
        estage = [view(take(128), 128) for _ in range(2)]
        mv = view(take(2), 2)
        tiny = view(take(8), 8)
        sc, sh = view(take(1), 1), view(take(1), 1)
        proj = view(take(32), 32)
        qbias = view(take(1), 1)
        eps_col = view(take(1), 1)
        hrow = [view(at_img + s * 1024, 1024) for s in range(2)]

        tables_in = sem("tables_in")
        zeroed = sem("zeroed")
        grids_in = sem("grids_in")
        layer_in = sem("layer_in")
        t_ready = sem("t_ready")
        t_prod = sem("t_prod")
        e_copied = sems("e_copied")
        f_in = sems("f_in")
        f_high, f_low = sem("f_high"), sem("f_low")
        t_split = sem("t_split")
        r_copied = sems("r_copied")
        g_high, g_low = sem("g_high"), sem("g_low")
        ld = [sems("ld_a"), sems("ld_b")]
        relu_done = sem("relu_done")
        transposed = sem("transposed")
        dft_full = sem("dft_full")
        part_a, part_v = sem("part_a"), sem("part_v")
        xs_full = sem("xs_full")
        modes_a, modes_v = sem("modes_a"), sem("modes_v")
        w_in = sems("w_in", 4)
        signed = sem("signed")
        mix_full = sems("mix_full")
        mix_ev = sems("mix_ev")
        mix_st = sems("mix_st")
        kx_in = sems("kx_in")
        ix_full = sems("ix_full")
        ix_ev = sems("ix_ev")
        ix_st = sems("ix_st")
        ix_head = sem("ix_head")
        g_in = sems("g_in")
        out_full = sems("out_full")
        out_ev = sems("out_ev")
        stat_done = sems("stat_done")
        map_st = sems("map_st")
        bn_v, bn_p, bn_s = sem("bn_v"), sem("bn_p"), sem("bn_s")
        bn_ready = sem("bn_ready")
        vchain = sem("vchain")
        proj_full, proj_ev, proj_st = sems("proj_full"), sems("proj_ev"), sems("proj_st")
        passed = sem("passed")
        from_one = [dft_full, xs_full, modes_a, modes_v, *out_ev, *stat_done, *map_st, *proj_ev, *proj_st]

        def past(n):
            return n + 1

        at_tail = at_small - 4 * SLOTS - 3 * SLOTS * HEADS

        COLS = SLOTS * DIM
        MAPS = (BATCH // 2) * DIM
        TCOLS = SLOTS * 128
        tok = lambda n=COLS: view(take(n), n)
        as_slots = lambda t: t.rearrange("p (s d) -> p s d", d=DIM)
        as_heads = lambda t: t.rearrange("p (g d) -> p g d", d=HEAD_DIM)
        bf16 = mybir.dt.bfloat16
        top[0] = at_modes
        h0, n1, dev, sq, kk, vk, hsum = (tok() for _ in range(7))
        hrows = view(take(256), 256)
        router = view(take(EXPERTS), EXPERTS)
        w1 = view(take(512), 512)
        w2 = view(take(256), 256).rearrange("p (e d) -> p e d", d=DIM)
        b1 = view(take(4), 4)
        b2 = view(take(DIM), DIM)
        picks = view(take(512), 512)
        pick = view(take(256), 256).bitcast(bf16)
        b2p = [view(take(DIM // 2), DIM // 2).bitcast(bf16) for _ in range(3)]
        assert top[0] <= at_map
        top[0] = at_map
        n1t = view(take(TCOLS), TCOLS)
        hid = [n1t] + [view(take(TCOLS), TCOLS) for _ in range(EXPERTS // 2 - 1)]
        combt = view(take(TCOLS // 2), TCOLS // 2).bitcast(bf16)
        assert top[0] <= at_tail
        h1, n2 = kk, vk
        outt = view(at_modes + 4 * COLS, 2048 + 128)
        top[0] = 0

        def take_r(n):
            at = take(n)
            return inputs_r[:, at:at + n]

        n2r = take_r(TCOLS)
        w1h, w1l, rth, rtl = take_r(512), take_r(512), take_r(EXPERTS), take_r(EXPERTS)
        kvm = hid[1][:, 0:4096]
        kvc = view(take(DIM), DIM)
        clst = view(take(DIM), DIM)
        assert top[0] <= at_modes
        comb3 = h0[:, 1320:2112].rearrange("p (s e) -> p s e", e=24)
        s1, s2, s3, s4 = (view(at_tail + SLOTS * i, SLOTS) for i in range(4))
        g1, g2, g3 = (view(at_tail + 4 * SLOTS + SLOTS * HEADS * i, SLOTS * HEADS) for i in range(3))

        tok_in = sem("tok_in")
        ln_sum, ln_root = sem("ln_sum"), sem("ln_root")
        n1_ready, kv_ready = sem("n1_ready"), sem("kv_ready")
        n2_ready = sem("n2_ready")
        job_full = sems("job_full")
        job_ev = sems("job_ev")
        tok_st = sems("tok_st", 5)
        n2_high = sem("n2_high")
        parted = sem("parted")
        exp_out = sem("exp_out")
        spread_full, spread_ev = sem("spread_full"), sem("spread_ev")
        split_ready = sem("split_ready")
        out_ready = sem("out_ready")
        stored = sem("stored")
        (J_N1T, J_N1T2, J_N1C, J_KVC, J_KV, J_KV2, J_ATT, J_ATT2, J_CLS, J_CLST, J_N2T, J_N2T2, J_N2C, J_LOG,
         J_UP) = range(15)
        J_CT = J_UP + 12
        J_OUT = J_CT + 3
        SPREAD = tuple((c, min(1024, TCOLS - c)) for c in range(0, TCOLS, 1024))

        PROJECTED = [QUADS - 2, QUADS - 1, *range(QUADS - 2)]
        GROUPS = ((14, 2), (0, 4), (4, 4), (8, 4), (12, 2))
        ENDS = (2, 6, 10, 14, 16)
        NORMED = ((BATCH // 2, 1), *((2 * a, 2 * n) for a, n in GROUPS))
        PARTS = ((0, 2048), (2048, 2048), (4096, 128))

        def bank(k):
            return 4 * (k % 2)

        def wait_full(eng, k):
            eng.wait_ge(job_full[k % 2], k // 2 + 1)

        def wait_evacuated(eng, k):
            eng.wait_ge(job_ev[k % 2], k // 2 + 1)

        def sync_constants(sp):
            sp.dma_start(as_slots(h0)[:, BATCH // 2, :], cls_tok.broadcast_to([128, DIM])).then_inc(tok_in, 16)
            sp.dma_start(hrows.rearrange("p (a d) -> p a d", a=4),
                         head_rows.unsqueeze(0).broadcast_to([128, 4, DIM])).then_inc(tok_in, 16)
            for i in range(2):
                rows = slice(64 * i, 64 * i + 64)
                sp.dma_start(router[rows], router_t).then_inc(tok_in, 16)
                sp.dma_start(w1[rows].rearrange("p (e f) -> p e f", e=EXPERTS), w1_t).then_inc(tok_in, 16)
            sp.dma_start(w2, w2_rows).then_inc(tok_in, 16)
            sp.dma_start(b1, b1_cols).then_inc(tok_in, 16)
            sp.dma_start(picks[0:24], picks_d).then_inc(tok_in, 16)
            for i in range(3):
                sp.dma_start(b2[8 * i:8 * i + 8], b2_rows).then_inc(tok_in, 16)

        def group_load(sp, c):
            quad, n = GROUPS[c]
            for s in range(2):
                sp.wait_ge(proj_st[s], past(64 * ENDS[c] // 2))
            sp.dma_start(as_slots(h0)[:, 2 * quad:2 * (quad + n), :],
                         tok_d[QUAD * quad:QUAD * (quad + n)].rearrange("(s e) r (u y) -> (e r u) s y", e=2, y=DIM))\
              .then_inc(tok_st[c], 16)

        def sync_tokens(sp):
            o = as_slots(dev)
            for i in range(2):
                sp.wait_ge(out_ready, i + 1)
                for e in range(2):
                    sp.dma_start(out[32 * i + e:32 * i + 32:2, 1:TOKENS, :].rearrange("s t d -> t s d"),
                                 o[64 * e:64 * e + 64, 16 * i:16 * i + 16, :]).then_inc(stored, 16)
            sp.wait_ge(out_ready, 3)
            sp.dma_start(out[:, 0, :], o[0:BATCH, BATCH // 2, :]).then_inc(stored, 16)
            sp.wait_ge(stored, 80)

        def spans(a, n):
            return slice(a, a + n), slice(HEADS * a, HEADS * (a + n))

        def first_root(act, i):
            sl, hd = spans(*NORMED[i // 2])
            which, step = i % 2, i + 1
            act.wait_ge(ln_sum, step)
            if which == 0:
                nc.scalar.activation(s3[:, sl], s2[:, sl], ACT.Sqrt, bias=eps_col, scale=1.0 / DIM)\
                    .then_inc(ln_root, 1)
            else:
                nc.scalar.activation(g3[:, hd], g2[:, hd], ACT.Sqrt, bias=0.0, scale=1.0 / (HEAD_DIM - 1))\
                    .then_inc(ln_root, 1)

        def scalar_tokens(act):
            def evac(k, dst, rows, width):
                wait_full(act, k)
                src = ps[0:rows, bank(k):bank(k) + 4, :].rearrange("p b n -> p (b n)")[:, 0:width]
                return nc.scalar.copy(dst, src)

            def last_root(i, a, n):
                act.wait_ge(ln_sum, 2 * len(NORMED) + 1 + i)
                nc.scalar.activation(s3[:, a:a + n], s2[:, a:a + n], ACT.Sqrt, bias=eps_col, scale=1.0 / DIM)\
                    .then_inc(ln_root, 1)

            for k, (at, n) in zip((J_N1T, J_N1T2, J_N1C), PARTS):
                evac(k, n1t[0:64, at:at + n], 64, n).then_inc(job_ev[k % 2], 1)
            last_root(0, 0, 16)
            last_root(1, 16, 16)
            evac(J_CLS, clst[0:64], 64, BATCH).then_inc(job_ev[J_CLS % 2], 1)
            last_root(2, 32, 1)
            for k, (at, n) in zip((J_N2T, J_N2T2, J_N2C), PARTS):
                evac(k, n2r[:, at:at + n], 128, n).then_inc(n2_high, 1)
            wait_evacuated(act, J_LOG)
            nc.scalar.activation(g2, g1, ACT.Exp).then_inc(exp_out, 1)

            def gelu(p):
                for i, (at, n) in enumerate(PARTS):
                    k = J_UP + 3 * p + i
                    wait_full(act, k)
                    src = ps[:, bank(k):bank(k) + 4, :].rearrange("p b n -> p (b n)")[:, 0:n]
                    nc.scalar.activation(hid[p][:, at:at + n], src, ACT.Gelu, bias=b1[:, p:p + 1])\
                        .then_inc(job_ev[k % 2], 1)

            for p in range(EXPERTS // 2):
                gelu(p)
            at, n = PARTS[1]
            evac(J_CT + 1, combt[0:24, at:at + n], 24, n).then_inc(job_ev[(J_CT + 1) % 2], 1)
            evac(J_OUT, outt[:, 0:2048], 128, 2048).then_inc(job_ev[J_OUT % 2], 1)
            evac(J_OUT + 1, outt[0:64, 2048:2176], 64, 128).then_inc(job_ev[(J_OUT + 1) % 2], 1)

        def tensor_tokens(pe):
            def begin(k):
                pe.wait_ge(job_ev[k % 2], k // 2)

            def cols(k, rows, width):
                return ps[rows, bank(k):bank(k) + 4, :].rearrange("p b n -> p (b n)")[:, 0:width]

            def turn(k, tiles, source, rows):
                begin(k)
                for i, t in enumerate(tiles):
                    last = nc.tensor.transpose(cols(k, rows, 2048)[:, 128 * i:128 * i + 128], source[:, t, :],
                                               ident)
                last.then_inc(job_full[k % 2], 1)

            groups = (range(0, 16), range(16, 32), range(32, 33))
            low, high = slice(0, 64), slice(64, 128)
            for s in range(2):
                pe.wait_ge(proj_ev[s], past(PAIRS))
            pe.wait_ge(tok_in, 16 * 12)
            pe.wait_ge(n1_ready, len(NORMED))
            for k, tiles in zip((J_N1T, J_N1T2, J_N1C), groups):
                turn(k, tiles, as_slots(n1), low)
            pe.wait_ge(kv_ready, len(NORMED))
            k3, v3 = as_slots(kk), as_slots(vk)
            begin(J_KVC)
            nc.tensor.matmul(cols(J_KVC, low, 64), k3[low, BATCH // 2, :], v3[low, BATCH // 2, :], start=True,
                             stop=True).then_inc(job_full[J_KVC % 2], 1)
            for e, k in ((0, J_KV), (1, J_KV2)):
                begin(k)
                rows = slice(64 * e, 64 * e + 64)
                for t in range(BATCH // 2):
                    last = nc.tensor.matmul(cols(k, low, 2048)[:, 64 * t:64 * t + 64], k3[rows, t, :],
                                            v3[rows, t, :], start=True, stop=True)
                last.then_inc(job_full[k % 2], 1)
            for k, tiles in ((J_ATT, groups[0]), (J_ATT2, groups[1])):
                for e in range(2):
                    wait_evacuated(pe, (J_KV, J_KV2)[e])
                    if e == 0:
                        begin(k)
                    for i, t in enumerate(tiles):
                        last = nc.tensor.matmul(cols(k, slice(64 * e, 64 * e + 64), 2048)[:, 64 * i:64 * i + 64],
                                                n1t[0:64, 128 * t + 64 * e:128 * t + 64 * e + 64],
                                                kvm[0:64, 2048 * e + 64 * t:2048 * e + 64 * t + 64],
                                                start=True, stop=True)
                last.then_inc(job_full[k % 2], 1)
            begin(J_CLS)
            for b in range(BATCH):
                at = 2048 * (b % 2) + 64 * (b // 2)
                last = nc.tensor.matmul(cols(J_CLS, low, 64)[:, b:b + 1], kvm[0:64, at:at + 64],
                                        n1t[0:64, 4096:4097], start=True, stop=True)
            last.then_inc(job_full[J_CLS % 2], 1)
            wait_evacuated(pe, J_CLS)
            begin(J_CLST)
            nc.tensor.transpose(cols(J_CLST, low, 64), clst[0:64], ident[0:64, 0:64])\
                .then_inc(job_full[J_CLST % 2], 1)
            for i, (k, tiles) in enumerate(zip((J_N2T, J_N2T2, J_N2C), groups)):
                pe.wait_ge(n2_ready, i + 1)
                begin(k)
                for j, t in enumerate(tiles):
                    for rows in (low, high):
                        last = nc.tensor.matmul(cols(k, rows, 2048)[:, 128 * j:128 * j + 128], as_slots(n2)[:, t, :],
                                                ident, start=True, stop=True)
                last.then_inc(job_full[k % 2], 1)
            wait_evacuated(pe, J_N2C)
            wait_evacuated(pe, J_N2T2)
            pe.wait_ge(parted, 4)
            begin(J_LOG)
            for t in range(SLOTS):
                for i, part in enumerate((rth, rtl)):
                    last = nc.tensor.matmul(cols(J_LOG, slice(0, 128), 264)[:, 8 * t:8 * t + 8],
                                            n2r[:, 128 * t:128 * t + 128], part, start=(i == 0), stop=(i == 1))
            last.then_inc(job_full[J_LOG % 2], 1)

            def up(p):
                for i, (at, n) in enumerate(PARTS):
                    k = J_UP + 3 * p + i
                    begin(k)
                    for j, part in enumerate((w1h, w1l)):
                        for c in range(0, n, 512):
                            w = min(512, n - c)
                            last = nc.tensor.matmul(ps[:, bank(k) + c // 512, 0:w], part[:, 128 * p:128 * p + 128],
                                                    n2r[:, at + c:at + c + w], start=(j == 0), stop=(j == 1))
                    last.then_inc(job_full[k % 2], 1)

            for p in range(EXPERTS // 2):
                up(p)
            pe.wait_ge(split_ready, 1)
            for i, tiles in enumerate(groups):
                turn(J_CT + i, tiles, comb3, slice(0, 24))
            for i in range(3):
                wait_evacuated(pe, J_CT + i)
            def second_layer(k, step, c, width, parts, first, last_one):
                weights, tokens = step
                for i, (at, n) in enumerate(parts):
                    last = nc.tensor.matmul(ps[64 * i:64 * i + 64, bank(k) + c, 0:width], weights,
                                            tokens[:, at + width * c:at + width * c + width], start=first,
                                            stop=last_one)
                return last

            biases = [(b2p[i][0:24, :], combt[0:24]) for i in range(3)]
            experts = [(w2[:, p, :], hid[p]) for p in range(EXPERTS // 2)]
            begin(J_OUT)
            pe.wait_ge(job_ev[(J_OUT + 1) % 2], (J_OUT + 1) // 2)
            for p in range(EXPERTS // 2):
                for j, (at, n) in enumerate(SPREAD):
                    step = len(SPREAD) * p + j
                    if step >= 2:
                        pe.wait_ge(spread_ev, step - 1)
                    for c in range(0, n, 512):
                        w = min(512, n - c)
                        last = nc.tensor.matmul(ps[:, bank(J_OUT + 1) + 2 * (step % 2) + c // 512, 0:w],
                                                pick[0:24, 128 * p:128 * p + 128],
                                                combt[0:24, at + c:at + c + w], start=True, stop=True)
                    last.then_inc(spread_full, 1)
                    if j < 4:
                        if p == 0:
                            for i, bias in enumerate(biases):
                                second_layer(J_OUT, bias, j, 512, PARTS[0:2], i == 0, False)
                        else:
                            pe.wait_ge(spread_ev, len(SPREAD) * p)
                            second_layer(J_OUT, experts[p - 1], j, 512, PARTS[0:2], False, False)
            pe.wait_ge(spread_ev, len(SPREAD) * (EXPERTS // 2))
            for j in range(4):
                last = second_layer(J_OUT, experts[-1], j, 512, PARTS[0:2], False, True)
            last.then_inc(job_full[J_OUT % 2], 1)
            for i, step in enumerate(biases + experts):
                last = second_layer(J_OUT + 1, step, 0, 128, PARTS[2:3], i == 0, i == 6)
            last.then_inc(job_full[(J_OUT + 1) % 2], 1)
            begin(J_OUT + 2)
            for c in range(16):
                last = nc.tensor.transpose(cols(J_OUT + 2, slice(0, 128), 2048)[:, 128 * c:128 * c + 128],
                                           outt[:, 128 * c:128 * c + 128], ident)
            last.then_inc(job_full[(J_OUT + 2) % 2], 1)
            begin(J_OUT + 3)
            nc.tensor.transpose(cols(J_OUT + 3, slice(0, 128), 64), outt[0:64, 2048:2176], ident[0:64, 0:64])\
                .then_inc(job_full[(J_OUT + 3) % 2], 1)

        def vector_first_norms(dve, link, a, n, k):
            sl, hd = spans(a, n)
            at = slice(DIM * a, DIM * (a + n))
            x3, d3, q3 = (as_slots(t)[:, sl, :] for t in (h0, dev, sq))
            wide = lambda t: t[:, sl].unsqueeze(2).broadcast_to([128, n, DIM])
            link(nc.vector.reduce_sum(s1[:, sl], x3, AX.X))
            link(nc.vector.tensor_scalar(s4[:, sl], s1[:, sl], 1.0 / DIM, None, ALU.mult))
            link(nc.vector.tensor_tensor(d3, x3, wide(s4), ALU.subtract))
            link(nc.vector.tensor_tensor(sq[:, at], dev[:, at], dev[:, at], ALU.mult))
            nc.vector.reduce_sum(s2[:, sl], q3, AX.X).then_inc(ln_sum, 1)
            dve.wait_ge(ln_root, k)
            link(nc.vector.reciprocal(s4[:, sl], s3[:, sl]))
            link(nc.vector.tensor_tensor(as_slots(n1)[:, sl, :], d3, wide(s4), ALU.mult))
            nc.vector.tensor_tensor(hsum[:, at], h0[:, at], n1[:, at], ALU.add).then_inc(n1_ready, 1)
            n3, d3, q3 = (as_heads(t)[:, hd, :] for t in (n1, dev, sq))
            wide = lambda t: t[:, hd].unsqueeze(2).broadcast_to([128, n * HEADS, HEAD_DIM])
            link(nc.vector.reduce_sum(g1[:, hd], n3, AX.X))
            link(nc.vector.tensor_scalar(g2[:, hd], g1[:, hd], 1.0 / HEAD_DIM, None, ALU.mult))
            link(nc.vector.tensor_tensor(d3, n3, wide(g2), ALU.subtract))
            link(nc.vector.tensor_tensor(sq[:, at], dev[:, at], dev[:, at], ALU.mult))
            nc.vector.reduce_sum(g2[:, hd], q3, AX.X).then_inc(ln_sum, 1)
            dve.wait_ge(ln_root, k + 1)
            link(nc.vector.tensor_scalar(g1[:, hd], g3[:, hd], LN_EPS, None, ALU.add))
            link(nc.vector.reciprocal(g2[:, hd], g1[:, hd]))
            link(nc.vector.tensor_tensor(q3, d3, wide(g2), ALU.mult))
            row = lambda i: hrows[:, 64 * i:64 * i + 64].unsqueeze(1).broadcast_to([128, n, DIM])
            k3, v3, q3 = (as_slots(t)[:, sl, :] for t in (kk, vk, sq))
            link(nc.vector.tensor_tensor(k3, q3, row(0), ALU.mult))
            nc.vector.tensor_tensor(v3, q3, row(2), ALU.mult)
            link(nc.vector.tensor_tensor(k3, k3, row(1), ALU.add))
            last = nc.vector.tensor_tensor(v3, v3, row(3), ALU.add)
            if a == BATCH // 2:
                link(last)
                last = nc.vector.tensor_scalar(vk[:, MAPS:COLS], vk[:, MAPS:COLS], 1.0 / 64, None, ALU.mult)
            last.then_inc(kv_ready, 1)

        def vector_chain(dve, links):
            def link(ins):
                links[0] += 1
                ins.then_inc(vchain, 1)
                dve.wait_ge(vchain, links[0])

            dve.wait_ge(tok_in, 16 * 12)
            for i, (a, n) in enumerate(NORMED):
                if i:
                    dve.wait_ge(tok_st[i - 1], 16)
                vector_first_norms(dve, link, a, n, 2 * i + 1)
            for s in range(2):
                dve.wait_ge(proj_full[s], PAIRS)
                dve.wait_ge(proj_st[s], past(64 * PAIRS))
            for whole, high, low in ((w1, w1h, w1l), (router, rth, rtl)):
                nc.vector.tensor_copy(high, whole).then_inc(parted, 1)
                dve.wait_ge(parted, 1 if whole is w1 else 3)
                nc.vector.tensor_tensor(low, whole, high.bitcast(fp32), ALU.subtract).then_inc(parted, 1)
            heads = lambda n: head_mask[0:64].unsqueeze(1).broadcast_to([64, n, DIM])
            wait_full(dve, J_KVC)
            link(nc.vector.tensor_tensor(kvc[0:64], ps[0:64, bank(J_KVC), 0:64], head_mask[0:64], ALU.mult))
            dve.sem_inc(job_ev[J_KVC % 2], 1)
            for k, at in ((J_KV, 0), (J_KV2, 2048)):
                wait_full(dve, k)
                src = ps[0:64, bank(k):bank(k) + 4, :].rearrange("p b (i d) -> p (b i) d", d=DIM)
                dst = kvm[0:64, at:at + 2048].rearrange("p (i d) -> p i d", d=DIM)
                link(nc.vector.tensor_tensor(dst, src, heads(32), ALU.mult))
                nc.vector.tensor_tensor(dst, dst, kvc[0:64].unsqueeze(1).broadcast_to([64, 32, DIM]), ALU.add)\
                    .then_inc(job_ev[k % 2], 1)

            def last_norm(i, a, n):
                x3, d3, q3 = (as_slots(t)[:, a:a + n, :] for t in (h1, dev, sq))
                at = slice(DIM * a, DIM * (a + n))
                wide = lambda t: t[:, a:a + n].unsqueeze(2).broadcast_to([128, n, DIM])
                link(nc.vector.reduce_sum(s1[:, a:a + n], x3, AX.X))
                link(nc.vector.tensor_scalar(s4[:, a:a + n], s1[:, a:a + n], 1.0 / DIM, None, ALU.mult))
                link(nc.vector.tensor_tensor(d3, x3, wide(s4), ALU.subtract))
                link(nc.vector.tensor_tensor(sq[:, at], dev[:, at], dev[:, at], ALU.mult))
                nc.vector.reduce_sum(s2[:, a:a + n], q3, AX.X).then_inc(ln_sum, 1)
                dve.wait_ge(ln_root, 2 * len(NORMED) + 1 + i)
                link(nc.vector.reciprocal(s4[:, a:a + n], s3[:, a:a + n]))
                nc.vector.tensor_tensor(as_slots(n2)[:, a:a + n, :], d3, wide(s4), ALU.mult).then_inc(n2_ready, 1)

            def attended(k, at):
                wait_full(dve, k)
                nc.vector.tensor_tensor(h1[:, at:at + 1024], ps[:, bank(k):bank(k) + 2, :]
                                        .rearrange("p b n -> p (b n)"), hsum[:, at:at + 1024], ALU.add)\
                    .then_inc(job_ev[k % 2], 1)
                wait_evacuated(dve, k)

            attended(J_ATT, 0)
            last_norm(0, 0, 16)
            attended(J_ATT2, 1024)
            last_norm(1, 16, 16)
            link(nc.vector.tensor_copy(h1[:, MAPS:COLS], hsum[:, MAPS:COLS]))
            wait_full(dve, J_CLST)
            nc.vector.tensor_tensor(h1[0:BATCH, MAPS:COLS], hsum[0:BATCH, MAPS:COLS], ps[0:64, bank(J_CLST), 0:64],
                                    ALU.add).then_inc(job_ev[J_CLST % 2], 1)
            wait_evacuated(dve, J_CLST)
            last_norm(2, 32, 1)
            for i, (k, (at, n)) in enumerate(zip((J_N2T, J_N2T2, J_N2C), PARTS)):
                dve.wait_ge(n2_high, i + 1)
                src = ps[64:128, bank(k):bank(k) + 4, :].rearrange("p b n -> p (b n)")[:, 0:n]
                nc.vector.tensor_tensor(n2r[64:128, at:at + n], src, n2r[64:128, at:at + n].bitcast(fp32),
                                        ALU.subtract).then_inc(job_ev[k % 2], 1)
            wait_full(dve, J_LOG)
            e3 = lambda t: t.rearrange("p (s e) -> p s e", e=EXPERTS)
            wide = lambda t: t.unsqueeze(2).broadcast_to([128, SLOTS, EXPERTS])
            fall = falling.unsqueeze(1).broadcast_to([128, SLOTS, EXPERTS])
            logits = ps[:, bank(J_LOG), 0:SLOTS * EXPERTS]
            link(nc.vector.reduce_max(s1, e3(logits), AX.X))
            nc.vector.tensor_tensor(e3(g1), e3(logits), wide(s1), ALU.subtract).then_inc(job_ev[J_LOG % 2], 1)
            wait_evacuated(dve, J_LOG)
            dve.wait_ge(exp_out, 1)
            link(nc.vector.reduce_sum(s1, e3(g2), AX.X))
            link(nc.vector.reciprocal(s2, s1))
            link(nc.vector.tensor_tensor(e3(g1), e3(g2), wide(s2), ALU.mult))
            link(nc.vector.reduce_max(s1, e3(g1), AX.X))
            first, other, key = e3(h0[:, 0:264]), e3(h0[:, 264:528]), e3(h0[:, 528:792])
            second, flag = e3(h0[:, 792:1056]), e3(h0[:, 1056:1320])
            link(nc.vector.tensor_tensor(flag, e3(g1), wide(s1), ALU.is_equal))
            link(nc.vector.tensor_tensor(key, flag, fall, ALU.mult))
            link(nc.vector.reduce_max(s2, key, AX.X))
            link(nc.vector.tensor_tensor(first, key, wide(s2), ALU.is_equal))
            link(nc.vector.scalar_tensor_tensor(out=other, in0=first, scalar=-2.0, in1=e3(g1), op0=ALU.mult,
                                                op1=ALU.add))
            link(nc.vector.reduce_max(s3, other, AX.X))
            link(nc.vector.tensor_tensor(flag, other, wide(s3), ALU.is_equal))
            link(nc.vector.tensor_tensor(key, flag, fall, ALU.mult))
            link(nc.vector.reduce_max(s2, key, AX.X))
            link(nc.vector.tensor_tensor(second, key, wide(s2), ALU.is_equal))
            link(nc.vector.tensor_tensor(flag, first, second, ALU.add))
            link(nc.vector.tensor_tensor(key, flag, e3(g1), ALU.mult))
            link(nc.vector.tensor_tensor(s4, s1, s3, ALU.add))
            link(nc.vector.tensor_scalar(s4, s4, 1e-12, None, ALU.max))
            link(nc.vector.reciprocal(s2, s4))
            link(nc.vector.tensor_tensor(flag, key, wide(s2), ALU.mult))
            def three(value, rest, half, outs):
                link(nc.vector.tensor_copy(half, value))
                link(nc.vector.tensor_copy(outs[0], half))
                link(nc.vector.tensor_tensor(rest, value, half, ALU.subtract))
                link(nc.vector.tensor_copy(half, rest))
                link(nc.vector.tensor_copy(outs[1], half))
                link(nc.vector.tensor_tensor(rest, rest, half, ALU.subtract))
                link(nc.vector.tensor_copy(outs[2], rest))

            three(flag, key, e3(n1[:, 0:132].bitcast(bf16)), [comb3[:, :, 8 * i:8 * i + 8] for i in range(3)])
            three(b2[0:24], n1[0:24, 132:196], n1[0:24, 196:228].bitcast(bf16), [t[0:24] for t in b2p])
            nc.vector.tensor_copy(pick[0:24], picks[0:24]).then_inc(split_ready, 1)
            nc.vector.tensor_tensor(hsum, h1, n2, ALU.add).then_inc(n2_ready, 1)
            for i in (0, 2):
                k, (at, n) = J_CT + i, PARTS[i]
                wait_full(dve, k)
                src = ps[0:24, bank(k):bank(k) + 4, :].rearrange("p b n -> p (b n)")[:, 0:n]
                nc.vector.tensor_copy(combt[0:24, at:at + n], src).then_inc(job_ev[k % 2], 1)
            for p in range(EXPERTS // 2):
                for j, (at, n) in enumerate(SPREAD):
                    step = len(SPREAD) * p + j
                    dve.wait_ge(spread_full, step + 1)
                    b = bank(J_OUT + 1) + 2 * (step % 2)
                    src = ps[:, b:b + 2, :].rearrange("p b n -> p (b n)")[:, 0:n]
                    nc.vector.tensor_tensor(hid[p][:, at:at + n], hid[p][:, at:at + n], src, ALU.mult)\
                        .then_inc(spread_ev, 1)
            dve.wait_ge(n2_ready, 4)
            wait_full(dve, J_OUT + 2)
            turned = ps[:, bank(J_OUT + 2):bank(J_OUT + 2) + 4, :].rearrange("p b (t h d) -> p h (b t) d", h=2, d=DIM)
            for i in range(2):
                here = slice(1024 * i, 1024 * i + 1024)
                nc.vector.tensor_tensor(as_slots(dev[:, here]), turned[:, i], as_slots(hsum[:, here]), ALU.add)\
                    .then_inc(out_ready, 1)
            wait_full(dve, J_OUT + 3)
            nc.vector.tensor_tensor(dev[:, MAPS:COLS], ps[:, bank(J_OUT + 3), 0:64], hsum[:, MAPS:COLS], ALU.add)\
                .then_inc(out_ready, 1)

        block = ctx.enter_context(nc.Block())

        def apart(eng):
            eng.sem_inc(passed, 1)

        def raw_half(l, q, h):
            if isinstance(l, int) and isinstance(q, int):
                return raw_d[l, q, :, 2048 * h:2048 * h + 2048]
            return raw_d[bass.ds(l, 1), bass.ds(q, 1), :, 2048 * h:2048 * h + 2048].rearrange("a b p n -> (a b p) n")

        def half(tile, h):
            return tile[:, 2048 * h:2048 * h + 2048]

        def y_step(l, q):
            return 1 + QUADS * (l - 1) + q

        def x_step(l, q):
            return 1 + QUADS * l + q

        def input_use(p, it):
            return PAIRS * p + it

        MIX_ORDER = [("mix", 0), ("mix", 1)]
        for p in range(1, KY // 2):
            MIX_ORDER += [("mix", 2 * p), ("mix", 2 * p + 1), ("inverse", p - 1)]
        MIX_ORDER += [("inverse", KY // 2 - 1)]
        RING = KY // 2
        AHEAD = 4

        @block.sync
        def _(sp):
            for s in from_one:
                sp.sem_inc(s, 1)
            for dst, src in ((img[0:BATCH, :], images), (fy.rearrange("p h n -> p (h n)"), fy_d), (fx, fx_d),
                             (ix[0:96, :], ix_d), (iy[0:96, :], iy_d), (masks, masks_d), (qcols, q_cols),
                             (pcol[0:32, :], p_cols), (p0, p_rows[0:1, :].broadcast_to([128, 32]))):
                sp.dma_start(dst, src).then_inc(tables_in, 16)
            sp.wait_ge(zeroed, 4)
            for row in (BATCH, 96):
                sp.dma_start(img[row:row + FEATURE_ROWS, :], grids_d).then_inc(grids_in, 16)
            sp.dma_start(prow[BATCH:BATCH + FEATURE_ROWS, :], p_rows[1:4, :]).then_inc(grids_in, 16)

            def layer_tables(l):
                for j in range(QUAD):
                    src = conv_w[l] if isinstance(l, int) else \
                        conv_w[bass.ds(l, 1), :, :].rearrange("a c o -> (a c) o")
                    sp.dma_start(wbd[32 * j:32 * j + 32, 32 * j:32 * j + 32], src).then_inc(layer_in, 16)
                src = layer_cols[l] if isinstance(l, int) else \
                    layer_cols[bass.ds(l, 1), :, :].rearrange("a p n -> (a p) n")
                sp.dma_start(lcols, src).then_inc(layer_in, 16)

            def weights(l, ky):
                src = mode_w[l, ky] if isinstance(l, int) else \
                    mode_w[bass.ds(l, 1), ky, :, :].rearrange("a p n -> (a p) n")
                sp.dma_start(wring[ky % AHEAD][0:64].rearrange("p x n -> p (x n)"), src)\
                  .then_inc(w_in[ky % AHEAD], 16)

            HEAD = 4 * QUAD * CHANNELS

            def store_columns(ky, a, b, done):
                sp.dma_start(half_d[2 * ky:2 * ky + 2].rearrange("r x g n -> (r x g) n")[:, a:b],
                             xhalf[ky % 2][:, a:b]).then_inc(done, 16)

            def mix(l):
                def next_weights(ky):
                    if ky + AHEAD < KY:
                        sp.wait_ge(mix_full[ky % 2], RING * l + ky // 2 + 1)
                        weights(l, ky + AHEAD)

                def bring_back(p):
                    sp.wait_ge(mix_st[p % 2], 64 * (RING // 2 * l + p // 2 + 1))
                    if p >= 2:
                        sp.wait_ge(ix_full[1], KY * l + 2 * p - 2)
                    for h in range(2):
                        sp.dma_start(kxin[p % 2][48 * h:48 * h + 48].rearrange("k (o n) -> k o n", o=16),
                                     mixed_d[:, p, 16 * h:16 * h + 16, :]).then_inc(kx_in[p % 2], 16)

                def store_inverse(ky):
                    for h in range(2):
                        sp.wait_ge(ix_ev[h], KY * l + ky + 1)
                    if ky < KY - 1:
                        store_columns(ky, 0, 2048, ix_st[ky % 2])
                    else:
                        store_columns(ky, 0, HEAD, ix_head)

                sp.wait_ge(dft_full, past(2 * y_step(l, QUADS)))
                apart(sp)
                weights(l, 3)
                for p in range(KY // 2):
                    next_weights(2 * p)
                    for s in range(2):
                        sp.wait_ge(mix_ev[s], RING * l + p + 1)
                    for m in range(2):
                        for ri in range(2):
                            k = ri * KX + m * KX_HALF
                            sp.dma_start(mixed_d[k:k + KX_HALF, p, :, :].rearrange("k o n -> o k n"),
                                         view(at_map + POSITIONS + p % 2 * 1536, 1536)
                                         [64 * m + 32 * ri:64 * m + 32 * ri + 32]
                                         .rearrange("o (k n) -> o k n", n=2 * BATCH)).then_inc(mix_st[p % 2], 16)
                    next_weights(2 * p + 1)
                    if 0 < p < KY // 2 - 1:
                        store_inverse(2 * p - 2)
                    bring_back(p)
                    if p == KY // 2 - 1:
                        store_inverse(2 * p - 2)
                    if p:
                        store_inverse(2 * p - 1)
                store_inverse(KY - 2)
                store_inverse(KY - 1)

            def g_load(q, s):
                for x in range(4):
                    src = half_d[:, x, :, bass.ds(q * 128, 128)]
                    sp.dma_start(gtile[s][24 * x:24 * x + 24], src).then_inc(g_in[s], 16)

            def input_load(l, q, s, h):
                sp.dma_start(half(vin[s], h), raw_half(l - 1, q, h)).then_inc(ld[s][h], 16)

            def output_pass(l, first):
                sp.wait_ge(ix_st[0], 16 * RING * (l + 1))
                sp.wait_ge(ix_st[1], 16 * (RING * (l + 1) - 1))
                apart(sp)
                sp.wait_ge(ix_head, 16 * (l + 1))
                g_load(0, 0)
                store_columns(KY - 1, HEAD, 2048, ix_st[1])
                if not first:
                    for h in range(2):
                        input_load(l, 1, 1, h)
                sp.wait_ge(ix_st[1], 16 * RING * (l + 1))
                g_load(1, 1)
                if first:
                    sp.wait_ge(f_high, 1)
                    sp.wait_ge(f_low, 1)
                    features(1)

                def steps(it, more):
                    for s in range(2):
                        q = 2 * it + s
                        for h in range(2):
                            if more and first:
                                if h == 0:
                                    sp.wait_ge(g_low, q + 1)
                                    g_load(q + 2, s)
                            elif more:
                                sp.wait_ge(out_full[h], QUADS * l + q + 1)
                                input_load(l, q + 2, s, h)
                                if h:
                                    g_load(q + 2, s)
                            else:
                                if h == 0:
                                    sp.wait_ge(map_st[s], past(32 * (PAIRS * l + 1)))
                                sp.wait_ge(out_full[h], QUADS * l + q + 1)
                                apart(sp)
                                input_load(l + 1, s, s, h)
                            sp.wait_ge(out_ev[h], past(QUADS * l + q + 1))
                            sp.dma_start(raw_half(l, q, h), half(vmap[s], h)).then_inc(map_st[s], 16)

                with sp.Fori(0, PAIRS - 1) as it:
                    steps(it, True)
                steps(PAIRS - 1, False)

            def spectrum_pass(l):
                for ky in range(AHEAD - 1):
                    weights(l, ky)
                for s in range(2):
                    sp.wait_ge(map_st[s], past(32 * PAIRS * l))
                apart(sp)
                with sp.Fori(0, PAIRS - 1) as it:
                    for s in range(2):
                        for h in range(2):
                            sp.wait_ge(transposed, 2 * y_step(l, 2 * it + s) + h + 1)
                            input_load(l, 2 * it + s + 2, s, h)
                for h in range(2):
                    sp.wait_ge(transposed, 2 * y_step(l, QUADS - 2) + h + 1)
                    apart(sp)
                    input_load(l, 0, 0, h)
                sp.wait_ge(transposed, 2 * y_step(l, QUADS - 1) + 2)
                apart(sp)

            def features(u):
                for row in (0, 64):
                    sp.dma_start(img[row:row + 32, :], images[32 * u:32 * u + 32, :]).then_inc(f_in[u], 16)

            layer_tables(0)
            sp.wait_ge(transposed, 2)
            features(0)
            sp.dma_start(img[32:32 + FEATURE_ROWS, :], grids_d).then_inc(f_in[0], 16)
            for ky in range(AHEAD - 1):
                weights(0, ky)
            mix(0)
            output_pass(0, True)
            with sp.Fori(1, LAYERS) as l:
                spectrum_pass(l)
                layer_tables(l)
                mix(l)
                output_pass(l, False)

            for s in range(2):
                sp.wait_ge(map_st[s], past(32 * PAIRS * LAYERS))

            sp.wait_ge(bn_ready, LAYERS)
            sync_constants(sp)
            for k, q in enumerate(PROJECTED):
                s, it = k % 2, k // 2
                if 2 <= k < QUADS - 2:
                    sp.wait_ge(proj_full[s], it + 1)
                    for h in range(2):
                        input_load(LAYERS, k, s, h)
                if k in ENDS:
                    group_load(sp, ENDS.index(k))
                sp.wait_ge(proj_ev[s], past(it + 1))
                for c in range(4):
                    dst = tok_d[QUAD * q:QUAD * q + QUAD, c:c + 5:4, :]
                    sp.dma_start(dst, hrow[s][32 * c:32 * c + QUAD].rearrange("j (r n) -> j r n", r=2))\
                      .then_inc(proj_st[s], 16)
            group_load(sp, len(GROUPS) - 1)
            sync_tokens(sp)

        @block.scalar
        def _(act):
            def part_evac(l, q, s, c, halves=(0, 1)):
                for h in halves:
                    act.wait_ge(dft_full, past(2 * c + h + 1))
                    if h == 0 and not isinstance(c, int):
                        act.wait_ge(xs_full, past(x_step(l, q) - 1))
                    for ri in range(2):
                        src = ps[0:64, 2 * h:2 * h + 2, 0:384].rearrange("p b (c n) -> p n b c", c=4)
                        last = nc.scalar.copy(
                            part[s][64 * ri:64 * ri + 64, :, 16 * h:16 * h + 16:2]
                            .rearrange("p k (b c) -> p k b c", c=4), src[:, 48 * ri:48 * ri + 48])
                    last.then_inc(part_a, 1)

            def modes_evac(q, s, c):
                act.wait_ge(xs_full, past(c + 1))
                for j in range(2):
                    for ri in range(2):
                        src = ps[32 * j:32 * j + 32, 4 + 2 * s:6 + 2 * s, 0:288]\
                            .rearrange("p h (y r x) -> p h y r x", y=6, r=2)[:, :, :, ri, :]
                        dst = modes[32 * ri:32 * ri + 32, :, :, bass.ds(QUAD * q + j, 1)]\
                            .rearrange("p (h y) x b -> p h y (x b)", h=2)
                        last = nc.scalar.copy(dst, src)
                last.then_inc(modes_a, 1)

            def relu(p, it, s, h):
                act.wait_ge(ld[s][h], 16 * (input_use(p, it) + 1))
                nc.scalar.activation(half(vin[s], h), half(vin[s], h), ACT.Relu, bias=sh, scale=sc)\
                    .then_inc(relu_done, 1)

            def mix(l):
                for what, n in MIX_ORDER:
                    if what == "mix":
                        s, i = n % 2, RING * l + n // 2
                        act.wait_ge(mix_full[s], i + 1)
                        if s == 0:
                            act.wait_ge(mix_st[n // 2 % 2], 64 * (RING // 2 * l + n // 4))
                        nc.scalar.copy(mixed[n // 2 % 2][:, s],
                                       ps[:, 2 * s:2 * s + 2, 0:384].rearrange("p h (k b) -> p h k b", b=BATCH))\
                            .then_inc(mix_ev[s], 1)
                    else:
                        for ky in (2 * n, 2 * n + 1):
                            act.wait_ge(ix_full[0], KY * l + ky + 1)
                            act.wait_ge(ix_st[ky % 2], 16 * (RING * l + n))
                            nc.scalar.copy(xhalf[ky % 2].rearrange("p (b o) -> p b o", o=CHANNELS)[:, :, 0:16],
                                           ps[:, 4:6, :].rearrange("p h (b o) -> p (h b) o", o=16))\
                                .then_inc(ix_ev[0], 1)

            def map_evac(l, it, s, h):
                act.wait_ge(out_full[h], QUADS * l + 2 * it + s + 1)
                if h == 0:
                    act.wait_ge(map_st[s], past(32 * (PAIRS * l + it)))
                    act.wait_ge(stat_done[s], past(PAIRS * l + it))
                nc.scalar.copy(half(vmap[s], h).rearrange("p (b n) -> p b n", b=4), ps[:, 4 * h:4 * h + 4, :])\
                    .then_inc(out_ev[h], 1)

            def norm_root(l):
                act.wait_ge(bn_p, 2 * l + 2)
                nc.scalar.activation(tiny[:, 3:4], ps[:, 1, 0:1], ACT.Sqrt, bias=eps_col).then_inc(bn_s, 1)

            act.wait_ge(zeroed, 5)
            part_evac(0, 0, 0, 0)
            act.wait_ge(xs_full, past(1))
            nc.scalar.copy(spect[:, 0:288], ps[:, 4, 0:288]).then_inc(modes_a, 1)

            def features_high(u):
                act.wait_ge(f_in[u], 48 if u == 0 else 32)
                nc.scalar.copy(feats[u], img).then_inc(f_high, 1)

            features_high(0)
            with act.Fori(0, PAIRS) as it:
                for s in range(2):
                    modes_evac(2 * it + s, s, x_step(0, 2 * it + s))
            mix(0)
            act.wait_ge(mix_ev[1], RING)
            nc.scalar.copy(exphigh, expconv).then_inc(t_split, 1)
            nc.scalar.copy(iyhigh[0:96], iy[0:96]).then_inc(t_split, 1)

            def g_part(it, s):
                act.wait_ge(g_in[s], 64 * (it + 1))
                q = 2 * it + s
                if not isinstance(q, int) or q >= 2:
                    act.wait_ge(out_full[1], q - 1)
                nc.scalar.copy(ghigh[s][0:96], gtile[s][0:96]).then_inc(g_high, 1)

            def first_output(it, more=True):
                for s in range(2):
                    if more or s == 0:
                        g_part(it + s, 1 - s)
                    for h in range(2):
                        map_evac(0, it, s, h)

            g_part(0, 0)
            first_output(0)
            act.wait_ge(ix_full[1], KY)
            features_high(1)
            with act.Fori(1, PAIRS - 1) as it:
                first_output(it)
            first_output(PAIRS - 1, False)
            norm_root(0)

            with act.Fori(1, LAYERS) as l:
                act.wait_ge(bn_ready, l)
                for s in range(2):
                    for h in range(2):
                        relu(2 * l - 2, 0, s, h)
                part_evac(l, 0, 0, y_step(l, 0))
                for h in range(2):
                    relu(2 * l - 2, 1, 0, h)

                def spectrum(l, it, s, more):
                    q = 2 * it + s
                    part = not isinstance(q, int) or q + 1 < QUADS
                    if part:
                        part_evac(l, q + 1, 1 - s, y_step(l, q + 1), (0,))
                    if more:
                        relu(2 * l - 2, it + 1 + s, 1 - s, 0)
                    if part:
                        part_evac(l, q + 1, 1 - s, y_step(l, q + 1), (1,))
                    modes_evac(q, s, x_step(l, q))
                    if more:
                        relu(2 * l - 2, it + 1 + s, 1 - s, 1)

                with act.Fori(0, PAIRS - 2) as it:
                    for s in range(2):
                        spectrum(l, it, s, True)
                for q in range(QUADS - 4, QUADS):
                    spectrum(l, q // 2, q % 2, q + 3 < QUADS)
                for h in range(2):
                    relu(2 * l - 1, 0, 0, h)
                mix(l)
                relu(2 * l - 1, 0, 1, 0)

                def output(l, it, last):
                    for i in range(4):
                        map_evac(l, it, i // 2, i % 2)
                        n = i + 3
                        if not last or n < 4:
                            relu(2 * l - 1, it + n // 4, n % 4 // 2, n % 2)

                with act.Fori(0, PAIRS - 1) as it:
                    output(l, it, False)
                output(l, PAIRS - 1, True)
                norm_root(l)

            act.wait_ge(bn_v, 3 * LAYERS + 2)
            roots = [0]
            for k in range(QUADS):
                s, it = k % 2, k // 2
                act.wait_ge(proj_full[s], it + 1)
                act.wait_ge(proj_st[s], past(64 * it))
                nc.scalar.activation(hrow[s].rearrange("p (r n) -> p r n", r=2), ps[:, 2 * s:2 * s + 2, :],
                                     ACT.Identity, bias=qbias).then_inc(proj_ev[s], 1)
                for _ in range(2 if k == 1 else k % 2 if k > 2 else 0):
                    first_root(act, roots[0])
                    roots[0] += 1
            while roots[0] < 2 * len(NORMED):
                first_root(act, roots[0])
                roots[0] += 1
            scalar_tokens(act)

        @block.tensor
        def _(pe):
            def y_transform(l, q, s, c):
                pe.wait_ge(transposed, 2 * c + 2)
                blocks = vmap[s].rearrange("p (h d m) -> p h d m", h=2, d=16)
                for h in range(2):
                    if not isinstance(c, int):
                        pe.wait_ge(part_a, 2 * c + h - 1)
                        pe.wait_ge(part_v, 2 * c + h - 1)
                    for d in range(8 * h, 8 * h + 8):
                        for yh in range(2):
                            last = nc.tensor.matmul(ps[:, d // 4, 96 * (d % 4):96 * (d % 4) + 96],
                                                    blocks[:, yh, d], fy[:, yh, :], start=(yh == 0), stop=(yh == 1))
                    last.then_inc(dft_full, 1)

            def x_transform(l, q, s, c, x):
                pe.wait_ge(part_a, 2 * c + 2)
                pe.wait_ge(part_v, 2 * c + 2)
                if not isinstance(x, int):
                    pe.wait_ge(modes_a, past(x - 1))
                    pe.wait_ge(modes_v, past(x - 1))
                for ky in range(KY):
                    last = nc.tensor.matmul(ps[:, 4 + 2 * s + ky // 6, 48 * (ky % 6):48 * (ky % 6) + 48],
                                            part[s][:, 4 * ky:4 * ky + 4, :].rearrange("p j c -> p (j c)"), fx,
                                            start=True, stop=True)
                last.then_inc(xs_full, 1)

            def mix(l):
                pe.wait_ge(modes_a, past(x_step(l, QUADS)))
                pe.wait_ge(modes_v, past(x_step(l, QUADS)))
                for what, n in MIX_ORDER:
                    if what == "mix":
                        s, i = n % 2, RING * l + n // 2
                        pe.wait_ge(signed, KY * l + n + 1)
                        pe.wait_ge(mix_ev[s], i)
                        apart(pe)
                        for k in range(KX_HALF):
                            for m in range(2):
                                last = nc.tensor.matmul(
                                    ps[64 * m:64 * m + 64, 2 * s + k // 6, 64 * (k % 6):64 * (k % 6) + 64],
                                    wring[n % AHEAD][0:64, KX_HALF * m + k, :], modes[0:64, n, KX_HALF * m + k, :],
                                    start=True, stop=True)
                        last.then_inc(mix_full[s], 1)
                    else:
                        pe.wait_ge(kx_in[n % 2], 32 * (RING // 2 * l + n // 2 + 1))
                        rows = kxin[n % 2][0:96].rearrange("k (o e b) -> k e b o", e=2, b=BATCH)
                        for e in range(2):
                            for h in range(2):
                                pe.wait_ge(ix_ev[h], KY * l + 2 * n + e)
                                for g in range(2):
                                    last = nc.tensor.matmul(ps[:, 4 + 2 * h + g, :], ix[0:96, 128 * h:128 * h + 128],
                                                            rows[:, e, 32 * g:32 * g + 32, :], start=True, stop=True)
                                last.then_inc(ix_full[h], 1)

            def map_out(l, it, s, stationary, source, ready):
                for h in range(2):
                    ready(h)
                    pe.wait_ge(out_ev[h], past(QUADS * l + 2 * it + s))
                    for i in range(2):
                        if h:
                            pe.wait_ge(ix_ev[i], KY * (l + 1))
                        else:
                            pe.wait_ge(mix_ev[i], RING * (l + 1))
                    for n in range(4 * h, 4 * h + 4):
                        nc.tensor.matmul(ps[:, n, :], stationary, source[:, 512 * n:512 * n + 512],
                                         start=True, stop=False)
                    if h == 0:
                        pe.wait_ge(g_in[s], 64 * (PAIRS * l + it + 1))
                    for n in range(4 * h, 4 * h + 4):
                        for g in range(2):
                            last = nc.tensor.matmul(ps[:, n, 256 * g:256 * g + 256], gtile[s][0:96, 2 * n + g, :],
                                                    iy[0:96, :], start=False, stop=(g == 1))
                    last.then_inc(out_full[h], 1)

            def norm_sums(l):
                for h in range(2):
                    pe.wait_ge(out_ev[h], past(QUADS * (l + 1)))
                for k in range(2):
                    pe.wait_ge(bn_v, 3 * l + 1 + k)
                    nc.tensor.matmul(ps[:, k, 0:1], average, (mv if k == 0 else tiny)[:, 0:1], start=True, stop=True)\
                        .then_inc(bn_p, 1)

            pe.wait_ge(tables_in, 16 * 9)
            y_transform(0, 0, 0, 0)
            x_transform(0, 0, 0, 0, 0)
            pe.wait_ge(layer_in, 80)
            pe.wait_ge(t_ready, 2)
            nc.tensor.matmul(ps[:, 0, 0:32], pcol[0:32, 0:1].broadcast_to([32, 128]), wbd[0:32, 0:32],
                             start=True, stop=True)
            nc.tensor.matmul(ps[:, 1, 0:32], prt[0:32, :], wbd[0:32, 0:32], start=True, stop=True)\
                .then_inc(t_prod, 1)
            pe.wait_ge(modes_a, past(1))
            pe.wait_ge(modes_v, past(1))
            with pe.Fori(0, PAIRS) as it:
                for s in range(2):
                    pe.wait_ge(e_copied[s], it + 1)
                    pe.wait_ge(modes_a, past(2 * it + s))
                    pe.wait_ge(modes_v, past(2 * it + s))
                    for h in range(2):
                        last = nc.tensor.matmul(ps[:, 4 + 2 * s + h, 0:288], estage[s], spect[:, 288 * h:288 * h + 288],
                                                start=True, stop=True)
                    last.then_inc(xs_full, 1)
            mix(0)
            def first_output(it, u):
                for s in range(2):
                    q = 2 * it + s
                    pe.wait_ge(r_copied[s], it + 1)
                    pe.wait_ge(g_low, q + 1)
                    for h in range(2):
                        pe.wait_ge(out_ev[h], past(q))
                        for i in range(2):
                            for n in range(4 * h, 4 * h + 4):
                                nc.tensor.matmul(ps[:, n, :], rstage[s][i], feats[u][:, 512 * n:512 * n + 512],
                                                 start=(i == 0), stop=False)
                        for n in range(4 * h, 4 * h + 4):
                            for g in range(2):
                                dst = ps[:, n, 256 * g:256 * g + 256]
                                tile = 2 * n + g
                                nc.tensor.matmul(dst, ghigh[s][0:96, tile, :], iyhigh[0:96], start=False, stop=False)
                                nc.tensor.matmul(dst, ghigh[s][0:96, tile, :], iylow[0:96], start=False, stop=False)
                                last = nc.tensor.matmul(dst, glow[s][0:96, tile, :], iyhigh[0:96], start=False,
                                                        stop=(g == 1))
                        last.then_inc(out_full[h], 1)

            for i in range(2):
                pe.wait_ge(mix_ev[i], RING)
                pe.wait_ge(ix_ev[i], KY)
            pe.wait_ge(t_split, 4)
            for u in range(2):
                pe.wait_ge(f_high, u + 1)
                pe.wait_ge(f_low, u + 1)
                apart(pe)
                with pe.Fori(u * PAIRS // 2, (u + 1) * PAIRS // 2) as it:
                    first_output(it, u)
            norm_sums(0)

            with pe.Fori(1, LAYERS) as l:
                pe.wait_ge(bn_ready, l)
                y_transform(l, 0, 0, y_step(l, 0))
                with pe.Fori(0, PAIRS - 1) as it:
                    for s in range(2):
                        q = 2 * it + s
                        y_transform(l, q + 1, 1 - s, y_step(l, q + 1))
                        x_transform(l, q, s, y_step(l, q), x_step(l, q))
                y_transform(l, QUADS - 1, 1, y_step(l, QUADS - 1))
                for s in range(2):
                    x_transform(l, QUADS - 2 + s, s, y_step(l, QUADS - 2 + s), x_step(l, QUADS - 2 + s))
                pe.wait_ge(layer_in, 80 * (l + 1))
                mix(l)
                with pe.Fori(0, PAIRS) as it:
                    for s in range(2):
                        halves = 2 * (QUADS * (2 * l - 1) + 2 * it + s)
                        map_out(l, it, s, wbd, vin[s], lambda h: pe.wait_ge(relu_done, halves + h + 1))
                norm_sums(l)

            pe.wait_ge(bn_v, 3 * LAYERS + 1)
            nc.tensor.matmul(ps[:, 7, 0:1], tiny[:, 6:7].broadcast_to([128, 128]), tiny[:, 7:8], start=True, stop=True)\
                .then_inc(bn_p, 1)

            def project(source, it, s, h):
                if h == 0:
                    pe.wait_ge(proj_ev[s], past(it))
                for n in range(4):
                    last = nc.tensor.matmul(ps[32 * n:32 * n + 32, 2 * s + h, :], proj,
                                            half(source, h)[:, 512 * n:512 * n + 512], start=True, stop=True)
                if h:
                    last.then_inc(proj_full[s], 1)

            for s in range(2):
                for h in range(2):
                    project(vmap[s], 0, s, h)
            with pe.Fori(1, PAIRS) as it:
                for s in range(2):
                    for h in range(2):
                        pe.wait_ge(ld[s][h], 16 * input_use(2 * LAYERS - 2, it))
                        project(vin[s], it, s, h)
            tensor_tokens(pe)

        @block.vector
        def _(dve):
            links = [0]

            def link(ins):
                links[0] += 1
                ins.then_inc(vchain, 1)
                dve.wait_ge(vchain, links[0])

            def part_evac(l, q, s, c, halves=(0, 1)):
                for h in halves:
                    dve.wait_ge(dft_full, past(2 * c + h + 1))
                    if h == 0 and not isinstance(c, int):
                        dve.wait_ge(xs_full, past(x_step(l, q) - 1))
                    for ri in range(2):
                        src = ps[64:128, 2 * h:2 * h + 2, 0:384].rearrange("p b (c n) -> p n b c", c=4)
                        last = nc.vector.tensor_copy(
                            part[s][64 * ri:64 * ri + 64, :, 16 * h + 1:16 * h + 16:2]
                            .rearrange("p k (b c) -> p k b c", c=4), src[:, 48 * ri:48 * ri + 48])
                    last.then_inc(part_v, 1)

            def modes_evac(q, s, c):
                dve.wait_ge(xs_full, past(c + 1))
                for j in range(2, 4):
                    for ri in range(2):
                        src = ps[32 * j:32 * j + 32, 4 + 2 * s:6 + 2 * s, 0:288]\
                            .rearrange("p h (y r x) -> p h y r x", y=6, r=2)[:, :, :, ri, :]
                        dst = modes[32 * ri:32 * ri + 32, :, :, bass.ds(QUAD * q + j, 1)]\
                            .rearrange("p (h y) x b -> p h y (x b)", h=2)
                        last = nc.vector.tensor_copy(dst, src)
                last.then_inc(modes_v, 1)

            def y_rows(tile):
                return tile.rearrange("p (h c x) -> p x h c", h=2, x=SIDE)

            def x_y(tile):
                return tile.rearrange("p (x h y) -> p x h y", h=2, x=SIDE)

            def block_transpose(l, q, s, c, h):
                dve.wait_ge(relu_done, 2 * (QUADS * (2 * l - 2) + q) + h + 1)
                if h == 0:
                    dve.wait_ge(dft_full, past(2 * c - 2))
                xs = slice(32 * h, 32 * h + 32)
                nc.vector.transpose(y_rows(vmap[s])[:, xs], x_y(vin[s])[:, xs]).then_inc(transposed, 1)

            def mix(l):
                def sign(ky):
                    w = wring[ky % AHEAD][32:64, :, 0:32]
                    dve.wait_ge(w_in[ky % AHEAD], 16 * (KY // AHEAD * l + ky // AHEAD + 1))
                    nc.vector.tensor_scalar(w, w, -1.0, None, ALU.mult).then_inc(signed, 1)

                for ky in range(AHEAD - 1):
                    sign(ky)
                for what, n in MIX_ORDER:
                    if what == "mix":
                        if n + AHEAD - 1 < KY:
                            sign(n + AHEAD - 1)
                    else:
                        for ky in (2 * n, 2 * n + 1):
                            dve.wait_ge(ix_full[1], KY * l + ky + 1)
                            dve.wait_ge(ix_st[ky % 2], 16 * (RING * l + n))
                            nc.vector.tensor_copy(
                                xhalf[ky % 2].rearrange("p (b o) -> p b o", o=CHANNELS)[:, :, 16:32],
                                ps[:, 6:8, :].rearrange("p h (b o) -> p (h b) o", o=16)).then_inc(ix_ev[1], 1)

            def statistics(l, it, s):
                for h in range(2):
                    dve.wait_ge(out_ev[h], past(QUADS * l + 2 * it + s + 1))
                    for k in range(4):
                        n = 4 * h + k
                        last = nc.vector.bn_stats(
                            out=bnst[:, bass.ds((2 * it + s) * 8 + n, 1), :].rearrange("p a s -> p (a s)"),
                            in_=vmap[s][:, 512 * n:512 * n + 512])
                last.then_inc(stat_done[s], 1)

            def norm(l):
                for s in range(2):
                    dve.wait_ge(stat_done[s], past(PAIRS * (l + 1)))
                dve.wait_ge(layer_in, 80 * (l + 1))
                apart(dve)
                nc.vector.bn_aggr(out=mv, in_=bnst).then_inc(bn_v, 1)
                dve.wait_ge(bn_p, 2 * l + 1)
                dve.wait_ge(bn_v, 3 * l + 1)
                nc.vector.tensor_tensor(tiny[:, 1:2], mv[:, 0:1], ps[:, 0, 0:1], ALU.subtract).then_inc(t_ready, 1)
                dve.wait_ge(t_ready, 4 + 6 * l + 1)
                nc.vector.scalar_tensor_tensor(out=tiny[:, 0:1], in0=tiny[:, 1:2], scalar=tiny[:, 1:2],
                                               in1=mv[:, 1:2], op0=ALU.mult, op1=ALU.add).then_inc(bn_v, 1)
                nc.vector.tensor_tensor(tiny[:, 2:3], ps[:, 0, 0:1], lcols[:, 0:1], ALU.add).then_inc(t_ready, 1)
                dve.wait_ge(t_ready, 4 + 6 * l + 2)
                nc.vector.tensor_tensor(tiny[:, 4:5], lcols[:, 0:1], tiny[:, 2:3], ALU.subtract).then_inc(t_ready, 1)
                dve.wait_ge(bn_s, l + 1)
                nc.vector.reciprocal(tiny[:, 5:6], tiny[:, 3:4]).then_inc(t_ready, 1)
                dve.wait_ge(t_ready, 4 + 6 * l + 4)
                nc.vector.tensor_tensor(sc, tiny[:, 5:6], lcols[:, 1:2], ALU.mult).then_inc(t_ready, 1)
                dve.wait_ge(t_ready, 4 + 6 * l + 5)
                nc.vector.scalar_tensor_tensor(out=sh, in0=sc, scalar=tiny[:, 4:5], in1=lcols[:, 2:3],
                                               op0=ALU.mult, op1=ALU.add).then_inc(t_ready, 1)
                dve.wait_ge(t_ready, 4 + 6 * l + 6)
                nc.vector.tensor_copy(tiny[:, 6:7], sh).then_inc(bn_v, 1)
                dve.wait_ge(bn_v, 3 * l + 3)
                nc.vector.tensor_copy(tiny[:, 7:8], sh).then_inc(bn_ready, 1)

            nc.vector.memset(img[64:128, :], 0.0).then_inc(zeroed, 1)
            nc.vector.memset(prow, 0.0).then_inc(zeroed, 1)
            nc.vector.memset(wbd, 0.0).then_inc(zeroed, 1)
            nc.vector.memset(prt, 0.0).then_inc(zeroed, 1)
            nc.vector.memset(eps_col, BN_EPS).then_inc(zeroed, 1)

            dve.wait_ge(tables_in, 16 * 9)
            dve.wait_ge(grids_in, 48)
            dve.wait_ge(zeroed, 5)
            nc.vector.transpose(y_rows(vmap[0]), x_y(img)).then_inc(transposed, 2)
            exp3 = expand.rearrange("p (b c) -> p b c", c=CHANNELS)
            link(nc.vector.tensor_tensor(exp3, ident[:, 0:BATCH].unsqueeze(2).broadcast_to([128, BATCH, CHANNELS]),
                                         p0.unsqueeze(1).broadcast_to([128, BATCH, CHANNELS]), ALU.mult))
            nc.vector.tensor_tensor(exp3, exp3, prow.unsqueeze(1).broadcast_to([128, BATCH, CHANNELS]),
                                    ALU.add).then_inc(t_ready, 1)
            for row in (32, 96):
                last = nc.vector.tensor_copy(prt[0:32, row:row + FEATURE_ROWS], pcol[0:32, 1:4])
            last.then_inc(t_ready, 1)
            part_evac(0, 0, 0, 0)
            dve.wait_ge(xs_full, past(1))
            nc.vector.tensor_copy(spect[:, 288:576], ps[:, 5, 0:288]).then_inc(modes_v, 1)
            dve.wait_ge(t_ready, 1)
            for s in range(2):
                nc.vector.tensor_copy(estage[s], expand[:, 128 * s:128 * s + 128]).then_inc(e_copied[s], 1)
            dve.wait_ge(t_prod, 1)
            nc.vector.tensor_copy(p0c, ps[:, 0, 0:32])
            link(nc.vector.tensor_copy(prc, ps[:, 1, 0:32]))
            expc3 = expconv.rearrange("p (b c) -> p b c", c=CHANNELS)
            nc.vector.tensor_tensor(expc3, split_rows.unsqueeze(2).broadcast_to([128, 32, CHANNELS]),
                                    p0c.unsqueeze(1).broadcast_to([128, 32, CHANNELS]), ALU.mult).then_inc(t_ready, 1)
            dve.wait_ge(t_ready, 3)
            nc.vector.tensor_tensor(expc3, expc3, prc.unsqueeze(1).broadcast_to([128, 32, CHANNELS]),
                                    ALU.add).then_inc(t_ready, 1)
            dve.wait_ge(t_ready, 4)

            def expanded(it, more):
                for s in range(2):
                    dve.wait_ge(xs_full, past(x_step(0, 2 * it + s) + 1))
                    if more:
                        nc.vector.tensor_copy(estage[s], expand[:, bass.ds((2 * it + s + 2) * 128, 128)])\
                            .then_inc(e_copied[s], 1)
                    modes_evac(2 * it + s, s, x_step(0, 2 * it + s))

            with dve.Fori(0, PAIRS - 1) as it:
                expanded(it, True)
            expanded(PAIRS - 1, False)

            def features_low(u):
                dve.wait_ge(f_high, u + 1)
                nc.vector.tensor_tensor(feats[u][64:128], img[64:128], feats[u][64:128].bitcast(fp32), ALU.subtract)\
                    .then_inc(f_low, 1)

            features_low(0)
            mix(0)
            dve.wait_ge(t_split, 2)
            nc.vector.tensor_tensor(explow, expconv, exphigh.bitcast(fp32), ALU.subtract).then_inc(t_split, 1)
            nc.vector.tensor_tensor(iylow[0:96], iy[0:96], iyhigh[0:96].bitcast(fp32), ALU.subtract)\
                .then_inc(t_split, 1)
            dve.wait_ge(t_split, 4)

            def stage(q, s):
                if not isinstance(q, int) or q >= 2:
                    dve.wait_ge(out_full[1], q - 1)
                for i, source in enumerate((exphigh, explow)):
                    last = nc.vector.tensor_copy(rstage[s][i], source[:, bass.ds(q % 8 * 128, 128)])
                last.then_inc(r_copied[s], 1)

            def g_part(q, s):
                dve.wait_ge(g_high, q + 1)
                nc.vector.tensor_tensor(glow[s][0:96], gtile[s][0:96], ghigh[s][0:96].bitcast(fp32), ALU.subtract)\
                    .then_inc(g_low, 1)

            def first_output(it, more=True):
                for s in range(2):
                    q = 2 * it + s
                    if more or s == 0:
                        stage(q + 1, 1 - s)
                        g_part(q + 1, 1 - s)
                    statistics(0, it, s)

            stage(0, 0)
            g_part(0, 0)
            first_output(0)
            features_low(1)
            with dve.Fori(1, PAIRS - 1) as it:
                first_output(it)
            first_output(PAIRS - 1, False)
            norm(0)

            with dve.Fori(1, LAYERS) as l:
                for s in range(2):
                    dve.wait_ge(map_st[s], past(32 * PAIRS * l))
                    for h in range(2):
                        block_transpose(l, s, s, y_step(l, s), h)
                part_evac(l, 0, 0, y_step(l, 0))
                with dve.Fori(0, PAIRS - 1) as it:
                    for s in range(2):
                        q = 2 * it + s
                        for h in range(2):
                            block_transpose(l, q + 2, s, y_step(l, q + 2), h)
                            part_evac(l, q + 1, 1 - s, y_step(l, q + 1), (h,))
                        modes_evac(q, s, x_step(l, q))
                part_evac(l, QUADS - 1, 1, y_step(l, QUADS - 1))
                for s in range(2):
                    modes_evac(QUADS - 2 + s, s, x_step(l, QUADS - 2 + s))
                mix(l)
                with dve.Fori(0, PAIRS) as it:
                    for s in range(2):
                        statistics(l, it, s)
                norm(l)

            dve.wait_ge(bn_ready, LAYERS)
            link(nc.vector.tensor_tensor(tiny[:, 1:2], sc, qcols[:, 0:1], ALU.mult))
            link(nc.vector.tensor_scalar(proj, image_of, tiny[:, 1:2], None, ALU.mult))
            nc.vector.tensor_scalar(tiny[:, 7:8], qcols[:, 0:1], 1.0 / QUAD, None, ALU.mult).then_inc(bn_v, 1)
            dve.wait_ge(bn_p, 2 * LAYERS + 1)
            nc.vector.tensor_tensor(qbias, ps[:, 7, 0:1], qcols[:, 1:2], ALU.add).then_inc(bn_v, 1)
            vector_chain(dve, links)


INPUTS = ["images", "p_rows", "p_cols", "mode_w", "conv_w", "layer_cols", "q_cols", "cls_tok", "head_rows",
          "router_t", "w1_t", "b1_cols", "w2_rows", "b2_rows", "fy", "fx", "ix", "iy", "grids", "masks", "picks"]


def laid_out(x, cls_tok, L0_tok_p_w, L0_tok_p_b, L0_tok_fw1, L0_tok_fw2, L0_tok_w_w, L0_tok_w_b, L0_tok_bn_g,
             L0_tok_bn_b, L0_tok_q_w, L0_tok_q_b, L0_attn_kln_weight, L0_attn_kln_bias, L0_attn_vln_weight,
             L0_attn_vln_bias, L0_ffn_router_w, L0_ffn_w1, L0_ffn_b1, L0_ffn_w2, L0_ffn_b2):
    a = np.asarray
    p_rows = np.concatenate([a(L0_tok_p_w), a(L0_tok_p_b).reshape(1, -1)])
    f = np.stack([a(L0_tok_fw1), a(L0_tok_fw2)], axis=1)
    f = f.transpose(0, 5, 6, 2, 1, 4, 3).reshape(LAYERS, KY, 2, CHANNELS, KX, CHANNELS)
    direct, swapped = f.transpose(0, 1, 3, 4, 2, 5), f[:, :, ::-1].transpose(0, 1, 3, 4, 2, 5)
    mode_w = np.stack([direct, swapped], axis=2).reshape(LAYERS, KY, 64, KX * 64)
    cols = np.stack([a(L0_tok_w_b), a(L0_tok_bn_g), a(L0_tok_bn_b)], axis=2)
    layer_cols = np.tile(cols, (1, QUAD, 1))
    q_cols = np.stack([np.tile(a(L0_tok_q_w)[:, 0], QUAD), np.tile(a(L0_tok_q_b), 128)], axis=1)
    head_rows = np.stack([a(v).reshape(-1) for v in
                          (L0_attn_kln_weight, L0_attn_kln_bias, L0_attn_vln_weight, L0_attn_vln_bias)])
    fy, fx, ix, iy = transform_tables()
    grids, masks, picks = shape_tables()
    return {
        "images": a(x).reshape(BATCH, POSITIONS), "p_rows": p_rows, "p_cols": p_rows.T, "mode_w": mode_w,
        "conv_w": a(L0_tok_w_w), "layer_cols": layer_cols, "q_cols": q_cols, "cls_tok": a(cls_tok).reshape(1, DIM),
        "head_rows": head_rows, "router_t": a(L0_ffn_router_w).T, "w1_t": a(L0_ffn_w1).transpose(1, 0, 2),
        "b1_cols": a(L0_ffn_b1).reshape(EXPERTS // 2, 128).T, "w2_rows": a(L0_ffn_w2).reshape(EXPERTS // 2, 128, DIM)
        .transpose(1, 0, 2), "b2_rows": a(L0_ffn_b2), "fy": fy, "fx": fx, "ix": ix, "iy": iy, "grids": grids,
        "masks": masks, "picks": picks}


def kernel(**inputs):
    import concourse.bacc as bacc
    from concourse.bass_utils import run_bass_kernel_spmd

    nc = bacc.Bacc("TRN2", target_bir_lowering=False, num_devices=1)
    laid = laid_out(**inputs)
    arrays, args = {}, []
    for name in INPUTS:
        array = np.ascontiguousarray(laid[name])
        arrays[f"in_{name}"] = array
        args.append(nc.dram_tensor(f"in_{name}", array.shape, mybir.dt.from_np(array.dtype), kind="ExternalInput").ap())
    out = nc.dram_tensor("out_tokens", (BATCH, TOKENS, DIM), mybir.dt.float32, kind="ExternalOutput").ap()
    tower_kernel(nc, *args, out)
    r = run_bass_kernel_spmd(nc, [arrays], core_ids=[0])
    return r.results[0]["out_tokens"]
```
